# Optimizing a Trainium2 kernel written in Bass

```python
import numpy as np
import jax
import jax.numpy as jnp

def _softmax(x, axis=-1):
    return jax.nn.softmax(x, axis=axis)

def _gelu(x):
    return jax.nn.gelu(x, approximate=True)

def _silu(x):
    return jax.nn.silu(x)

def _sigmoid(x):
    return jax.nn.sigmoid(x)

def _layernorm(x, axis=-1, eps=1e-05):
    m = jnp.mean(x, axis=axis, keepdims=True)
    v = jnp.var(x, axis=axis, keepdims=True)
    return (x - m) / jnp.sqrt(v + eps)

def _scatter_add(tgt, idx, src, axis=0):
    return tgt.at[idx].add(src)

def _segment_sum(src, seg, n):
    return jax.ops.segment_sum(src, seg, n)
kernel_name = 'mk_gnn_resnorm_d4_gnn_r64_b6b0af'

def setup_inputs(seed: int=0):
    np.random.seed(seed)
    _w = jnp.asarray

    def _rec_inputs():
        import jax
        import jax.numpy as jnp
        _gk = jax.random.key(seed)
        x = -0.000202 + 1 * jax.random.normal(jax.random.fold_in(_gk, 1), (100000, 64), jnp.float32)
        src = jax.random.randint(jax.random.fold_in(_gk, 2), (25000,), 0, 100000, jnp.int32)
        dst = jax.random.randint(jax.random.fold_in(_gk, 3), (25000,), 0, 100000, jnp.int32)
        _o = jnp.argsort(dst, stable=True)
        src = src[_o]
        dst = dst[_o]
        edge_attr_64 = -9.77346e-05 + 0.999888 * jax.random.normal(jax.random.fold_in(_gk, 12), (25000, 64), jnp.float32)
        edge_weight1 = jax.random.uniform(jax.random.fold_in(_gk, 14), (25000, 1), jnp.float32, 0.0, 1)
        return (x, src, dst, edge_attr_64, edge_weight1)
    x, src, dst, edge_attr_64, edge_weight1 = _rec_inputs()

    def _L0_gnn_setup():
        import jax, jax.numpy as jnp
        import numpy as np
        N_NODES = 100000

        def gcn_conv(x, W, b, src, dst, n):
            h = x @ W
            loop = jnp.arange(n, dtype=src.dtype)
            s = jnp.concatenate([src, loop])
            d = jnp.concatenate([dst, loop])
            deg = jax.ops.segment_sum(jnp.ones_like(d, dtype=h.dtype), d, num_segments=n)
            dinv = jnp.where(deg > 0, jax.lax.rsqrt(deg), 0.0)
            norm = dinv[s] * dinv[d]
            msg = h[s] * norm[:, None]
            out = jax.ops.segment_sum(msg, d, num_segments=n)
            return out + b
        key = jax.random.key(seed)
        k1, k2, k3, k4 = jax.random.split(key, 4)
        n, e = (N_NODES, 25000)
        z = jax.random.normal(k1, (n, 64), dtype=jnp.float32)
        edge_index = jax.random.randint(k2, (2, e), 0, n, dtype=jnp.int64)
        W1 = jax.random.normal(k3, (64, 128), dtype=jnp.float32) * (1.0 / np.sqrt(64))
        b1 = jnp.zeros((128,), dtype=jnp.float32)
        W2 = jax.random.normal(k4, (128, 64), dtype=jnp.float32) * (1.0 / np.sqrt(128))
        b2 = jnp.zeros((64,), dtype=jnp.float32)
        return {'z': z, 'edge_index': edge_index, 'W1': W1, 'b1': b1, 'W2': W2, 'b2': b2}
    _L0_gnn_all = _L0_gnn_setup()
    _L0_gnn_in = {k: v for k, v in _L0_gnn_all.items() if k in ('W1', 'b1', 'W2', 'b2')}
    del _L0_gnn_all

    def _L1_gnn_setup():
        import jax, jax.numpy as jnp
        import numpy as np
        N_NODES = 50000
        N_EDGES = 12500
        ATOM_F = 64
        NBR_F = 64
        EPS = 1e-05

        def batch_norm(x, gamma, beta):
            mu = x.mean(axis=0)
            var = x.var(axis=0)
            return gamma * (x - mu) * jax.lax.rsqrt(var + EPS) + beta
        key = jax.random.key(seed)
        ks = jax.random.split(key, 8)
        d_in = 2 * ATOM_F + NBR_F
        d_out = 2 * ATOM_F
        return {'atom_in_fea': jax.random.normal(ks[0], (N_NODES, ATOM_F), dtype=jnp.float32), 'nbr_fea': jax.random.normal(ks[1], (N_EDGES, NBR_F), dtype=jnp.float32), 'edge_src': jax.random.randint(ks[2], (N_EDGES,), 0, N_NODES), 'edge_dst': jax.random.randint(ks[3], (N_EDGES,), 0, N_NODES), 'W_full': jax.random.normal(ks[4], (d_in, d_out), dtype=jnp.float32) / np.sqrt(d_in), 'b_full': jnp.zeros((d_out,), dtype=jnp.float32), 'bn1_g': jnp.ones((d_out,), dtype=jnp.float32), 'bn1_b': jnp.zeros((d_out,), dtype=jnp.float32), 'bn2_g': jnp.ones((ATOM_F,), dtype=jnp.float32), 'bn2_b': jnp.zeros((ATOM_F,), dtype=jnp.float32)}
    _L1_gnn_all = _L1_gnn_setup()
    _L1_gnn_in = {k: v for k, v in _L1_gnn_all.items() if k in ('W_full', 'b_full', 'bn1_g', 'bn1_b', 'bn2_g', 'bn2_b')}
    del _L1_gnn_all

    def _L2_gnn_setup():
        import jax, jax.numpy as jnp
        import numpy as np
        N_NODES = 100000
        N_EDGES = 25000
        D_IN = 64
        D_HID = 64
        BN_EPS = 1e-05
        key = jax.random.key(seed)
        k1, k2, k3, k4 = jax.random.split(key, 4)
        x = jax.random.normal(k1, (N_NODES, D_IN), dtype=jnp.float32)
        edge_index = jax.random.randint(k2, (2, N_EDGES), 0, N_NODES, dtype=jnp.int64)
        W = jax.random.normal(k3, (D_IN, D_HID), dtype=jnp.float32) * (1.0 / np.sqrt(D_IN))
        b = jax.random.normal(k4, (D_HID,), dtype=jnp.float32) * 0.01
        gamma = jnp.ones((D_HID,), dtype=jnp.float32)
        beta = jnp.zeros((D_HID,), dtype=jnp.float32)
        return {'x': x, 'edge_index': edge_index, 'W': W, 'b': b, 'gamma': gamma, 'beta': beta}
    _L2_gnn_all = _L2_gnn_setup()
    _L2_gnn_in = {k: v for k, v in _L2_gnn_all.items() if k in ('W', 'b', 'gamma', 'beta')}
    del _L2_gnn_all

    def _L3_gnn_setup():
        import jax, jax.numpy as jnp
        import numpy as np
        N = 100000
        E = 25000
        D = 64

        def _gcn_layer(x, row, col, ew, W, b):
            n = x.shape[0]
            loop = jnp.arange(n, dtype=row.dtype)
            r = jnp.concatenate([row, loop])
            c = jnp.concatenate([col, loop])
            w = jnp.concatenate([ew, jnp.ones((n, 1), ew.dtype)])
            h = x @ W.T + b
            deg = jax.ops.segment_sum(jnp.ones(r.shape[0], h.dtype), c, num_segments=n)[:, None]
            dis = jnp.where(deg > 0, deg ** (-0.5), 0.0)
            norm = dis[r] * w * dis[c]
            return jax.ops.segment_sum(norm * h[r], c, num_segments=n)
        key = jax.random.key(seed)
        ks = jax.random.split(key, 8)
        x = jax.random.normal(ks[0], (N, D), dtype=jnp.float32)
        row = jax.random.randint(ks[1], (E,), 0, N, dtype=jnp.int32)
        off = jax.random.randint(ks[2], (E,), 1, N, dtype=jnp.int32)
        col = ((row + off) % N).astype(jnp.int32)
        edge_index = jnp.stack([row, col])
        edge_weight = jax.random.uniform(ks[3], (E, 1), dtype=jnp.float32)
        s = 1.0 / np.sqrt(D)
        W1 = jax.random.uniform(ks[4], (D, D), minval=-s, maxval=s, dtype=jnp.float32)
        b1 = jax.random.uniform(ks[5], (D,), minval=-s, maxval=s, dtype=jnp.float32)
        W2 = jax.random.uniform(ks[6], (D, D), minval=-s, maxval=s, dtype=jnp.float32)
        b2 = jax.random.uniform(ks[7], (D,), minval=-s, maxval=s, dtype=jnp.float32)
        return {'x': x, 'edge_index': edge_index, 'edge_weight': edge_weight, 'W1': W1, 'b1': b1, 'W2': W2, 'b2': b2}
    _L3_gnn_all = _L3_gnn_setup()
    _L3_gnn_in = {k: v for k, v in _L3_gnn_all.items() if k in ('W1', 'b1', 'W2', 'b2')}
    del _L3_gnn_all
    return {'x': x, 'src': src, 'dst': dst, 'edge_attr_64': edge_attr_64, 'edge_weight1': edge_weight1, 'L0_gnn_W1': _L0_gnn_in['W1'], 'L0_gnn_b1': _L0_gnn_in['b1'], 'L0_gnn_W2': _L0_gnn_in['W2'], 'L0_gnn_b2': _L0_gnn_in['b2'], 'L1_gnn_W_full': _L1_gnn_in['W_full'], 'L1_gnn_b_full': _L1_gnn_in['b_full'], 'L1_gnn_bn1_g': _L1_gnn_in['bn1_g'], 'L1_gnn_bn1_b': _L1_gnn_in['bn1_b'], 'L1_gnn_bn2_g': _L1_gnn_in['bn2_g'], 'L1_gnn_bn2_b': _L1_gnn_in['bn2_b'], 'L2_gnn_W': _L2_gnn_in['W'], 'L2_gnn_b': _L2_gnn_in['b'], 'L2_gnn_gamma': _L2_gnn_in['gamma'], 'L2_gnn_beta': _L2_gnn_in['beta'], 'L3_gnn_W1': _L3_gnn_in['W1'], 'L3_gnn_b1': _L3_gnn_in['b1'], 'L3_gnn_W2': _L3_gnn_in['W2'], 'L3_gnn_b2': _L3_gnn_in['b2']}

def reference(x, src, dst, edge_attr_64, edge_weight1, L0_gnn_W1, L0_gnn_b1, L0_gnn_W2, L0_gnn_b2, L1_gnn_W_full, L1_gnn_b_full, L1_gnn_bn1_g, L1_gnn_bn1_b, L1_gnn_bn2_g, L1_gnn_bn2_b, L2_gnn_W, L2_gnn_b, L2_gnn_gamma, L2_gnn_beta, L3_gnn_W1, L3_gnn_b1, L3_gnn_W2, L3_gnn_b2):
    import jax
    import jax.numpy as jnp

    def _L0_gnn_ref(z, edge_index, W1, b1, W2, b2):
        import jax, jax.numpy as jnp
        import numpy as np
        N_NODES = 100000

        def gcn_conv(x, W, b, src, dst, n):
            h = x @ W
            loop = jnp.arange(n, dtype=src.dtype)
            s = jnp.concatenate([src, loop])
            d = jnp.concatenate([dst, loop])
            deg = jax.ops.segment_sum(jnp.ones_like(d, dtype=h.dtype), d, num_segments=n)
            dinv = jnp.where(deg > 0, jax.lax.rsqrt(deg), 0.0)
            norm = dinv[s] * dinv[d]
            msg = h[s] * norm[:, None]
            out = jax.ops.segment_sum(msg, d, num_segments=n)
            return out + b
        n = z.shape[0]
        src, dst = (edge_index[0], edge_index[1])
        h = gcn_conv(z, W1, b1, src, dst, n)
        h = jax.nn.relu(h)
        x_hat = gcn_conv(h, W2, b2, src, dst, n)
        return x_hat

    def _L1_gnn_ref(atom_in_fea, nbr_fea, edge_src, edge_dst, W_full, b_full, bn1_g, bn1_b, bn2_g, bn2_b):
        import jax, jax.numpy as jnp
        import numpy as np
        N_NODES = 50000
        N_EDGES = 12500
        ATOM_F = 64
        NBR_F = 64
        EPS = 1e-05

        def batch_norm(x, gamma, beta):
            mu = x.mean(axis=0)
            var = x.var(axis=0)
            return gamma * (x - mu) * jax.lax.rsqrt(var + EPS) + beta
        atom_src = atom_in_fea[edge_src]
        atom_dst = atom_in_fea[edge_dst]
        total = jnp.concatenate([atom_src, atom_dst, nbr_fea], axis=1)
        total = batch_norm(total @ W_full + b_full, bn1_g, bn1_b)
        filter_fea, core_fea = jnp.split(total, 2, axis=1)
        nbr_msg = jax.nn.sigmoid(filter_fea) * jax.nn.softplus(core_fea)
        atom_update = jax.ops.segment_sum(nbr_msg, edge_dst, num_segments=atom_in_fea.shape[0])
        return jax.nn.softplus(atom_in_fea + batch_norm(atom_update, bn2_g, bn2_b))

    def _L2_gnn_ref(x, edge_index, W, b, gamma, beta):
        import jax, jax.numpy as jnp
        import numpy as np
        N_NODES = 100000
        N_EDGES = 25000
        D_IN = 64
        D_HID = 64
        BN_EPS = 1e-05
        src = edge_index[0]
        dst = edge_index[1]
        agg = jax.ops.segment_sum(x[src], dst, num_segments=x.shape[0])
        h = (x + agg) @ W + b
        mu = jnp.mean(h, axis=0)
        var = jnp.var(h, axis=0)
        h = gamma * (h - mu) * jax.lax.rsqrt(var + BN_EPS) + beta
        return jax.nn.relu(h)

    def _L3_gnn_ref(x, edge_index, edge_weight, W1, b1, W2, b2):
        import jax, jax.numpy as jnp
        import numpy as np
        N = 100000
        E = 25000
        D = 64

        def _gcn_layer(x, row, col, ew, W, b):
            n = x.shape[0]
            loop = jnp.arange(n, dtype=row.dtype)
            r = jnp.concatenate([row, loop])
            c = jnp.concatenate([col, loop])
            w = jnp.concatenate([ew, jnp.ones((n, 1), ew.dtype)])
            h = x @ W.T + b
            deg = jax.ops.segment_sum(jnp.ones(r.shape[0], h.dtype), c, num_segments=n)[:, None]
            dis = jnp.where(deg > 0, deg ** (-0.5), 0.0)
            norm = dis[r] * w * dis[c]
            return jax.ops.segment_sum(norm * h[r], c, num_segments=n)
        row, col = (edge_index[0], edge_index[1])
        h = jax.nn.relu(_gcn_layer(x, row, col, edge_weight, W1, b1))
        out = jax.nn.sigmoid(_gcn_layer(h, row, col, edge_weight, W2, b2))
        return out
    edge_index = jnp.stack([src, dst])
    x = _layernorm(x + _L0_gnn_ref(x, edge_index, L0_gnn_W1, L0_gnn_b1, L0_gnn_W2, L0_gnn_b2), axis=-1)
    x = _layernorm(x + _L1_gnn_ref(x, edge_attr_64, src, dst, L1_gnn_W_full, L1_gnn_b_full, L1_gnn_bn1_g, L1_gnn_bn1_b, L1_gnn_bn2_g, L1_gnn_bn2_b), axis=-1)
    x = _layernorm(x + _L2_gnn_ref(x, edge_index, L2_gnn_W, L2_gnn_b, L2_gnn_gamma, L2_gnn_beta), axis=-1)
    x = _layernorm(x + _L3_gnn_ref(x, edge_index, edge_weight1, L3_gnn_W1, L3_gnn_b1, L3_gnn_W2, L3_gnn_b2), axis=-1)
    return x

_drawn_inputs = setup_inputs


def setup_inputs(seed=0):
    import zlib

    import numpy as np

    out = dict(_drawn_inputs(seed))
    spreads = {'L0_gnn_b1': (0.0, 0.1),
     'L0_gnn_b2': (0.0, 0.1),
     'L1_gnn_b_full': (0.0, 0.8),
     'L1_gnn_bn1_g': (1.0, 0.2),
     'L1_gnn_bn1_b': (0.0, 0.8),
     'L1_gnn_bn2_g': (1.0, 0.2),
     'L1_gnn_bn2_b': (0.0, 0.303),
     'L2_gnn_gamma': (1.0, 0.2),
     'L2_gnn_beta': (0.0, 0.1)}
    factors = {'edge_weight1': 6.962, 'L2_gnn_b': 8.0, 'L3_gnn_b1': 7.938, 'L3_gnn_b2': 3.052}
    for name, (base, spread) in spreads.items():
        noise = np.random.default_rng([zlib.crc32(name.encode()), seed]).standard_normal(out[name].shape)
        drawn = base * np.exp(spread * noise) if base else spread * noise
        out[name] = jnp.asarray(drawn.astype(out[name].dtype))
    for name, factor in factors.items():
        out[name] = (out[name] * factor).astype(out[name].dtype)
    return out
```

```python
import numpy as np
import concourse.bass as bass
import concourse.mybir as mybir
from contextlib import ExitStack

F32 = mybir.dt.float32
I32 = mybir.dt.int32
ALU = mybir.AluOpType
ACT = mybir.ActivationFunctionType

NODES, EDGES, D, HID = 100000, 25000, 64, 128
COLS = 500
PACK = 2 * COLS
TILE = 125
TILES = PACK // TILE
NODE_CHUNKS = NODES // PACK
BLOCKS = EDGES // PACK
NAT = 100
SKIP = 1 << 20
EPS = 1e-5


class Sems:

    def __init__(self, make):
        self.make, self.sem, self.total = make, {}, {}
        self.passed = {}

    def wait(self, eng, sem, value):
        eng.wait_ge(sem, value)
        if not isinstance(value, int) and id(eng) in self.passed:
            eng.sem_inc(self.passed[id(eng)], 1)

    def get(self, name):
        if name not in self.sem:
            self.sem[name], self.total[name] = self.make(name), 0
        return self.sem[name]


class Phase:

    def __init__(self, sems, chunks, steps, dmas):
        self.chunks, self.sems, self.steps, self.dmas = chunks, sems, steps, dmas
        self.base = {}
        for name, count in steps.items():
            sems.get(name)
            self.base[name] = sems.total[name]
            sems.total[name] += chunks * count
        for name, count in dmas.items():
            for u in (0, 1):
                slot = f"{name}{u}"
                sems.get(slot)
                self.base[slot] = sems.total[slot]
                sems.total[slot] += (chunks + 1 - u) // 2 * 16 * count
        self.ends = [(sems.sem[n], self.base[n] + chunks * c) for n, c in steps.items()]
        self.ends += [(sems.sem[f"{n}{u}"], self.base[f"{n}{u}"] + (chunks + 1 - u) // 2 * 16 * c)
                      for n, c in dmas.items() for u in (0, 1)]

    def s(self, name):
        return self.sems.sem[name]

    def wait(self, eng, step, n, part=None):
        q = self.steps[step]
        part = q if part is None else part
        self.sems.wait(eng, self.s(step), self.base[step] + n * q + part)

    def free(self, eng, step, i, u):
        if not (isinstance(i, int) and i == 0):
            self.wait(eng, step, 2 * i + u - 2)

    def landed(self, eng, dma, i, u):
        slot = f"{dma}{u}"
        self.sems.wait(eng, self.s(slot), self.base[slot] + (i + 1) * (16 * self.dmas[dma]))

    def stored(self, eng, dma, i, u):
        if not (isinstance(i, int) and i == 0):
            slot = f"{dma}{u}"
            self.sems.wait(eng, self.s(slot), self.base[slot] + i * (16 * self.dmas[dma]))

    def all_done(self, eng):
        for sem, value in self.ends:
            if value:
                eng.wait_ge(sem, value)


def in_pairs(eng, chunks, body):
    body(0, (0, 1))
    if chunks // 2 > 1:
        with eng.Fori(1, chunks // 2) as i:
            body(i, (0, 1))
    if chunks % 2:
        body(chunks // 2, (0,))


def gnn(nc, xt, x, src_in, dstp, ea_in, ew, w1, w2, w2t, b1, b2, wf, bf, g1, be1, g2, be2,
        wl2, bl2, g3, be3, w31t, b31, w32t, b32, out):
    def dram(name, *shape):
        return nc.dram_tensor(name, list(shape), F32).ap()

    XDR, XSR = dram("xdr", BLOCKS, TILE, 512), dram("xsr", BLOCKS, TILE, 512)
    SLOTS = dram("slots", NODES, 4)
    XE = dram("xe", 2 * BLOCKS, 128, COLS)
    X1 = dram("x1", NODE_CHUNKS + 2 * BLOCKS, 128, COLS)
    X2 = dram("x2", NODE_CHUNKS + 2 * BLOCKS, 128, COLS)
    GU, GD = dram("gu", 2 * BLOCKS, 128, COLS), dram("gd", BLOCKS, 128, COLS)
    X1D, X1F = dram("x1d", BLOCKS, 128, COLS), dram("x1f", BLOCKS, 128, COLS)
    TF, TC, UPD = (dram(n, BLOCKS, 128, COLS) for n in ("tf", "tc", "upd"))
    X2D, X2S, HD = (dram(n, BLOCKS, 128, COLS) for n in ("x2d", "x2s", "hd"))
    X3D, X3S, QS, QD = (dram(n, BLOCKS, 128, COLS) for n in ("x3d", "x3s", "qs", "qd"))
    TAB = [dram(f"tab{n}", EDGES, D) for n in range(5)]
    OV = [dram(f"ov{n}", BLOCKS, TILE, 512) for n in range(5)]
    ROWS = {n: dram(f"row_{n}", EDGES) for n in ("same", "more", "dinv", "keep", "sdinv", "wd", "w")}
    META_S = dram("meta_sorted", EDGES + 2, 4)
    EA_S = dram("ea_sorted", EDGES + 2, D)

    ctx = ExitStack()
    with ctx:
        def sb(name, shape, dt=F32):
            return ctx.enter_context(nc.sbuf_tensor(name, list(shape), dt))

        def sem(name):
            return ctx.enter_context(nc.semaphore(name))

        bank = [ctx.enter_context(nc.psum_tensor(f"bank{k}", [128, 512], F32)) for k in range(8)]

        ident, J, C, HALF = (sb(n, [128, 128]) for n in ("ident", "J", "C", "HALF"))
        MATS = ["w1a", "w1b", "w2a", "w2b", "w2ca", "w2cb", "srcf", "dstf", "nbrf", "srcc", "dstc",
                "nbrc", "wl2", "w31", "w32"]
        mats = sb("mats", [128, len(MATS), 128])
        M = {n: mats[:, k, :] for k, n in enumerate(MATS)}
        w2t_sb = sb("w2t_sb", [D, HID])
        CN = ["b1", "b2", "bf", "bc", "g1f", "g1c", "be1f", "be1c", "g2", "be2", "bl2", "g3", "be3",
              "b31", "b32", "cb2", "s1f", "t1f", "s1c", "t1c", "s2", "t2", "nt2",
              "ct2", "s3", "t3", "eps", "tmp0", "tmp1", "tmp2", "tmp3"]
        cols = sb("cols", [128, len(CN)])
        K = {n: cols[:, k:k + 1] for k, n in enumerate(CN)}
        nat_i = sb("nat_i", [NAT, 4, 250], I32)
        nat = sb("nat", [NAT, 12, 250])
        tiny = sb("tiny", [1, 4, NAT])
        carry_in = sb("carry_in", [NAT, 1])
        col = sb("col", [TILE, 4, 200])
        idx_src, idx_dst, idx_last = (sb(n, [TILE, 200], I32) for n in ("idx_src", "idx_dst", "idx_last"))
        idx_f = sb("idx_f", [TILE, 200])
        slot_rows = sb("slot_rows", [TILE, 200, 4])
        row_no = sb("row_no", [TILE, 200], I32)
        src_info = sb("src_info", [TILE, 200, 4])
        default = sb("default", [TILE, NODES // TILE, 4])
        gat = sb("gat", [TILE, 2, TILES, D])
        gidx = sb("gidx", [TILE, 2, TILES], I32)
        grow = sb("grow", [TILE, 2, TILES, 4])
        NB = ["in0", "in1", "in2", "in3", "in4", "same", "keep", "more", "wts", "dinv",
              "a", "b", "c", "d", "e", "f", "g", "h", "g2", "o0", "o1", "o2", "o3"]
        bufs = sb("bufs", [128, len(NB), 2, COLS])
        B = {n: bufs[:, k] for k, n in enumerate(NB)}
        rows_in = [sb(f"rows_in{k}", [TILE, 2, TILES, D]) for k in range(2)]
        rows_out = sb("rows_out", [TILE, 2, TILES, D])
        carry = sb("carry", [128, 1])
        viol = sb("viol", [NAT, 1])
        flag = sb("flag", [1, 1], I32)
        pad = sb("pad", [1, 4])
        key_col, edge_col = sb("key_col", [TILE, 1]), sb("edge_col", [TILE, 1])
        part, rank = sb("part", [TILE, PER]), sb("rank", [TILE, PER])
        arena = bufs[0:TILE, :, :, :].rearrange("p n u c -> p (n u c)")
        key_i, key_f, no_i, no_f = (arena[:, k * KEYS:(k + 1) * KEYS] for k in range(4))
        key_i, no_i, work = key_i.bitcast(I32), no_i.bitcast(I32), no_i
        own_i = arena[:, 4 * KEYS:4 * KEYS + 2 * PER].rearrange("p (k t) -> p k t", k=2).bitcast(I32)
        own_no = arena[:, 4 * KEYS + 2 * PER:4 * KEYS + 3 * PER].bitcast(I32)
        own_f = arena[:, 4 * KEYS + 3 * PER:4 * KEYS + 6 * PER].rearrange("p (k t) -> p k t", k=3)
        meta = src_info
        rank_i = idx_last
        meta_in = bufs[0:NAT, :, :, :].rearrange("p n u c -> p (n u c)")[:, 0:3000].rearrange("p (k c) -> p k c", k=3)
        stats = {n: sb(f"stats_{n}", [128, k, 6]) for n, k in
                 (("f", BLOCKS), ("c", BLOCKS), ("u", BLOCKS), ("n", NODE_CHUNKS), ("hd", BLOCKS), ("hu", BLOCKS))}
        mv = sb("mv", [128, 8, 2])
        mom = sb("mom", [128, 8, 2])
        hold = sb("hold", [128, 8])

        sems = Sems(sem)
        SIG = {"nabs": 1, "lsig": 2, "arg": 1, "sig": 1}
        LN = {"y": 1, "sq": 1, "var": 1, "lnv": 1, "rstd": 1, "out": 1}
        P_node0 = Phase(sems, NODE_CHUNKS, {"hid": 1, "relu0": 1, "relu1": 1, **LN}, {"ld": 1, "st": 1})
        P_e0 = Phase(sems, BLOCKS, {"tr": 1, "evs": 1, "evd": 1, "msg": 1, "scan": 4, "vec": 3, "hid": 1,
                                    "relu0": 1, "relu1": 1, "g": 1, "out": 1, "row": 1, "evrow": 1},
                     {"ld": 8, "st": 4})
        P_node0e = Phase(sems, 2 * BLOCKS, {"hid": 1, "relu0": 1, "relu1": 1, "g": 1, "evs": 1, **LN},
                         {"ld": 1, "st": 2})
        P_e1 = Phase(sems, BLOCKS, {"tr": 1, "msg": 2, "scan": 4, "vec": 3, **LN, "row": 1, "evrow": 1},
                     {"ld": 10, "st": 2})
        P_e2 = Phase(sems, BLOCKS, {"tr": 1, "evs": 1, "msg": 2, "vec": 1, "scan": 4, "t": 1, "evf": 1,
                                    "evc": 1, "bnf": 1, "bnc": 1}, {"ld": 9, "st": 4})
        P_e3 = Phase(sems, BLOCKS, {"act": 3, "msg": 2, **SIG, "vec": 2, "scan": 4, "out": 1, "bnf": 1}, {"ld": 6, "st": 1})
        P_e4 = Phase(sems, BLOCKS, {"msg": 1, "vec": 2, "act": 3, **LN, "row": 1, "evrow": 1}, {"ld": 2, "st": 2})
        P_node1 = Phase(sems, NODE_CHUNKS, {"vec": 2, "act": 3, **LN, "h": 1, "bnf": 1}, {"ld": 1, "st": 1})
        P_node1e = Phase(sems, 2 * BLOCKS, {"vec": 2, "act": 3, **LN}, {"ld": 1, "st": 1})
        P_e5 = Phase(sems, BLOCKS, {"tr": 1, "msg": 2, "scan": 4, "vec": 1, "h": 1, "evs": 1, "mask": 2,
                                    "bnf": 1, "bnc": 1}, {"ld": 10, "st": 2})
        P_e6 = Phase(sems, BLOCKS, {"act": 1, "vec": 1, **LN, "row": 1, "evrow": 1}, {"ld": 2, "st": 2})
        P_e6s = Phase(sems, BLOCKS, {"h": 1, "act": 1, "vec": 1, **LN}, {"ld": 1, "st": 1})
        P_node2 = Phase(sems, NODE_CHUNKS,
                        {"h": 1, "act": 1, "vec": 1, **LN, "hid": 1, "relu0": 1, "g": 1, "z": 1, **SIG,
                         "add": 1, "y2": 1, "sq2": 1, "var2": 1, "lnv2": 1, "rstd2": 1, "out2": 1, "row": 1, "evrow": 1},
                        {"ld": 1, "st": 1})
        P_e7 = Phase(sems, BLOCKS, {"tr": 1, "msg": 2, "hid": 1, "evs": 1, "evd": 1, "relu0": 1, "vec": 4,
                                    "scan": 4, "relu1": 1, "g": 1, "h": 1, "act": 1, "out": 1, "row": 1,
                                    "evrow": 1}, {"ld": 11, "st": 3})
        P_e8 = Phase(sems, BLOCKS, {"tr": 1, "msg": 3, "scan": 4, "vec": 2, **SIG, "add": 1,
                                    **LN, "row": 1, "evrow": 1}, {"ld": 12})

        s_w, s_nat, s_def, s_rows = sem("s_w"), sem("s_nat"), sem("s_def"), sem("s_rows")
        s_const, s_dconst, s_setup, s_tcol, s_ccol = (sem(n) for n in
                                                      ("s_const", "s_dconst", "s_setup", "s_tcol", "s_ccol"))
        s_pe_small, s_dv_small, s_idx = sem("s_pe_small"), sem("s_dv_small"), sem("s_idx")
        s_info, s_ac_small = sem("s_info"), sem("s_ac_small")
        s_gcopy, s_gather = sem("s_gcopy"), [sem("s_gather0"), sem("s_gather1")]
        s_gstore = [sem("s_gstore0"), sem("s_gstore1")]
        s_scatter = [sem("s_scatter0"), sem("s_scatter1")]
        s_iota = sem("s_iota")
        s_flag, s_own, s_keys, s_keys_used, s_rank, s_numbered, s_ranked = (sem(n) for n in (
            "s_flag", "s_own", "s_keys", "s_keys_used", "s_rank", "s_numbered", "s_ranked"))
        s_ea_in, s_rank_copy, s_sorted, s_meta, s_pad, s_ea = (sem(n) for n in (
            "s_ea_in", "s_rank_copy", "s_sorted", "s_meta", "s_pad", "s_ea"))
        s_passed_sp, s_passed_pool = sem("s_passed_sp"), sem("s_passed_pool")

        POOL = ["xd", "slot", "info", "xs", "ov0", "ov1", "ov2", "ov3", "ov4", "final"]
        per_slot = [(BLOCKS + 1 - u) // 2 for u in (0, 1)]
        GATHERS = [n for n in POOL if n not in ("slot", "final")]
        STORES = [n for n in GATHERS if n != "info"]

        def gather_base(name, u):
            return GATHERS.index(name) * per_slot[u] * 16 * TILES

        def store_base(name, u):
            return STORES.index(name) * per_slot[u] * 16

        def gathered(eng, name, i, u):
            sems.wait(eng, s_gstore[u], store_base(name, u) + (i + 1) * 16)

        block = ctx.enter_context(nc.Block())

        @block.sync
        def _(sp):
            def halves(name, tile, blk):
                row = ROWS[name]
                for h in (0, 1):
                    yield tile[64 * h:64 * h + 64, :], \
                        row[bass.ds(blk * PACK + h * COLS, COLS)].rearrange("(o c) -> o c", o=1).to_broadcast([64, COLS])

            for k, off in enumerate((0, 1, 2)):
                sp.dma_start(nat_i[:, k, :], dstp[off:off + EDGES].rearrange("(a b) -> a b", a=NAT)).then_inc(s_nat, 16)
            sp.dma_start(nat_i[:, 3, :], src_in.rearrange("(a b) -> a b", a=NAT)).then_inc(s_nat, 16)
            sp.dma_start(nat[:, 11, :], ew.rearrange("(a b) -> a b", a=NAT)).then_inc(s_nat, 16)
            sems.passed[id(sp)] = s_passed_sp
            sp.wait_ge(s_dconst, 1)

            def twice(name, src):
                for h in (0, 1):
                    sp.dma_start(M[name][64 * h:64 * h + 64, 64 * h:64 * h + 64], src).then_inc(s_w, 16)

            sp.dma_start(M["w1a"][0:64, :], w1).then_inc(s_w, 16)
            sp.dma_start(M["w1b"][64:128, :], w1).then_inc(s_w, 16)
            sp.dma_start(M["w2a"][:, 0:64], w2).then_inc(s_w, 16)
            sp.dma_start(M["w2b"][:, 64:128], w2).then_inc(s_w, 16)
            sp.dma_start(w2t_sb[:, :], w2t).then_inc(s_w, 16)
            for part, o in (("f", 0), ("c", 64)):
                for k, name in enumerate(("src", "dst", "nbr")):
                    twice(name + part, wf[64 * k:64 * k + 64, o:o + 64])
            twice("wl2", wl2)
            twice("w31", w31t)
            twice("w32", w32t)

            def column(name, src):
                n = src.shape[0]
                for h in range(128 // n):
                    sp.dma_start(K[name][n * h:n * h + n, :], src.rearrange("(a o) -> a o", o=1)).then_inc(s_w, 16)

            for name, src in (("b1", b1), ("b2", b2), ("bf", bf[0:64]), ("bc", bf[64:128]), ("g1f", g1[0:64]),
                              ("g1c", g1[64:128]), ("be1f", be1[0:64]), ("be1c", be1[64:128]), ("g2", g2),
                              ("be2", be2), ("bl2", bl2), ("g3", g3), ("be3", be3), ("b31", b31), ("b32", b32)):
                column(name, src)
            sp.wait_ge(s_dconst, 6)
            sp.dma_start(SLOTS.rearrange("(p t) c -> p (t c)", p=TILE),
                         default[:, :, :].rearrange("p t c -> p (t c)")).then_inc(s_def, 16)
            sp.wait_ge(s_flag, 2)
            unsorted = sp.value_load(flag[0:1, 0:1])
            with sp.If(unsorted > 0):
                for k, row in enumerate((dstp[1:1 + EDGES], src_in)):
                    sp.dma_start(own_i[:, k, :], row.rearrange("(p t) -> p t", p=TILE)).then_inc(s_own, 16)
                sp.dma_start(own_f[:, 2, :], ew.rearrange("(p t) -> p t", p=TILE)).then_inc(s_own, 16)
                for r in (0, EDGES + 1):
                    sp.dma_start(META_S[r:r + 1, :], pad[:, :]).then_inc(s_pad, 16)
                for c in range(EDGES // KEYS):
                    if c:
                        sp.wait_ge(s_keys_used, c)
                    sp.dma_start(key_i, dstp[1 + c * KEYS:1 + (c + 1) * KEYS].rearrange("(o c) -> o c", o=1)
                                 .to_broadcast([TILE, KEYS])).then_inc(s_keys, 16)
                sp.wait_ge(s_sorted, BLOCKS * TILES * 2 * 16)
                sp.wait_ge(s_pad, 32)
                for off in (0, 1, 2):
                    sp.dma_start(meta_in[:, off, :], META_S[off:off + EDGES, :].rearrange("(a b) c -> a (b c)", a=NAT))\
                      .then_inc(s_meta, 16)
                sp.wait_ge(s_rank, SORT_END)
                sp.sem_inc(s_ea, 16)
            with sp.Else():
                sp.dma_start(EA_S[1:1 + EDGES, :], ea_in).then_inc(s_ea, 16)
            sp.wait_ge(s_setup, SETUP_ROWS)
            sp.dma_start(ROWS["w"].rearrange("(a b) -> a b", a=NAT), nat[:, 11, :]).then_inc(s_rows, 16)
            for k, name in ((4, "same"), (6, "more"), (10, "dinv")):
                sp.dma_start(ROWS[name].rearrange("(a b) -> a b", a=NAT), nat[:, k, :]).then_inc(s_rows, 16)

            def run(P, load, store, before=None):
                if before:
                    before()
                last = (P.chunks + 1) // 2

                def slots(i):
                    return (0, 1) if i * 2 + 1 < P.chunks else (0,)

                def loads(i, us):
                    for u in us:
                        for dst, src in load(i, u):
                            sp.dma_start(dst, src).then_inc(P.s(f"ld{u}"), 16)

                def stores(i, us):
                    for u in us:
                        for dst, src in store(i, u):
                            sp.dma_start(dst, src).then_inc(P.s(f"st{u}"), 16)

                loads(0, slots(0))
                loads(1, slots(1))
                stores(0, slots(0))
                if last - 2 > 1:
                    with sp.Fori(1, last - 2) as i:
                        loads(i + 1, (0, 1))
                        stores(i, (0, 1))
                loads(last - 1, slots(last - 1))
                stores(last - 2, (0, 1))
                stores(last - 1, slots(last - 1))

            def load(i, u):
                P_node0.free(sp, "y", i, u)
                yield B["in0"][:, u, :], xt[2 * i + u, :, :]

            def store(i, u):
                P_node0.wait(sp, "out", 2 * i + u)
                yield X1[2 * i + u, :, :], B["o0"][:, u, :]
            run(P_node0, load, store)
            P_node0.all_done(sp)

            sp.wait_ge(s_info, INFO_ROWS)
            for k, name in ((0, "keep"), (1, "sdinv"), (2, "wd")):
                sp.dma_start(ROWS[name].rearrange("(a b) -> a b", a=NAT), nat[:, k, :]).then_inc(s_rows, 16)
            sp.wait_ge(s_rows, 7 * 16)

            def load(i, u):
                n = 2 * i + u
                P_e0.free(sp, "tr", i, u)
                P_e0.free(sp, "out", i, u)
                gathered(sp, "xs", i, u)
                yield rows_in[0][:, u, :, :].rearrange("p t f -> p (t f)"), XSR[n, :, :]
                yield rows_in[1][:, u, :, :].rearrange("p t f -> p (t f)"), XDR[n, :, :]
                yield from halves("same", B["same"][:, u, :], n)
                yield from halves("sdinv", B["wts"][:, u, :], n)
                yield from halves("dinv", B["dinv"][:, u, :], n)

            def store(i, u):
                n = 2 * i + u
                P_e0.wait(sp, "evs", n)
                yield XE[n, :, :], B["o1"][:, u, :]
                P_e0.wait(sp, "evd", n)
                yield XE[BLOCKS + n, :, :], B["o2"][:, u, :]
                P_e0.wait(sp, "out", n)
                yield GD[n, :, :], B["o0"][:, u, :]
                P_e0.wait(sp, "evrow", n)
                yield table(0, n), flat(u)

            def table(t, n):
                return TAB[t].rearrange("(k p t) f -> k p (t f)", p=TILE, t=TILES)[n, :, :]

            def flat(u):
                return rows_out[:, u, :, :].rearrange("p t f -> p (t f)")
            run(P_e0, load, store)
            P_e0.all_done(sp)

            def load(i, u):
                P_node0e.free(sp, "y", i, u)
                yield B["in0"][:, u, :], XE[2 * i + u, :, :]

            def store(i, u):
                P_node0e.wait(sp, "evs", 2 * i + u)
                yield GU[2 * i + u, :, :], B["o1"][:, u, :]
                P_node0e.wait(sp, "out", 2 * i + u)
                yield X1[2 * i + u + NODE_CHUNKS, :, :], B["o0"][:, u, :]
            run(P_node0e, load, store)
            P_node0e.all_done(sp)

            def load(i, u):
                n = 2 * i + u
                P_e1.free(sp, "out", i, u)
                gathered(sp, "ov0", i, u)
                yield rows_in[0][:, u, :, :].rearrange("p t f -> p (t f)"), OV[0][n, :, :]
                yield B["in0"][:, u, :], GU[n, :, :]
                yield B["in1"][:, u, :], XE[BLOCKS + n, :, :]
                yield B["in2"][:, u, :], GD[n, :, :]
                yield from halves("same", B["same"][:, u, :], n)
                yield from halves("keep", B["keep"][:, u, :], n)
                yield from halves("dinv", B["dinv"][:, u, :], n)

            def store(i, u):
                n = 2 * i + u
                P_e1.wait(sp, "out", n)
                yield X1D[n, :, :], B["o0"][:, u, :]
                P_e1.wait(sp, "evrow", n)
                yield table(1, n), flat(u)
            run(P_e1, load, store)
            P_e1.all_done(sp)

            sp.wait_ge(s_ea, 16)

            def load(i, u):
                n = 2 * i + u
                k = BLOCKS - 1 - n
                P_e2.free(sp, "bnf", i, u)
                P_e2.free(sp, "bnc", i, u)
                gathered(sp, "ov1", i, u)
                yield rows_in[0][:, u, :, :].rearrange("p t f -> p (t f)"), OV[1][k, :, :]
                for h in (0, 1):
                    yield rows_in[1][:, u, h::2, :], \
                        EA_S[bass.ds(k * PACK + h * COLS + 1, COLS), :].rearrange("(t p) f -> p t f", p=TILE)
                yield B["in0"][:, u, :], X1[k + NODE_CHUNKS, :, :]
                yield B["in1"][:, u, :], X1D[k, :, :]
                yield from halves("keep", B["keep"][:, u, :], k)
                yield from halves("more", B["more"][:, u, :], k)

            def store(i, u):
                n = 2 * i + u
                k = BLOCKS - 1 - n
                P_e2.wait(sp, "scan", n)
                yield X1F[k, :, :], B["o0"][:, u, :]
                P_e2.wait(sp, "evf", n)
                yield TF[k, :, :], B["o1"][:, u, :]
                P_e2.wait(sp, "evc", n)
                yield TC[k, :, :], B["o2"][:, u, :]
                P_e2.wait(sp, "msg", n)
                yield X2S[k, :, :], B["o3"][:, u, :]
            run(P_e2, load, store)
            P_e2.all_done(sp)

            def load(i, u):
                n = 2 * i + u
                P_e3.free(sp, "out", i, u)
                yield B["in0"][:, u, :], TF[n, :, :]
                yield B["in1"][:, u, :], TC[n, :, :]
                yield from halves("same", B["same"][:, u, :], n)
                yield from halves("more", B["more"][:, u, :], n)

            def store(i, u):
                P_e3.wait(sp, "out", 2 * i + u)
                yield UPD[2 * i + u, :, :], B["o0"][:, u, :]
            run(P_e3, load, store)
            P_e3.all_done(sp)

            def load(i, u):
                P_e4.free(sp, "out", i, u)
                yield B["in0"][:, u, :], X1F[2 * i + u, :, :]
                yield B["in1"][:, u, :], UPD[2 * i + u, :, :]

            def store(i, u):
                P_e4.wait(sp, "out", 2 * i + u)
                yield X2D[2 * i + u, :, :], B["o0"][:, u, :]
                P_e4.wait(sp, "evrow", 2 * i + u)
                yield table(2, 2 * i + u), flat(u)
            run(P_e4, load, store)
            P_e4.all_done(sp)

            def load(i, u):
                P_node1.free(sp, "out", i, u)
                yield B["in0"][:, u, :], X1[2 * i + u, :, :]

            def store(i, u):
                P_node1.wait(sp, "out", 2 * i + u)
                yield X2[2 * i + u, :, :], B["o0"][:, u, :]
            run(P_node1, load, store)
            P_node1.all_done(sp)

            def load(i, u):
                P_node1e.free(sp, "out", i, u)
                yield B["in0"][:, u, :], X1[2 * i + u + NODE_CHUNKS, :, :]

            def store(i, u):
                P_node1e.wait(sp, "out", 2 * i + u)
                yield X2[2 * i + u + NODE_CHUNKS, :, :], B["o0"][:, u, :]
            run(P_node1e, load, store)
            P_node1e.all_done(sp)

            def load(i, u):
                n = 2 * i + u
                P_e5.free(sp, "mask", i, u)
                gathered(sp, "ov2", i, u)
                yield rows_in[0][:, u, :, :].rearrange("p t f -> p (t f)"), OV[2][n, :, :]
                yield B["in0"][:, u, :], X2[n + NODE_CHUNKS, :, :]
                yield B["in1"][:, u, :], X2D[n, :, :]
                yield B["in2"][:, u, :], X2[n + NODE_CHUNKS + BLOCKS, :, :]
                yield from halves("same", B["same"][:, u, :], n)
                yield from halves("keep", B["keep"][:, u, :], n)
                yield from halves("more", B["more"][:, u, :], n)

            def store(i, u):
                n = 2 * i + u
                P_e5.wait(sp, "msg", n)
                yield X2S[n, :, :], B["o0"][:, u, :]
                P_e5.wait(sp, "evs", n)
                yield HD[n, :, :], B["o1"][:, u, :]
            run(P_e5, load, store)
            P_e5.all_done(sp)

            def load(i, u):
                P_e6.free(sp, "out", i, u)
                yield B["in0"][:, u, :], HD[2 * i + u, :, :]
                yield B["in1"][:, u, :], X2D[2 * i + u, :, :]

            def store(i, u):
                P_e6.wait(sp, "out", 2 * i + u)
                yield X3D[2 * i + u, :, :], B["o0"][:, u, :]
                P_e6.wait(sp, "evrow", 2 * i + u)
                yield table(3, 2 * i + u), flat(u)
            run(P_e6, load, store)
            P_e6.all_done(sp)

            def load(i, u):
                P_e6s.free(sp, "out", i, u)
                yield B["in0"][:, u, :], X2S[2 * i + u, :, :]

            def store(i, u):
                P_e6s.wait(sp, "out", 2 * i + u)
                yield X3S[2 * i + u, :, :], B["o0"][:, u, :]
            run(P_e6s, load, store)
            P_e6s.all_done(sp)

            def load(i, u):
                P_node2.free(sp, "vec", i, u)
                yield B["in0"][:, u, :], X2[2 * i + u, :, :]

            def store(i, u):
                P_node2.wait(sp, "evrow", 2 * i + u)
                yield out.rearrange("(k p t) f -> k p (t f)", p=TILE, t=TILES)[2 * i + u, :, :], flat(u)
            run(P_node2, load, store)
            P_node2.all_done(sp)

            def load(i, u):
                n = 2 * i + u
                P_e7.free(sp, "out", i, u)
                gathered(sp, "ov3", i, u)
                yield rows_in[0][:, u, :, :].rearrange("p t f -> p (t f)"), OV[3][n, :, :]
                yield B["in0"][:, u, :], X3S[n, :, :]
                yield B["in1"][:, u, :], X3D[n, :, :]
                yield from halves("same", B["same"][:, u, :], n)
                yield from halves("keep", B["keep"][:, u, :], n)
                yield from halves("dinv", B["dinv"][:, u, :], n)
                yield from halves("wd", B["wts"][:, u, :], n)

            def store(i, u):
                n = 2 * i + u
                P_e7.wait(sp, "act", n)
                yield QS[n, :, :], B["o1"][:, u, :]
                P_e7.wait(sp, "out", n)
                yield QD[n, :, :], B["o0"][:, u, :]
                P_e7.wait(sp, "evrow", n)
                yield table(4, n), flat(u)
            run(P_e7, load, store)
            P_e7.all_done(sp)

            def load(i, u):
                n = 2 * i + u
                P_e8.free(sp, "out", i, u)
                gathered(sp, "ov4", i, u)
                yield rows_in[0][:, u, :, :].rearrange("p t f -> p (t f)"), OV[4][n, :, :]
                yield B["in0"][:, u, :], QS[n, :, :]
                yield B["in1"][:, u, :], X3D[n, :, :]
                yield B["in2"][:, u, :], QD[n, :, :]
                yield from halves("same", B["same"][:, u, :], n)
                yield from halves("keep", B["keep"][:, u, :], n)
                yield from halves("dinv", B["dinv"][:, u, :], n)
                yield from halves("w", B["wts"][:, u, :], n)

            run(P_e8, load, lambda i, u: ())
            for u in (0, 1):
                sp.wait_ge(s_scatter[u], 2 * per_slot[u] * 16 * TILES)

        @block.gpsimd
        def _(po):
            po.memset(ident[:, :], 0.0).then_inc(s_const, 1)
            po.memset(HALF[:, :], 0.0).then_inc(s_const, 1)
            po.wait_ge(s_const, 2)
            po.affine_select(out=ident[:, :], in_=ident[:, :], compare_op=ALU.not_equal, fill=1.0, base=0,
                             pattern=[[-1, 128]], channel_multiplier=1).then_inc(s_const, 1)
            for k, base in enumerate((0, 64, -64)):
                po.affine_select(out=HALF[:, :], in_=HALF[:, :], compare_op=ALU.not_equal, fill=0.5, base=base,
                                 pattern=[[-1, 128]], channel_multiplier=1).then_inc(s_const, 1)
                po.wait_ge(s_const, 4 + k)
            po.iota(row_no[:, :].rearrange("p (k t) -> p k t", t=TILES), pattern=[[PACK, BLOCKS], [1, TILES]],
                    base=0, channel_multiplier=TILES).then_inc(s_iota, 1)
            po.wait_ge(s_iota, 1)
            po.tensor_copy(slot_rows[:, :, 0].bitcast(I32), row_no[:, :]).then_inc(s_iota, 1)
            po.memset(slot_rows[:, :, 1], 0.0).then_inc(s_iota, 1)
            po.memset(slot_rows[:, :, 3], 0.0).then_inc(s_iota, 1)
            po.wait_ge(s_iota, 4)
            sems.passed[id(po)] = s_passed_pool
            po.wait_ge(s_flag, 2)
            unsorted = po.value_load(flag[0:1, 0:1])
            with po.If(unsorted > 0):
                po.iota(no_i, pattern=[[1, KEYS]], base=0, channel_multiplier=0).then_inc(s_numbered, 1)
                po.iota(own_no, pattern=[[1, PER]], base=0, channel_multiplier=PER).then_inc(s_numbered, 1)
                po.wait_ge(s_ranked, 4)
                with po.Fori(0, BLOCKS) as i:
                    po.dma_start(gat[:, 0, :, :], ea_in.rearrange("(p t) f -> p t f", p=TILE)[:, bass.ds(i * TILES, TILES), :])\
                      .then_inc(s_ea_in, 16)
                    po.tensor_copy(gidx[:, 0, :], rank_i[:, bass.ds(i * TILES, TILES)]).then_inc(s_rank_copy, 1)
                    po.tensor_copy(grow[:, 0, :, :], meta[:, bass.ds(i * TILES, TILES), :]).then_inc(s_rank_copy, 1)
                    sems.wait(po, s_ea_in, i * 16 + 16)
                    sems.wait(po, s_rank_copy, i * 2 + 2)
                    for t in range(TILES):
                        for table, rows in ((EA_S, gat[:, 0, t, :]), (META_S, grow[:, 0, t, :])):
                            po.indirect_dma_start(
                                table, bass.IndirectOffsetOnAxis(ap=gidx[:, 0, t:t + 1], axis=0),
                                rows, None, bounds_check=EDGES + 1, oob_is_err=False).then_inc(s_sorted, 16)
                    sems.wait(po, s_sorted, i * (TILES * 32) + TILES * 32)
            po.end_ifs()
            po.wait_ge(s_idx, 4)

            copies = [0]

            def gather_pass(name, index, source, rows, bound, target, backwards=False):
                base = copies[0]

                def body(i, us):
                    for u in us:
                        n = 2 * i + u
                        k = BLOCKS - 1 - n if backwards else n
                        dst = grow if target is None else gat
                        if not (isinstance(i, int) and i == 0):
                            if target is None:
                                sems.wait(po, s_info, 2 * i + u - 1)
                            else:
                                sems.wait(po, s_gstore[u], store_base(name, u) + i * 16)
                        po.tensor_copy(gidx[:, u, :], index(k)).then_inc(s_gcopy, 1)
                        po.memset(dst[:, u, :, :], 0.0).then_inc(s_gcopy, 1)
                        sems.wait(po, s_gcopy, base + n * 2 + 2)
                        for t in range(TILES):
                            at = t if target is None else 2 * (t % 4) + t // 4
                            po.indirect_dma_start(
                                dst[:, u, at, :], None, source,
                                bass.IndirectOffsetOnAxis(ap=gidx[:, u, t:t + 1], axis=0),
                                bounds_check=bound, oob_is_err=False).then_inc(s_gather[u], 16)
                    for u in us:
                        n = 2 * i + u
                        k = BLOCKS - 1 - n if backwards else n
                        sems.wait(po, s_gather[u], gather_base(name, u) + (i + 1) * (16 * TILES))
                        if target is None:
                            po.tensor_copy(src_info[:, bass.ds(k * TILES, TILES), :], grow[:, u, :, :]).then_inc(s_info, 1)
                        else:
                            po.dma_start(target[k, :, :], gat[:, u, :, :].rearrange("p t f -> p (t f)"))\
                              .then_inc(s_gstore[u], 16)
                in_pairs(po, BLOCKS, body)
                copies[0] += 2 * BLOCKS

            def all_stored(name):
                for u in (0, 1):
                    po.wait_ge(s_gstore[u], store_base(name, u) + per_slot[u] * 16)

            gather_pass("xd", lambda k: idx_dst[:, bass.ds(k * TILES, TILES)], x, D, NODES - 1, XDR)
            all_stored("xd")
            po.wait_ge(s_def, 16)
            base = copies[0]

            def body(i, us):
                for u in us:
                    n = 2 * i + u
                    if not (isinstance(i, int) and i == 0):
                        sems.wait(po, s_scatter[u], i * (16 * TILES))
                    po.tensor_copy(gidx[:, u, :], idx_last[:, bass.ds(n * TILES, TILES)]).then_inc(s_gcopy, 1)
                    po.tensor_copy(grow[:, u, :, :], slot_rows[:, bass.ds(n * TILES, TILES), :]).then_inc(s_gcopy, 1)
                    sems.wait(po, s_gcopy, base + n * 2 + 2)
                    for t in range(TILES):
                        po.indirect_dma_start(
                            SLOTS, bass.IndirectOffsetOnAxis(ap=gidx[:, u, t:t + 1], axis=0),
                            grow[:, u, t, :], None, bounds_check=NODES - 1, oob_is_err=False)\
                          .then_inc(s_scatter[u], 16)
            in_pairs(po, BLOCKS, body)
            copies[0] += 2 * BLOCKS
            for u in (0, 1):
                po.wait_ge(s_scatter[u], per_slot[u] * 16 * TILES)
            gather_pass("info", lambda k: idx_src[:, bass.ds(k * TILES, TILES)], SLOTS, 4, NODES - 1, None)
            gather_pass("xs", lambda k: idx_src[:, bass.ds(k * TILES, TILES)], x, D, NODES - 1, XSR)
            all_stored("xs")
            for t, (P, back) in enumerate(((P_e0, False), (P_e1, True), (P_e4, False), (P_e6, False), (P_e7, False))):
                P.all_done(po)
                gather_pass(f"ov{t}", lambda k: src_info[:, bass.ds(k * TILES, TILES), 0].bitcast(I32),
                            TAB[t], D, EDGES - 1, OV[t], back)
                all_stored(f"ov{t}")
            P_node2.all_done(po)
            base = copies[0]

            def body(i, us):
                for u in us:
                    n = 2 * i + u
                    sems.wait(po, s_scatter[u], (per_slot[u] + i) * (16 * TILES))
                    po.tensor_copy(gidx[:, u, :], idx_last[:, bass.ds(n * TILES, TILES)]).then_inc(s_gcopy, 1)
                    sems.wait(po, s_gcopy, base + n + 1)
                    P_e8.wait(po, "evrow", n)
                    for t in range(TILES):
                        po.indirect_dma_start(
                            out, bass.IndirectOffsetOnAxis(ap=gidx[:, u, t:t + 1], axis=0),
                            rows_out[:, u, t, :], None, bounds_check=NODES - 1, oob_is_err=False)\
                          .then_inc(s_scatter[u], 16)
            in_pairs(po, BLOCKS, body)

        def bk(u, k):
            return bank[4 * u + k][:, 0:COLS]

        @block.tensor
        def _(pe):
            mm = nc.tensor.matmul

            def to_features(dst, rows):
                rows = rows.rearrange("p t f -> p (t f)")
                for j in range(4):
                    last = nc.tensor.transpose(dst[:, TILE * j:TILE * j + TILE], rows[:, 128 * j:128 * j + 128],
                                               ident[0:TILE, 0:TILE])
                return last

            def to_rows(dst, value):
                for j in range(4):
                    last = nc.tensor.transpose(dst[0:TILE, 128 * j:128 * j + 128], value[:, TILE * j:TILE * j + TILE],
                                               ident[:, :])
                return last

            def acc(dst, *pairs):
                for k, (w, v) in enumerate(pairs):
                    last = mm(dst, w, v, start=(k == 0), stop=(k == len(pairs) - 1))
                return last

            def one(dst, w, v):
                return mm(dst, w, v, start=True, stop=True)

            pe.wait_ge(s_const, 6)
            pe.wait_ge(s_w, WEIGHT_DMAS * 16)
            pe.wait_ge(s_dconst, 6)
            one(bank[0][:, 0:64], w2t_sb[:, :], C[0:64, 0:64])
            one(bank[1][:, 0:1], C[:, :], K["b2"]).then_inc(s_pe_small, 1)
            pe.wait_ge(s_setup, 3)
            one(bank[5][0:1, 0:1], viol[:, :], carry_in[:, :]).then_inc(s_flag, 1)
            pe.wait_ge(s_setup, SETUP_SCAN)
            one(bank[2][0:1, 0:NAT], nat[:, 8, 249:250], ident[0:NAT, 0:NAT])
            one(bank[3][0:1, 0:NAT], nat[:, 9, 249:250], ident[0:NAT, 0:NAT]).then_inc(s_pe_small, 1)
            pe.wait_ge(s_setup, SETUP_CARRY)
            one(bank[4][0:NAT, 0:1], tiny[:, 3, :], ident[0:1, 0:1]).then_inc(s_pe_small, 1)
            pe.wait_ge(s_setup, SETUP_ROWS)
            for q, k in enumerate((1, 3, 5, 10)):
                for par in (0, 1):
                    last = one(bank[q][0:TILE, 128 * par:128 * par + NAT], nat[:, k, TILE * par:TILE * par + TILE],
                               ident[0:NAT, 0:NAT])
            last.then_inc(s_tcol, 1)
            pe.wait_ge(s_ccol, 8)

            def node0(P, with_g):
                def body(i, us):
                    for u in us:
                        P.landed(pe, "ld", i, u)
                        if with_g:
                            P.free(pe, "evs", i, u)
                        one(bk(u, 0), M["w1a"], B["in0"][:, u, :])
                        one(bk(u, 1), M["w1b"], B["in0"][:, u, :]).then_inc(P.s("hid"), 1)
                    for u in us:
                        P.free(pe, "out", i, u)
                        P.wait(pe, "relu0", 2 * i + u)
                        P.wait(pe, "relu1", 2 * i + u)
                        acc(bk(u, 2), (C[:, :], B["in0"][:, u, :]), (M["w2ca"], B["a"][:, u, :]),
                            (M["w2cb"], B["b"][:, u, :])).then_inc(P.s("y"), 1)
                        if with_g:
                            acc(bk(u, 0), (M["w2a"], B["a"][:, u, :]), (M["w2b"], B["b"][:, u, :])).then_inc(P.s("g"), 1)
                    for u in us:
                        variance(P, i, u, 3)
                in_pairs(pe, P.chunks, body)
                P.all_done(pe)

            def variance(P, i, u, k, sq="sq", var="var", lnv="lnv", buf="c"):
                P.free(pe, lnv, i, u)
                P.wait(pe, sq, 2 * i + u)
                one(bk(u, k), J[:, :], B[buf][:, u, :]).then_inc(P.s(var), 1)

            def rows_of(P, i, u, k, buf="o0", done="out"):
                P.free(pe, "evrow", i, u)
                P.wait(pe, done, 2 * i + u)
                to_rows(bank[4 * u + k], B[buf][:, u, :]).then_inc(P.s("row"), 1)

            node0(P_node0, False)

            pe.wait_ge(s_info, BLOCKS)
            for q, k in enumerate((1, 2)):
                for par in (0, 1):
                    last = one(bank[q][0:NAT, 128 * par:128 * par + TILE], src_info[:, par::2, k],
                               ident[0:TILE, 0:TILE])
            last.then_inc(s_pe_small, 1)
            pe.wait_ge(s_info, INFO_ROWS)

            def body(i, us):
                for u in us:
                    P_e0.landed(pe, "ld", i, u)
                    P_e0.free(pe, "evrow", i, u)
                    P_e0.free(pe, "out", i, u)
                    to_features(bk(u, 0), rows_in[0][:, u])
                    to_features(bk(u, 1), rows_in[1][:, u]).then_inc(P_e0.s("tr"), 1)
                for u in us:
                    P_e0.wait(pe, "vec", 2 * i + u)
                    one(bk(u, 2), M["w1a"], B["b"][:, u, :])
                    one(bk(u, 3), M["w1b"], B["b"][:, u, :]).then_inc(P_e0.s("hid"), 1)
                for u in us:
                    P_e0.wait(pe, "relu0", 2 * i + u)
                    P_e0.wait(pe, "relu1", 2 * i + u)
                    P_e0.wait(pe, "evd", 2 * i + u)
                    acc(bk(u, 1), (M["w2a"], B["c"][:, u, :]), (M["w2b"], B["d"][:, u, :])).then_inc(P_e0.s("g"), 1)
                for u in us:
                    P_e0.wait(pe, "evs", 2 * i + u)
                    rows_of(P_e0, i, u, 0)
            in_pairs(pe, BLOCKS, body)
            P_e0.all_done(pe)

            node0(P_node0e, True)

            def body(i, us):
                for u in us:
                    P_e1.landed(pe, "ld", i, u)
                    P_e1.free(pe, "msg", i, u)
                    to_features(bk(u, 0), rows_in[0][:, u]).then_inc(P_e1.s("tr"), 1)
                for u in us:
                    P_e1.free(pe, "out", i, u)
                    P_e1.wait(pe, "vec", 2 * i + u)
                    one(bk(u, 1), C[:, :], B["c"][:, u, :]).then_inc(P_e1.s("y"), 1)
                for u in us:
                    variance(P_e1, i, u, 2, buf="d")
                for u in us:
                    rows_of(P_e1, i, u, 3)
            in_pairs(pe, BLOCKS, body)
            P_e1.all_done(pe)

            def body(i, us):
                for u in us:
                    P_e2.landed(pe, "ld", i, u)
                    P_e2.free(pe, "msg", i, u)
                    P_e2.free(pe, "evs", i, u)
                    to_features(bk(u, 0), rows_in[0][:, u])
                    to_features(bk(u, 1), rows_in[1][:, u]).then_inc(P_e2.s("tr"), 1)
                for u in us:
                    n = 2 * i + u
                    P_e2.free(pe, "evf", i, u)
                    P_e2.free(pe, "evc", i, u)
                    P_e2.wait(pe, "evs", n)
                    P_e2.wait(pe, "msg", n)
                    P_e2.wait(pe, "scan", n)
                    for k, part in ((2, "f"), (3, "c")):
                        last = acc(bk(u, k), (M["src" + part], B["o3"][:, u, :]), (M["dst" + part], B["o0"][:, u, :]),
                                   (M["nbr" + part], B["a"][:, u, :]))
                    last.then_inc(P_e2.s("t"), 1)
            in_pairs(pe, BLOCKS, body)
            P_e2.all_done(pe)

            def halves_mean(want, k0, k1):
                pe.wait_ge(s_dv_small, want)
                one(bank[0][:, 0:2 * (k1 - k0)], HALF[:, :], mom[:, k0:k1, :].rearrange("p k c -> p (k c)"))\
                    .then_inc(s_pe_small, 1)

            halves_mean(STATS1, 0, 2)
            P_e3.all_done(pe)
            halves_mean(STATS2, 0, 1)
            pe.wait_ge(s_dv_small, STATS2B)
            one(bank[1][:, 0:1], C[:, :], K["t2"]).then_inc(s_pe_small, 1)

            def plain_ln(P, wait_y, rows=None, first=None):
                def body(i, us):
                    if first:
                        for u in us:
                            first(i, u)
                    for u in us:
                        P.free(pe, "out", i, u)
                        P.wait(pe, "vec", 2 * i + u)
                        one(bk(u, 1), C[:, :], B["c"][:, u, :]).then_inc(P.s("y"), 1)
                    for u in us:
                        variance(P, i, u, 2, buf="d")
                    if rows:
                        for u in us:
                            rows_of(P, i, u, 3)
                    elif rows is None and "bnf" in P.steps:
                        for u in us:
                            P.free(pe, "bnf", i, u)
                            P.wait(pe, "out", 2 * i + u)
                            one(bk(u, 3), M["wl2"], B["o0"][:, u, :]).then_inc(P.s("h"), 1)
                in_pairs(pe, P.chunks, body)
                P.all_done(pe)

            plain_ln(P_e4, 3, rows=True)
            plain_ln(P_node1, 2)
            plain_ln(P_node1e, 2, rows=False)

            def body(i, us):
                for u in us:
                    P_e5.landed(pe, "ld", i, u)
                    P_e5.free(pe, "msg", i, u)
                    to_features(bk(u, 0), rows_in[0][:, u]).then_inc(P_e5.s("tr"), 1)
                for u in us:
                    P_e5.free(pe, "mask", i, u)
                    P_e5.free(pe, "evs", i, u)
                    P_e5.wait(pe, "vec", 2 * i + u)
                    one(bk(u, 1), M["wl2"], B["b"][:, u, :])
                    one(bk(u, 2), M["wl2"], B["in2"][:, u, :]).then_inc(P_e5.s("h"), 1)
            in_pairs(pe, BLOCKS, body)
            P_e5.all_done(pe)
            halves_mean(STATS3, 0, 3)

            plain_ln(P_e6, 1, rows=True)

            def first_h(P):
                def first(i, u):
                    P.landed(pe, "ld", i, u)
                    P.free(pe, "act", i, u)
                    one(bk(u, 0), M["wl2"], B["in0"][:, u, :]).then_inc(P.s("h"), 1)
                return first
            plain_ln(P_e6s, 1, rows=False, first=first_h(P_e6s))

            P = P_node2

            def body(i, us):
                for u in us:
                    P.landed(pe, "ld", i, u)
                    P.free(pe, "evrow", i, u)
                    one(bk(u, 0), M["wl2"], B["in0"][:, u, :]).then_inc(P.s("h"), 1)
                for u in us:
                    P.wait(pe, "vec", 2 * i + u)
                    one(bk(u, 1), C[:, :], B["c"][:, u, :]).then_inc(P.s("y"), 1)
                for u in us:
                    P.free(pe, "lnv2", i, u)
                    variance(P, i, u, 2, buf="d")
                for u in us:
                    P.wait(pe, "out", 2 * i + u)
                    one(bk(u, 0), M["w31"], B["o0"][:, u, :]).then_inc(P.s("hid"), 1)
                for u in us:
                    P.wait(pe, "relu0", 2 * i + u)
                    one(bk(u, 1), M["w32"], B["a"][:, u, :]).then_inc(P.s("g"), 1)
                for u in us:
                    P.free(pe, "out2", i, u)
                    P.wait(pe, "add", 2 * i + u)
                    one(bk(u, 3), C[:, :], B["f"][:, u, :]).then_inc(P.s("y2"), 1)
                for u in us:
                    variance(P, i, u, 2, "sq2", "var2", "lnv2", "g")
                for u in us:
                    rows_of(P, i, u, 0, "o1", "out2")
            in_pairs(pe, P.chunks, body)
            P.all_done(pe)

            P = P_e7

            def body(i, us):
                for u in us:
                    n = 2 * i + u
                    P.landed(pe, "ld", i, u)
                    P.free(pe, "out", i, u)
                    to_features(bk(u, 0), rows_in[0][:, u]).then_inc(P.s("tr"), 1)
                for u in us:
                    n = 2 * i + u
                    P.free(pe, "evrow", i, u)
                    P.wait(pe, "msg", n, 1 + 1)
                    one(bk(u, 1), M["w31"], B["a"][:, u, :])
                    one(bk(u, 2), M["w31"], B["in1"][:, u, :]).then_inc(P.s("hid"), 1)
                for u in us:
                    n = 2 * i + u
                    P.free(pe, "act", i, u)
                    P.wait(pe, "relu0", n)
                    one(bk(u, 3), M["w32"], B["d"][:, u, :]).then_inc(P.s("g"), 1)
                for u in us:
                    n = 2 * i + u
                    P.wait(pe, "relu1", n)
                    one(bk(u, 0), M["w32"], B["h"][:, u, :]).then_inc(P.s("h"), 1)
                for u in us:
                    rows_of(P, i, u, 2)
            in_pairs(pe, BLOCKS, body)
            P.all_done(pe)

            P = P_e8

            def body(i, us):
                for u in us:
                    P.landed(pe, "ld", i, u)
                    P.free(pe, "msg", i, u)
                    to_features(bk(u, 0), rows_in[0][:, u]).then_inc(P.s("tr"), 1)
                for u in us:
                    P.free(pe, "out", i, u)
                    P.wait(pe, "add", 2 * i + u)
                    one(bk(u, 1), C[:, :], B["f"][:, u, :]).then_inc(P.s("y"), 1)
                for u in us:
                    variance(P, i, u, 2, buf="d")
                for u in us:
                    rows_of(P, i, u, 3)
            in_pairs(pe, BLOCKS, body)

        @block.scalar
        def _(ac):
            act = nc.scalar.activation

            def square(P, i, u, k, bias, buf="c", y="y", sq="sq", var="var"):
                P.free(ac, var, i, u)
                P.wait(ac, y, 2 * i + u)
                act(B[buf][:, u, :], bk(u, k), ACT.Square, bias=bias).then_inc(P.s(sq), 1)

            def rstd(P, i, u, k, buf="g", var="var", lnv="lnv", name="rstd", read="out"):
                P.free(ac, read, i, u)
                P.wait(ac, var, 2 * i + u)
                act(B[buf][:, u, :], bk(u, k), ACT.Ln, bias=K["eps"]).then_inc(P.s(lnv), 1)
                P.wait(ac, lnv, 2 * i + u)
                act(B[buf][:, u, :], B[buf][:, u, :], ACT.Exp, scale=-0.5).then_inc(P.s(name), 1)

            def small_rstd(want, col):
                ac.wait_ge(s_dv_small, want)
                act(col, col, ACT.Ln, bias=K["eps"]).then_inc(s_ac_small, 1)
                small[0] += 2
                ac.wait_ge(s_ac_small, small[0] - 1)
                act(col, col, ACT.Exp, scale=-0.5).then_inc(s_ac_small, 1)

            small = [0]

            def rows_evac(P, i, u, k, stored=True):
                if stored:
                    P.stored(ac, "st", i, u)
                P.wait(ac, "row", 2 * i + u)
                act(rows_out[:, u, :, :].rearrange("p (h j) f -> p j h f", h=2),
                    bank[4 * u + k][0:TILE, :].rearrange("p (j h f) -> p j h f", j=4, h=2), ACT.Copy)\
                    .then_inc(P.s("evrow"), 1)

            def sigmoid_log(P, i, u, out, z):
                n = 2 * i + u
                P.free(ac, "sig", i, u)
                P.wait(ac, "nabs", n)
                act(out, z, ACT.Exp).then_inc(P.s("lsig"), 1)
                P.wait(ac, "lsig", n, 1)
                act(out, out, ACT.Ln, bias=1.0).then_inc(P.s("lsig"), 1)

            def sigmoid_end(P, i, u, out, arg, used):
                P.free(ac, used, i, u)
                P.wait(ac, "arg", 2 * i + u)
                act(out, arg, ACT.Exp).then_inc(P.s("sig"), 1)

            def node0(P, with_g):
                def body(i, us):
                    for u in us:
                        P.free(ac, "y", i, u)
                        if with_g:
                            P.free(ac, "g", i, u)
                        P.wait(ac, "hid", 2 * i + u)
                        act(B["a"][:, u, :], bk(u, 0), ACT.Relu, bias=K["b1"]).then_inc(P.s("relu0"), 1)
                    for u in us:
                        square(P, i, u, 2, K["cb2"])
                    for u in us:
                        rstd(P, i, u, 3)
                    if with_g:
                        for u in us:
                            P.stored(ac, "st", i, u)
                            P.wait(ac, "g", 2 * i + u)
                            act(B["o1"][:, u, :], bk(u, 0), ACT.Copy).then_inc(P.s("evs"), 1)
                in_pairs(ac, P.chunks, body)
                P.all_done(ac)

            ac.preload_act_table_set("natural_log_exp_and_others")
            ac.wait_ge(s_setup, SETUP_CARRY + 2)
            act(nat[:, 10, :], nat[:, 7, :], ACT.Ln, bias=1.0).then_inc(s_setup, 1)
            ac.wait_ge(s_setup, SETUP_CARRY + 3)
            act(nat[:, 10, :], nat[:, 10, :], ACT.Exp, scale=-0.5).then_inc(s_setup, 1)
            ac.wait_ge(s_dconst, CONST_END)
            node0(P_node0, False)

            def body(i, us):
                for u in us:
                    P_e0.stored(ac, "st", i, u)
                    P_e0.wait(ac, "tr", 2 * i + u)
                    act(B["o1"][:, u, :], bk(u, 0), ACT.Copy).then_inc(P_e0.s("evs"), 1)
                for u in us:
                    P_e0.free(ac, "g", i, u)
                    P_e0.wait(ac, "hid", 2 * i + u)
                    act(B["c"][:, u, :], bk(u, 2), ACT.Relu, bias=K["b1"]).then_inc(P_e0.s("relu0"), 1)
                for u in us:
                    rows_evac(P_e0, i, u, 0)
            in_pairs(ac, BLOCKS, body)
            P_e0.all_done(ac)

            node0(P_node0e, True)

            def body(i, us):
                for u in us:
                    square(P_e1, i, u, 1, K["cb2"], "d")
                for u in us:
                    rstd(P_e1, i, u, 2)
                for u in us:
                    rows_evac(P_e1, i, u, 3)
            in_pairs(ac, BLOCKS, body)
            P_e1.all_done(ac)

            def body(i, us):
                for u in us:
                    P_e2.free(ac, "t", i, u)
                    P_e2.wait(ac, "tr", 2 * i + u)
                    act(B["a"][:, u, :], bk(u, 1), ACT.Copy).then_inc(P_e2.s("evs"), 1)
                for u in us:
                    P_e2.stored(ac, "st", i, u)
                    P_e2.wait(ac, "t", 2 * i + u)
                    act(B["o1"][:, u, :], bk(u, 2), ACT.Identity, bias=K["bf"]).then_inc(P_e2.s("evf"), 1)
                    act(B["o2"][:, u, :], bk(u, 3), ACT.Identity, bias=K["bc"]).then_inc(P_e2.s("evc"), 1)
            in_pairs(ac, BLOCKS, body)
            P_e2.all_done(ac)
            small_rstd(STATS1 + 3, K["tmp1"])
            small_rstd(STATS1 + 8, K["tmp1"])
            ac.wait_ge(s_dv_small, STATS1B)

            def body(i, us):
                for u in us:
                    n = 2 * i + u
                    P_e3.landed(ac, "ld", i, u)
                    P_e3.free(ac, "vec", i, u)
                    act(B["b"][:, u, :], B["in1"][:, u, :], ACT.Abs, scale=K["s1c"], bias=K["t1c"]).then_inc(P_e3.s("act"), 1)
                    P_e3.wait(ac, "act", n, 1)
                    act(B["c"][:, u, :], B["b"][:, u, :], ACT.Exp, scale=-1.0).then_inc(P_e3.s("act"), 1)
                    P_e3.wait(ac, "act", n, 2)
                    act(B["d"][:, u, :], B["c"][:, u, :], ACT.Ln, bias=1.0).then_inc(P_e3.s("act"), 1)
                    sigmoid_log(P_e3, i, u, B["a"][:, u, :], B["g2"][:, u, :])
                for u in us:
                    sigmoid_end(P_e3, i, u, B["in4"][:, u, :], B["in3"][:, u, :], "vec")
            in_pairs(ac, BLOCKS, body)
            P_e3.all_done(ac)
            small_rstd(STATS2 + 3, K["tmp1"])
            ac.wait_ge(s_dv_small, STATS2C)

            def soft(P, source, ready, rows=None):
                def body(i, us):
                    for u in us:
                        n = 2 * i + u
                        ready(i, u)
                        P.free(ac, "vec", i, u)
                        act(B["a"][:, u, :], B[source][:, u, :], ACT.Abs, bias=K["t2"]).then_inc(P.s("act"), 1)
                        P.wait(ac, "act", n, 1)
                        act(B["b"][:, u, :], B["a"][:, u, :], ACT.Exp, scale=-1.0).then_inc(P.s("act"), 1)
                        P.wait(ac, "act", n, 2)
                        act(B["e"][:, u, :], B["b"][:, u, :], ACT.Ln, bias=1.0).then_inc(P.s("act"), 1)
                    for u in us:
                        square(P, i, u, 1, K["ct2"], "d")
                    for u in us:
                        rstd(P, i, u, 2)
                    if rows:
                        for u in us:
                            rows_evac(P, i, u, 3)
                in_pairs(ac, P.chunks, body)
                P.all_done(ac)
            soft(P_e4, "f", lambda i, u: P_e4.wait(ac, "msg", 2 * i + u), True)
            soft(P_node1, "in0", lambda i, u: P_node1.landed(ac, "ld", i, u))
            soft(P_node1e, "in0", lambda i, u: P_node1e.landed(ac, "ld", i, u))

            def body(i, us):
                for u in us:
                    P_e5.stored(ac, "st", i, u)
                    P_e5.wait(ac, "h", 2 * i + u)
                    act(B["o1"][:, u, :], bk(u, 1), ACT.Copy).then_inc(P_e5.s("evs"), 1)
            in_pairs(ac, BLOCKS, body)
            P_e5.all_done(ac)
            small_rstd(STATS3 + 5, K["tmp1"])
            ac.wait_ge(s_dv_small, STATS3B)

            def relu_bn(P, source, ready, rows=None):
                def body(i, us):
                    for u in us:
                        ready(i, u)
                        P.free(ac, "vec", i, u)
                        act(B["a"][:, u, :], source(u), ACT.Relu, scale=K["s3"], bias=K["t3"]).then_inc(P.s("act"), 1)
                    for u in us:
                        square(P, i, u, 1, 0.0, "d")
                    for u in us:
                        rstd(P, i, u, 2)
                    if rows:
                        for u in us:
                            rows_evac(P, i, u, 3)
                in_pairs(ac, P.chunks, body)
                P.all_done(ac)
            relu_bn(P_e6, lambda u: B["in0"][:, u, :], lambda i, u: P_e6.landed(ac, "ld", i, u), True)
            relu_bn(P_e6s, lambda u: bk(u, 0), lambda i, u: P_e6s.wait(ac, "h", 2 * i + u))

            P = P_node2

            def body(i, us):
                for u in us:
                    P.wait(ac, "h", 2 * i + u)
                    P.free(ac, "vec", i, u)
                    act(B["b"][:, u, :], bk(u, 0), ACT.Relu, scale=K["s3"], bias=K["t3"]).then_inc(P.s("act"), 1)
                for u in us:
                    square(P, i, u, 1, 0.0, "d")
                for u in us:
                    rstd(P, i, u, 2, "h")
                for u in us:
                    sigmoid_log(P, i, u, B["e"][:, u, :], B["in1"][:, u, :])
                for u in us:
                    sigmoid_end(P, i, u, B["in4"][:, u, :], B["in3"][:, u, :], "add")
                for u in us:
                    square(P, i, u, 3, 0.0, "g", "y2", "sq2", "var2")
                for u in us:
                    rstd(P, i, u, 2, "dinv", "var2", "lnv2", "rstd2", "out2")
                for u in us:
                    rows_evac(P, i, u, 0)
            in_pairs(ac, P.chunks, body)
            P.all_done(ac)

            P = P_e7

            def body(i, us):
                for u in us:
                    n = 2 * i + u
                    P.wait(ac, "hid", n)
                    P.free(ac, "vec", i, u)
                    act(B["b"][:, u, :], bk(u, 1), ACT.Identity, bias=K["b31"]).then_inc(P.s("evs"), 1)
                    act(B["c"][:, u, :], bk(u, 2), ACT.Identity, bias=K["b31"]).then_inc(P.s("evd"), 1)
                    P.free(ac, "g", i, u)
                    P.wait(ac, "evs", n)
                    act(B["d"][:, u, :], B["b"][:, u, :], ACT.Relu).then_inc(P.s("relu0"), 1)
                for u in us:
                    P.stored(ac, "st", i, u)
                    P.wait(ac, "g", 2 * i + u)
                    act(B["o1"][:, u, :], bk(u, 3), ACT.Identity, bias=K["b32"]).then_inc(P.s("act"), 1)
                for u in us:
                    rows_evac(P, i, u, 2)
            in_pairs(ac, BLOCKS, body)
            P.all_done(ac)

            P = P_e8

            def body(i, us):
                for u in us:
                    sigmoid_log(P, i, u, B["e"][:, u, :], B["o1"][:, u, :])
                for u in us:
                    sigmoid_end(P, i, u, B["in4"][:, u, :], B["in3"][:, u, :], "add")
                for u in us:
                    square(P, i, u, 1, 0.0, "d")
                for u in us:
                    rstd(P, i, u, 2, "g2")
                for u in us:
                    ac.wait_ge(s_scatter[u], (per_slot[u] + i) * (16 * TILES))
                    rows_evac(P, i, u, 3, stored=False)
            in_pairs(ac, BLOCKS, body)

        @block.vector
        def _(dv):
            v = nc.vector
            marks = {}
            count = [0]

            def const(ins):
                ins.then_inc(s_dconst, 1)
                count[0] += 1
                dv.wait_ge(s_dconst, count[0])

            const(v.memset(mats[:, :, :], 0.0))
            const(v.memset(J[:, :], 0.0))
            v.memset(J[0:64, 0:64], 1.0 / D)
            v.memset(default[:, :, 0].bitcast(I32), SKIP)
            v.memset(default[:, :, 3], 0.0)
            const(v.memset(J[64:128, 64:128], 1.0 / D))
            v.memset(pad[:, :], -1.0)
            v.memset(carry_in[:, :], 1.0)
            const(v.memset(default[:, :, 1:3], 1.0))
            dv.wait_ge(s_const, 6)
            const(v.tensor_tensor(C[:, :], ident[:, :], J[:, :], ALU.subtract))
            v.memset(K["eps"], EPS)
            const(v.memset(carry[:, :], 0.0))
            dv.wait_ge(s_pe_small, 1)
            v.tensor_copy(M["w2ca"][:, 0:64], bank[0][:, 0:64])
            v.tensor_copy(M["w2cb"][:, 64:128], bank[0][:, 0:64])
            const(v.tensor_copy(K["cb2"], bank[1][:, 0:1]))
            assert count[0] == CONST_END

            def sort_edges():
                done = [0]

                def by_own(ins):
                    ins.then_inc(s_rank, 1)
                    done[0] += 1
                    dv.wait_ge(s_rank, done[0])

                dv.wait_ge(s_own, 48)
                dv.wait_ge(s_numbered, 2)
                by_own(v.tensor_copy(own_f[:, 0:2, :], own_i))
                by_own(v.tensor_copy(idx_f[:, :], own_no))
                v.memset(meta[:, :, 3], 0.0)
                by_own(v.memset(rank[:, :], 1.0))
                by_own(v.tensor_copy(no_f, no_i))
                for c in range(EDGES // KEYS):
                    dv.wait_ge(s_keys, 16 * c + 16)
                    by_own(v.tensor_copy(key_f, key_i))
                    dv.sem_inc(s_keys_used, 1)
                    base = done[0]
                    with dv.Fori(0, PER) as t:
                        def looped(k, ins):
                            ins.then_inc(s_rank, 1)
                            dv.wait_ge(s_rank, t * 6 + (base + k))
                        looped(1, v.tensor_copy(key_col[:, :], own_f[:, 0, bass.ds(t, 1)]))
                        looped(2, v.tensor_copy(edge_col[:, :], idx_f[:, bass.ds(t, 1)]))
                        looped(3, v.tensor_scalar(work, no_f, edge_col[:, 0:1], None, ALU.is_lt))
                        looped(4, v.scalar_tensor_tensor(out=work, in0=key_f, scalar=key_col[:, 0:1], in1=work,
                                                         op0=ALU.is_equal, op1=ALU.mult))
                        looped(5, v.scalar_tensor_tensor(out=work, in0=key_f, scalar=key_col[:, 0:1], in1=work,
                                                         op0=ALU.is_lt, op1=ALU.add))
                        looped(6, v.reduce_sum(part[:, bass.ds(t, 1)], work, mybir.AxisListType.X))
                    done[0] += PER * 6
                    by_own(v.tensor_tensor(rank[:, :], rank[:, :], part[:, :], ALU.add))
                    by_own(v.tensor_scalar(idx_f[:, :], idx_f[:, :], -float(KEYS), None, ALU.add))
                    by_own(v.memset(part[:, :], 0.0))
                assert done[0] == SORT_RANKED, done
                v.tensor_copy(rank_i[:, :], rank[:, :]).then_inc(s_ranked, 1)
                for k in range(3):
                    v.tensor_copy(meta[:, :, k], own_f[:, k, :]).then_inc(s_ranked, 1)
                dv.wait_ge(s_ranked, 4)
                dv.wait_ge(s_meta, 48)
                for k in range(3):
                    by_own(v.tensor_copy(nat[:, k, :], meta_in[:, k, 0::4]))
                by_own(v.tensor_copy(nat[:, 3, :], meta_in[:, 1, 1::4]))
                by_own(v.tensor_copy(nat[:, 11, :], meta_in[:, 1, 2::4]))

            steps = [0]

            def step(ins):
                ins.then_inc(s_setup, 1)
                steps[0] += 1
                dv.wait_ge(s_setup, steps[0])

            dv.wait_ge(s_nat, 5 * 16)
            step(v.tensor_copy(nat[:, 0:4, :], nat_i[:, :, :]))
            step(v.tensor_tensor(nat[:, 4, :], nat[:, 1, :], nat[:, 2, :], ALU.is_gt))
            step(v.reduce_sum(viol[:, :], nat[:, 4, :], mybir.AxisListType.X))
            dv.wait_ge(s_flag, 1)
            v.tensor_scalar(flag[:, :], bank[5][0:1, 0:1], 1.0, None, ALU.subtract).then_inc(s_flag, 1)
            dv.wait_ge(s_flag, 2)
            unsorted = dv.value_load(flag[0:1, 0:1])
            with dv.If(unsorted > 0):
                sort_edges()
            dv.end_ifs()
            dv.wait_ge(s_setup, 3)
            step(v.tensor_tensor(nat[:, 4, :], nat[:, 1, :], nat[:, 0, :], ALU.is_equal))
            step(v.tensor_tensor(nat[:, 5, :], nat[:, 1, :], nat[:, 2, :], ALU.not_equal))
            step(v.tensor_tensor(nat[:, 6, :], nat[:, 1, :], nat[:, 2, :], ALU.is_equal))
            step(v.memset(nat[:, 7, :], 1.0))
            step(v.tensor_tensor_scan(out=nat[:, 8, :], data0=nat[:, 4, :], data1=nat[:, 7, :], initial=0.0,
                                      op0=ALU.mult, op1=ALU.add))
            step(v.memset(nat[:, 7, :], 0.0))
            step(v.tensor_tensor_scan(out=nat[:, 9, :], data0=nat[:, 4, :], data1=nat[:, 7, :], initial=1.0,
                                      op0=ALU.mult, op1=ALU.add))
            assert steps[0] == SETUP_SCAN
            dv.wait_ge(s_pe_small, 2)
            step(v.tensor_copy(tiny[:, 0, :], bank[2][0:1, 0:NAT]))
            step(v.tensor_copy(tiny[:, 1, :], bank[3][0:1, 0:NAT]))
            step(v.tensor_tensor_scan(out=tiny[:, 2, :], data0=tiny[:, 1, :], data1=tiny[:, 0, :], initial=0.0,
                                      op0=ALU.mult, op1=ALU.add))
            step(v.memset(tiny[:, 3, 0:1], 0.0))
            step(v.tensor_copy(tiny[:, 3, 1:NAT], tiny[:, 2, 0:NAT - 1]))
            assert steps[0] == SETUP_CARRY
            dv.wait_ge(s_pe_small, 3)
            step(v.tensor_copy(carry_in[:, :], bank[4][0:NAT, 0:1]))
            step(v.scalar_tensor_tensor(out=nat[:, 7, :], in0=nat[:, 9, :], scalar=carry_in[:, 0:1],
                                        in1=nat[:, 8, :], op0=ALU.mult, op1=ALU.add))
            steps[0] += 2
            dv.wait_ge(s_setup, steps[0])
            step(v.tensor_tensor(nat[:, 0, :], nat[:, 10, :], nat[:, 10, :], ALU.mult))
            step(v.scalar_tensor_tensor(out=nat[:, 0, :], in0=nat[:, 7, :], scalar=1.0, in1=nat[:, 0, :],
                                        op0=ALU.add, op1=ALU.mult))
            step(v.tensor_scalar(nat[:, 0, :], nat[:, 0, :], -0.5, 1.5, ALU.mult, ALU.add))
            step(v.tensor_tensor(nat[:, 10, :], nat[:, 10, :], nat[:, 0, :], ALU.mult))
            assert steps[0] == SETUP_ROWS
            dv.wait_ge(s_tcol, 1)
            ccol = [0]

            def cstep(ins, wait=False):
                ins.then_inc(s_ccol, 1)
                ccol[0] += 1
                if wait:
                    dv.wait_ge(s_ccol, ccol[0])

            for q in range(4):
                for par in (0, 1):
                    cstep(v.tensor_copy(col[:, q, par::2], bank[q][0:TILE, 128 * par:128 * par + NAT]))
            dv.wait_ge(s_ccol, 8)
            v.tensor_copy(idx_dst[:, :], col[:, 0, :]).then_inc(s_idx, 1)
            v.tensor_copy(idx_src[:, :], col[:, 1, :]).then_inc(s_idx, 1)
            v.tensor_copy(slot_rows[:, :, 2], col[:, 3, :]).then_inc(s_idx, 1)
            cstep(v.tensor_scalar(idx_f[:, :], col[:, 2, :], -float(SKIP), float(SKIP), ALU.mult, ALU.add), True)
            cstep(v.tensor_tensor(idx_f[:, :], idx_f[:, :], col[:, 0, :], ALU.add), True)
            v.tensor_copy(idx_last[:, :], idx_f[:, :]).then_inc(s_idx, 1)

            def own(P, step, n, ins, part=None):
                ins.then_inc(P.s(step), 1)
                P.wait(dv, step, n, part)

            def normed(P, i, u, ky, bias, out="o0", stored=True, rs="g"):
                P.wait(dv, "rstd", 2 * i + u)
                if stored:
                    P.stored(dv, "st", i, u)
                if bias is None:
                    ins = v.tensor_tensor(B[out][:, u, :], bk(u, ky), B[rs][:, u, :], ALU.mult)
                else:
                    ins = v.scalar_tensor_tensor(out=B[out][:, u, :], in0=bk(u, ky), scalar=bias,
                                                 in1=B[rs][:, u, :], op0=ALU.add, op1=ALU.mult)
                ins.then_inc(P.s("out"), 1)

            def neg_abs(P, i, u, out, z):
                P.free(dv, "lsig", i, u)
                v.scalar_tensor_tensor(out=out, in0=z, scalar=-1.0, in1=z, op0=ALU.mult, op1=ALU.min)\
                 .then_inc(P.s("nabs"), 1)

            def sigmoid_arg(P, i, u, out, z, log):
                P.free(dv, "sig", i, u)
                P.wait(dv, "lsig", 2 * i + u)
                v.scalar_tensor_tensor(out=out, in0=z, scalar=0.0, in1=log, op0=ALU.min, op1=ALU.subtract)\
                 .then_inc(P.s("arg"), 1)

            def relu_hidden(P, i, u, k, buf):
                v.tensor_scalar(B[buf][:, u, :], bk(u, k), K["b1"], 0.0, ALU.add, ALU.max).then_inc(P.s("relu1"), 1)

            def node0(P, with_g):
                def body(i, us):
                    for u in us:
                        P.free(dv, "y", i, u)
                        if with_g:
                            P.free(dv, "g", i, u)
                        P.wait(dv, "hid", 2 * i + u)
                        relu_hidden(P, i, u, 1, "b")
                    for u in us:
                        normed(P, i, u, 2, K["cb2"])
                in_pairs(dv, P.chunks, body)
                P.all_done(dv)

            node0(P_node0, False)

            dv.wait_ge(s_info, BLOCKS)
            dv.wait_ge(s_pe_small, 4)
            dv.wait_ge(s_rows, 4 * 16)
            for q in (0, 1):
                for par in (0, 1):
                    v.tensor_copy(nat[:, q, TILE * par:TILE * par + TILE],
                                  bank[q][0:NAT, 128 * par:128 * par + TILE]).then_inc(s_info, 1)
            dv.wait_ge(s_info, BLOCKS + 4)
            v.tensor_tensor(nat[:, 2, :], nat[:, 1, :], nat[:, 11, :], ALU.mult).then_inc(s_info, 1)

            def scan(P, n, u, out, same, msg):
                def part(k, ins):
                    own(P, "scan", n, ins, k)
                for h in (0, 1):
                    lo, hi = slice(64 * h, 64 * h + 64), slice(64 - 64 * h, 128 - 64 * h)
                    part(2 * h + 1, v.tensor_tensor_scan(out=out[lo, u, :], data0=same[lo, u, :], data1=msg[lo, u, :],
                                                         initial=carry[lo, 0:1], op0=ALU.mult, op1=ALU.add))
                    part(2 * h + 2, v.tensor_copy(carry[hi, 0:1], out[lo, u, COLS - 1:COLS]))

            def tt(out, a, b, op):
                return v.tensor_tensor(out, a, b, op)

            def body(i, us):
                for u in us:
                    n = 2 * i + u
                    P_e0.landed(dv, "ld", i, u)
                    P_e0.stored(dv, "st", i, u)
                    P_e0.wait(dv, "tr", n)
                    own(P_e0, "evd", n, v.tensor_copy(B["o2"][:, u, :], bk(u, 1)))
                    P_e0.wait(dv, "evs", n)
                    own(P_e0, "msg", n, tt(B["a"][:, u, :], B["o1"][:, u, :], B["wts"][:, u, :], ALU.mult))
                    scan(P_e0, n, u, B["e"], B["same"], B["a"])
                    own(P_e0, "vec", n, tt(B["f"][:, u, :], B["o2"][:, u, :], B["dinv"][:, u, :], ALU.mult), 1)
                    own(P_e0, "vec", n, tt(B["g"][:, u, :], B["f"][:, u, :], B["e"][:, u, :], ALU.add), 2)
                    P_e0.free(dv, "hid", i, u)
                    tt(B["b"][:, u, :], B["g"][:, u, :], B["dinv"][:, u, :], ALU.mult).then_inc(P_e0.s("vec"), 1)
                for u in us:
                    P_e0.free(dv, "g", i, u)
                    P_e0.wait(dv, "hid", 2 * i + u)
                    relu_hidden(P_e0, i, u, 3, "d")
                for u in us:
                    P_e0.wait(dv, "g", 2 * i + u)
                    tt(B["o0"][:, u, :], bk(u, 1), B["dinv"][:, u, :], ALU.mult).then_inc(P_e0.s("out"), 1)
            in_pairs(dv, BLOCKS, body)
            P_e0.all_done(dv)

            def clear_carry(k):
                v.memset(carry[:, :], 0.0).then_inc(s_dconst, 1)
                dv.wait_ge(s_dconst, CONST_END + k)
            node0(P_node0e, True)
            clear_carry(1)

            def overlay(P, i, u, out):
                n = 2 * i + u
                P.landed(dv, "ld", i, u)
                own(P, "msg", n, tt(B["h"][:, u, :], B["in0"][:, u, :], B["keep"][:, u, :], ALU.mult), 1)
                P.wait(dv, "tr", n)
                own(P, "msg", n, tt(out[:, u, :], B["h"][:, u, :], bk(u, 0), ALU.add), 2)

            def body(i, us):
                for u in us:
                    n = 2 * i + u
                    overlay(P_e1, i, u, B["a"])
                    scan(P_e1, n, u, B["e"], B["same"], B["a"])
                    own(P_e1, "vec", n, tt(B["f"][:, u, :], B["e"][:, u, :], B["in2"][:, u, :], ALU.add), 1)
                    own(P_e1, "vec", n, tt(B["b"][:, u, :], B["f"][:, u, :], B["dinv"][:, u, :], ALU.mult), 2)
                    P_e1.free(dv, "y", i, u)
                    tt(B["c"][:, u, :], B["b"][:, u, :], B["in1"][:, u, :], ALU.add).then_inc(P_e1.s("vec"), 1)
                for u in us:
                    normed(P_e1, i, u, 1, K["cb2"])
            in_pairs(dv, BLOCKS, body)
            P_e1.all_done(dv)
            clear_carry(2)

            def body(i, us):
                P = P_e2
                for u in us:
                    n = 2 * i + u
                    P.stored(dv, "st", i, u)
                    P.free(dv, "t", i, u)
                    overlay(P, i, u, B["o3"])
                    own(P, "vec", n, v.scalar_tensor_tensor(out=B["b"][:, u, :], in0=B["more"][:, u, :], scalar=0.0,
                                                            in1=B["in1"][:, u, :], op0=ALU.is_equal, op1=ALU.mult))
                    for q, h in enumerate((1, 0)):
                        lo, hi = slice(64 * h, 64 * h + 64), slice(64 - 64 * h, 128 - 64 * h)
                        own(P, "scan", n, v.tensor_tensor_scan(
                            out=B["o0"][lo, u, ::-1], data0=B["more"][lo, u, ::-1], data1=B["b"][lo, u, ::-1],
                            initial=carry[lo, 0:1], op0=ALU.mult, op1=ALU.add), 2 * q + 1)
                        own(P, "scan", n, v.tensor_copy(carry[hi, 0:1], B["o0"][lo, u, 0:1]), 2 * q + 2)
                for u in us:
                    n = 2 * i + u
                    P.wait(dv, "evf", n)
                    v.bn_stats(stats["f"][:, bass.ds(n, 1), :], B["o1"][:, u, :]).then_inc(P.s("bnf"), 1)
                    P.wait(dv, "evc", n)
                    v.bn_stats(stats["c"][:, bass.ds(n, 1), :], B["o2"][:, u, :]).then_inc(P.s("bnc"), 1)
            in_pairs(dv, BLOCKS, body)
            P_e2.all_done(dv)

            small = [0]

            def sm(ins):
                ins.then_inc(s_dv_small, 1)
                small[0] += 1
                dv.wait_ge(s_dv_small, small[0])

            def moments(names):
                for k, name in enumerate(names):
                    sm(v.bn_aggr(mv[:, k, :], stats[name][:, :, :]))
                    sm(v.tensor_copy(mom[:, k, 0:1], mv[:, k, 0:1]))
                    sm(v.scalar_tensor_tensor(out=mom[:, k, 1:2], in0=mv[:, k, 0:1], scalar=mv[:, k, 0:1],
                                              in1=mv[:, k, 1:2], op0=ALU.mult, op1=ALU.add))

            roots = [0]

            def affine(mean, square, gain, shift, s, t):
                sm(v.tensor_tensor(K["tmp0"], mean, mean, ALU.mult))
                sm(v.tensor_tensor(K["tmp1"], square, K["tmp0"], ALU.subtract))
                roots[0] += 2
                dv.wait_ge(s_ac_small, roots[0])
                sm(v.tensor_tensor(s, gain, K["tmp1"], ALU.mult))
                sm(v.tensor_tensor(K["tmp0"], mean, s, ALU.mult))
                sm(v.tensor_tensor(t, shift, K["tmp0"], ALU.subtract))

            moments(("f", "c"))
            assert small[0] == STATS1
            dv.wait_ge(s_pe_small, 5)
            sm(v.tensor_copy(hold[:, 0:4], bank[0][:, 0:4]))
            affine(hold[:, 0:1], hold[:, 1:2], K["g1f"], K["be1f"], K["s1f"], K["t1f"])
            affine(hold[:, 2:3], hold[:, 3:4], K["g1c"], K["be1c"], K["s1c"], K["t1c"])
            assert small[0] == STATS1B, small
            clear_carry(3)

            def body(i, us):
                P = P_e3
                for u in us:
                    n = 2 * i + u
                    P.landed(dv, "ld", i, u)
                    own(P, "msg", n, v.tensor_scalar(B["e"][:, u, :], B["in1"][:, u, :], K["s1c"], K["t1c"],
                                                     ALU.mult, ALU.add), 1)
                    own(P, "msg", n, v.tensor_scalar(B["f"][:, u, :], B["in0"][:, u, :], K["s1f"], K["t1f"],
                                                     ALU.mult, ALU.add), 2)
                    neg_abs(P, i, u, B["g2"][:, u, :], B["f"][:, u, :])
                for u in us:
                    sigmoid_arg(P, i, u, B["in3"][:, u, :], B["f"][:, u, :], B["a"][:, u, :])
                for u in us:
                    P.wait(dv, "sig", 2 * i + u)
                    n = 2 * i + u
                    P.wait(dv, "act", n)
                    own(P, "vec", n, v.scalar_tensor_tensor(out=B["g"][:, u, :], in0=B["e"][:, u, :], scalar=0.0,
                                                            in1=B["d"][:, u, :], op0=ALU.max, op1=ALU.add), 1)
                    own(P, "vec", n, tt(B["h"][:, u, :], B["g"][:, u, :], B["in4"][:, u, :], ALU.mult), 2)
                    scan(P, n, u, B["o1"], B["same"], B["h"])
                    P.stored(dv, "st", i, u)
                    own(P, "out", n, v.scalar_tensor_tensor(out=B["o0"][:, u, :], in0=B["more"][:, u, :], scalar=0.0,
                                                            in1=B["o1"][:, u, :], op0=ALU.is_equal, op1=ALU.mult))
                    v.bn_stats(stats["u"][:, bass.ds(n, 1), :], B["o0"][:, u, :]).then_inc(P.s("bnf"), 1)
            in_pairs(dv, BLOCKS, body)
            P_e3.all_done(dv)

            moments(("u",))
            assert small[0] == STATS2, small
            dv.wait_ge(s_pe_small, 6)
            sm(v.tensor_scalar(hold[:, 0:2], bank[0][:, 0:2], float(EDGES) / NODES, None, ALU.mult))
            affine(hold[:, 0:1], hold[:, 1:2], K["g2"], K["be2"], K["s2"], K["t2"])
            sm(v.tensor_scalar(K["nt2"], K["t2"], -1.0, None, ALU.mult))
            assert small[0] == STATS2B, small
            dv.wait_ge(s_pe_small, 7)
            sm(v.tensor_copy(K["ct2"], bank[1][:, 0:1]))
            assert small[0] == STATS2C

            def body(i, us):
                P = P_e4
                for u in us:
                    P.landed(dv, "ld", i, u)
                    P.free(dv, "act", i, u)
                    v.scalar_tensor_tensor(out=B["f"][:, u, :], in0=B["in1"][:, u, :], scalar=K["s2"],
                                           in1=B["in0"][:, u, :], op0=ALU.mult, op1=ALU.add).then_inc(P.s("msg"), 1)
                for u in us:
                    n = 2 * i + u
                    P.wait(dv, "act", n)
                    own(P, "vec", n, v.scalar_tensor_tensor(out=B["h"][:, u, :], in0=B["f"][:, u, :], scalar=K["nt2"],
                                                            in1=B["e"][:, u, :], op0=ALU.max, op1=ALU.add), 1)
                    P.free(dv, "y", i, u)
                    tt(B["c"][:, u, :], B["h"][:, u, :], B["in0"][:, u, :], ALU.add).then_inc(P.s("vec"), 1)
                for u in us:
                    normed(P, i, u, 1, K["ct2"])
            in_pairs(dv, BLOCKS, body)
            P_e4.all_done(dv)

            def soft(P, stat):
                def body(i, us):
                    for u in us:
                        n = 2 * i + u
                        P.landed(dv, "ld", i, u)
                        P.wait(dv, "act", n)
                        own(P, "vec", n, v.scalar_tensor_tensor(out=B["h"][:, u, :], in0=B["in0"][:, u, :],
                                                                scalar=K["nt2"], in1=B["e"][:, u, :],
                                                                op0=ALU.max, op1=ALU.add), 1)
                        P.free(dv, "y", i, u)
                        tt(B["c"][:, u, :], B["h"][:, u, :], B["in0"][:, u, :], ALU.add).then_inc(P.s("vec"), 1)
                    for u in us:
                        if stat:
                            P.free(dv, "h", i, u)
                        normed(P, i, u, 1, K["ct2"])
                    if stat:
                        for u in us:
                            n = 2 * i + u
                            P.wait(dv, "h", n)
                            v.bn_stats(stats["n"][:, bass.ds(n, 1), :], bk(u, 3)).then_inc(P.s("bnf"), 1)
                in_pairs(dv, P.chunks, body)
                P.all_done(dv)
            soft(P_node1, True)
            soft(P_node1e, False)
            clear_carry(4)

            def body(i, us):
                P = P_e5
                for u in us:
                    n = 2 * i + u
                    P.stored(dv, "st", i, u)
                    overlay(P, i, u, B["o0"])
                    scan(P, n, u, B["e"], B["same"], B["o0"])
                    P.free(dv, "h", i, u)
                    tt(B["b"][:, u, :], B["e"][:, u, :], B["in1"][:, u, :], ALU.add).then_inc(P.s("vec"), 1)
                for u in us:
                    n = 2 * i + u
                    P.wait(dv, "evs", n)
                    for k, (buf, name, done) in enumerate((("f", "hd", "bnf"), ("g", "hu", "bnc"))):
                        own(P, "mask", n, v.scalar_tensor_tensor(out=B[buf][:, u, :], in0=B["more"][:, u, :], scalar=0.0,
                                                                 in1=(B["o1"][:, u, :], bk(u, 2))[k], op0=ALU.is_equal, op1=ALU.mult), k + 1)
                        v.bn_stats(stats[name][:, bass.ds(n, 1), :], B[buf][:, u, :]).then_inc(P.s(done), 1)
            in_pairs(dv, BLOCKS, body)
            P_e5.all_done(dv)

            moments(("n", "hd", "hu"))
            assert small[0] == STATS3, small
            dv.wait_ge(s_pe_small, 8)
            sm(v.tensor_copy(hold[:, 0:6], bank[0][:, 0:6]))
            sm(v.tensor_tensor(hold[:, 2:4], hold[:, 2:4], hold[:, 4:6], ALU.subtract))
            sm(v.scalar_tensor_tensor(out=hold[:, 6:8], in0=hold[:, 2:4], scalar=float(EDGES) / NODES,
                                      in1=hold[:, 0:2], op0=ALU.mult, op1=ALU.add))
            affine(hold[:, 6:7], hold[:, 7:8], K["g3"], K["be3"], K["s3"], K["t3"])
            sm(v.tensor_tensor(K["tmp2"], hold[:, 6:7], K["bl2"], ALU.add))
            sm(v.tensor_tensor(K["tmp2"], K["bl2"], K["tmp2"], ALU.subtract))
            sm(v.tensor_tensor(K["tmp2"], K["tmp2"], K["s3"], ALU.mult))
            sm(v.tensor_tensor(K["t3"], K["be3"], K["tmp2"], ALU.add))
            assert small[0] == STATS3B, small

            def relu_bn(P, x2):
                def body(i, us):
                    for u in us:
                        P.landed(dv, "ld", i, u)
                        P.free(dv, "y", i, u)
                        P.wait(dv, "act", 2 * i + u)
                        tt(B["c"][:, u, :], B["a"][:, u, :], B[x2][:, u, :], ALU.add).then_inc(P.s("vec"), 1)
                    for u in us:
                        normed(P, i, u, 1, None)
                in_pairs(dv, P.chunks, body)
                P.all_done(dv)
            relu_bn(P_e6, "in1")
            relu_bn(P_e6s, "in0")

            P = P_node2

            def body(i, us):
                for u in us:
                    P.landed(dv, "ld", i, u)
                    P.wait(dv, "act", 2 * i + u)
                    tt(B["c"][:, u, :], B["b"][:, u, :], B["in0"][:, u, :], ALU.add).then_inc(P.s("vec"), 1)
                for u in us:
                    P.wait(dv, "rstd", 2 * i + u)
                    tt(B["o0"][:, u, :], bk(u, 1), B["h"][:, u, :], ALU.mult).then_inc(P.s("out"), 1)
                for u in us:
                    P.wait(dv, "hid", 2 * i + u)
                    P.free(dv, "g", i, u)
                    v.tensor_scalar(B["a"][:, u, :], bk(u, 0), K["b31"], 0.0, ALU.add, ALU.max).then_inc(P.s("relu0"), 1)
                for u in us:
                    P.wait(dv, "g", 2 * i + u)
                    own(P, "z", 2 * i + u, v.tensor_scalar(B["wts"][:, u, :], bk(u, 1), K["b32"], None, ALU.add))
                    neg_abs(P, i, u, B["in1"][:, u, :], B["wts"][:, u, :])
                for u in us:
                    sigmoid_arg(P, i, u, B["in3"][:, u, :], B["wts"][:, u, :], B["e"][:, u, :])
                for u in us:
                    P.free(dv, "y2", i, u)
                    P.wait(dv, "sig", 2 * i + u)
                    tt(B["f"][:, u, :], B["in4"][:, u, :], B["o0"][:, u, :], ALU.add).then_inc(P.s("add"), 1)
                for u in us:
                    P.wait(dv, "rstd2", 2 * i + u)
                    tt(B["o1"][:, u, :], bk(u, 3), B["dinv"][:, u, :], ALU.mult).then_inc(P.s("out2"), 1)
            in_pairs(dv, P.chunks, body)
            P.all_done(dv)
            clear_carry(5)

            P = P_e7

            def body(i, us):
                for u in us:
                    n = 2 * i + u
                    overlay(P, i, u, B["a"])
                for u in us:
                    n = 2 * i + u
                    P.wait(dv, "evs", n)
                    own(P, "vec", n, tt(B["g"][:, u, :], B["b"][:, u, :], B["wts"][:, u, :], ALU.mult), 1)
                    scan(P, n, u, B["e"], B["same"], B["g"])
                    P.wait(dv, "evd", n)
                    own(P, "vec", n, tt(B["f"][:, u, :], B["c"][:, u, :], B["dinv"][:, u, :], ALU.mult), 2)
                    own(P, "vec", n, tt(B["in4"][:, u, :], B["f"][:, u, :], B["e"][:, u, :], ALU.add), 3)
                    own(P, "vec", n, tt(B["in3"][:, u, :], B["in4"][:, u, :], B["dinv"][:, u, :], ALU.mult), 4)
                    v.tensor_scalar(B["h"][:, u, :], B["in3"][:, u, :], 0.0, None, ALU.max).then_inc(P.s("relu1"), 1)
                for u in us:
                    n = 2 * i + u
                    P.wait(dv, "h", n)
                    P.stored(dv, "st", i, u)
                    v.scalar_tensor_tensor(out=B["o0"][:, u, :], in0=bk(u, 0), scalar=K["b32"], in1=B["dinv"][:, u, :],
                                           op0=ALU.add, op1=ALU.mult).then_inc(P.s("out"), 1)
            in_pairs(dv, BLOCKS, body)
            P.all_done(dv)
            clear_carry(6)

            P = P_e8

            def body(i, us):
                for u in us:
                    n = 2 * i + u
                    overlay(P, i, u, B["a"])
                    own(P, "msg", n, tt(B["g"][:, u, :], B["a"][:, u, :], B["wts"][:, u, :], ALU.mult), 3)
                    scan(P, n, u, B["b"], B["same"], B["g"])
                    own(P, "vec", n, tt(B["h"][:, u, :], B["b"][:, u, :], B["in2"][:, u, :], ALU.add), 1)
                    own(P, "vec", n, tt(B["c"][:, u, :], B["h"][:, u, :], B["dinv"][:, u, :], ALU.mult), 2)
                    neg_abs(P, i, u, B["o1"][:, u, :], B["c"][:, u, :])
                for u in us:
                    sigmoid_arg(P, i, u, B["in3"][:, u, :], B["c"][:, u, :], B["e"][:, u, :])
                for u in us:
                    n = 2 * i + u
                    P.wait(dv, "sig", n)
                    P.free(dv, "y", i, u)
                    tt(B["f"][:, u, :], B["in4"][:, u, :], B["in1"][:, u, :], ALU.add).then_inc(P.s("add"), 1)
                for u in us:
                    P.free(dv, "row", i, u)
                    normed(P, i, u, 1, None, stored=False, rs="g2")
            in_pairs(dv, BLOCKS, body)


KEYS, PER = 5000, EDGES // TILE
SORT_KEYS = 1 + PER * 6 + 3
SORT_RANKED = 4 + EDGES // KEYS * SORT_KEYS
SORT_END = SORT_RANKED + 5

WEIGHT_DMAS = 5 + 12 + 6 + 1 + 2 * 14
CONST_END = 7
SETUP_SCAN, SETUP_CARRY, SETUP_ROWS = 10, 15, 23
INFO_ROWS = BLOCKS + 5
STATS1 = 6
STATS1B = STATS1 + 1 + 10
STATS2 = STATS1B + 3
STATS2B = STATS2 + 1 + 5 + 1
STATS2C = STATS2B + 1
STATS3 = STATS2C + 9
STATS3B = STATS3 + 3 + 5 + 4

_ARGS = ["xt", "x", "src", "dstp", "ea", "ew", "w1", "w2", "w2t", "b1", "b2", "wf", "bf", "g1", "be1", "g2",
         "be2", "wl2", "bl2", "g3", "be3", "w31t", "b31", "w32t", "b32"]


def kernel(**inputs):
    import concourse.bacc as _bacc
    from concourse import mybir as _mybir
    from concourse.bass_utils import run_bass_kernel_spmd as _run

    a = {k: np.asarray(v) for k, v in inputs.items()}
    x = a["x"]
    arrays = {
        "xt": x.reshape(NODE_CHUNKS, TILE, 2, 4, D).transpose(0, 2, 4, 3, 1).reshape(NODE_CHUNKS, 128, COLS),
        "x": x, "src": a["src"],
        "dstp": np.concatenate([np.full(1, -1, a["dst"].dtype), a["dst"], np.full(1, -1, a["dst"].dtype)]),
        "ea": a["edge_attr_64"], "ew": a["edge_weight1"].reshape(-1),
        "w1": a["L0_gnn_W1"], "w2": a["L0_gnn_W2"], "w2t": a["L0_gnn_W2"].T, "b1": a["L0_gnn_b1"],
        "b2": a["L0_gnn_b2"], "wf": a["L1_gnn_W_full"], "bf": a["L1_gnn_b_full"], "g1": a["L1_gnn_bn1_g"],
        "be1": a["L1_gnn_bn1_b"], "g2": a["L1_gnn_bn2_g"], "be2": a["L1_gnn_bn2_b"], "wl2": a["L2_gnn_W"],
        "bl2": a["L2_gnn_b"], "g3": a["L2_gnn_gamma"], "be3": a["L2_gnn_beta"], "w31t": a["L3_gnn_W1"].T,
        "b31": a["L3_gnn_b1"], "w32t": a["L3_gnn_W2"].T, "b32": a["L3_gnn_b2"],
    }
    nc = _bacc.Bacc("TRN2", target_bir_lowering=False, num_devices=1)
    feed, args = {}, []
    for name in _ARGS:
        v = np.ascontiguousarray(arrays[name])
        feed[f"in_{name}"] = v
        args.append(nc.dram_tensor(f"in_{name}", v.shape, _mybir.dt.from_np(v.dtype), kind="ExternalInput").ap())
    args.append(nc.dram_tensor("out_0", (NODES, D), _mybir.dt.float32, kind="ExternalOutput").ap())
    gnn(nc, *args)
    r = _run(nc, [feed], core_ids=[0])
    return r.results[0]["out_0"]
```

```python
import numpy as np
import concourse.bass as bass
import concourse.mybir as mybir
from contextlib import ExitStack

F32 = mybir.dt.float32
I32 = mybir.dt.int32
ALU = mybir.AluOpType
ACT = mybir.ActivationFunctionType

NODES, EDGES, D, HID = 100000, 25000, 64, 128
COLS = 500
PACK = 2 * COLS
TILE = 125
TILES = PACK // TILE
NODE_CHUNKS = NODES // PACK
BLOCKS = EDGES // PACK
NODE2_EARLY = 32
CHUNK_BUFFERS = 11
NAT = 100
SKIP = 1 << 20
EPS = 1e-5


class Sems:

    def __init__(self, make):
        self.make, self.sem, self.total = make, {}, {}
        self.passed = {}

    def wait(self, eng, sem, value):
        eng.wait_ge(sem, value)
        if not isinstance(value, int) and id(eng) in self.passed:
            eng.sem_inc(self.passed[id(eng)], 1)

    def get(self, name):
        if name not in self.sem:
            self.sem[name], self.total[name] = self.make(name), 0
        return self.sem[name]


class Phase:

    def __init__(self, sems, chunks, steps, dmas, slots=4):
        self.chunks, self.sems, self.steps, self.dmas = chunks, sems, steps, dmas
        self.slots = slots
        self.label = f"{chunks} {list(steps)[:3]}"
        self.base = {}
        for name, count in steps.items():
            sems.get(name)
            self.base[name] = sems.total[name]
            sems.total[name] += chunks * count
        for name, count in dmas.items():
            for u in range(slots):
                slot = f"{name}{u}"
                sems.get(slot)
                self.base[slot] = sems.total[slot]
                sems.total[slot] += self.in_slot(u) * 16 * count
        self.ends = [(sems.sem[n], self.base[n] + chunks * c) for n, c in steps.items()]
        self.ends += [(sems.sem[f"{n}{u}"], self.base[f"{n}{u}"] + self.in_slot(u) * 16 * c)
                      for n, c in dmas.items() for u in range(slots)]

    def in_slot(self, u):
        return (self.chunks + self.slots - 1 - u) // self.slots

    def at(self, i, u):
        return self.slots * i + u

    def s(self, name):
        return self.sems.sem[name]

    def wait(self, eng, step, n, part=None):
        q = self.steps[step]
        part = q if part is None else part
        self.sems.wait(eng, self.s(step), self.base[step] + n * q + part)

    def free(self, eng, step, i, u):
        if not (isinstance(i, int) and i == 0):
            self.wait(eng, step, self.at(i, u) - self.slots)

    def landed(self, eng, dma, i, u):
        slot = f"{dma}{u}"
        self.sems.wait(eng, self.s(slot), self.base[slot] + (i + 1) * (16 * self.dmas[dma]))

    def stored(self, eng, dma, i, u):
        if not (isinstance(i, int) and i == 0):
            slot = f"{dma}{u}"
            self.sems.wait(eng, self.s(slot), self.base[slot] + i * (16 * self.dmas[dma]))

    def all_done(self, eng):
        for sem, value in self.ends:
            if value:
                eng.wait_ge(sem, value)


def in_groups(eng, P, body):
    body(0, range(P.slots))
    if P.chunks // P.slots > 1:
        with eng.Fori(1, P.chunks // P.slots) as i:
            body(i, range(P.slots))
    if P.chunks % P.slots:
        body(P.chunks // P.slots, range(P.chunks % P.slots))


def gnn(nc, xt, x, src_in, dstp, ea_in, ew, w1, w2, w2t, b1, b2, wf, bf, g1, be1, g2, be2,
        wl2, bl2, g3, be3, w31t, b31, w32t, b32, out):
    def dram(name, *shape):
        return nc.dram_tensor(name, list(shape), F32).ap()

    XDR, XSR = dram("xdr", BLOCKS, TILE, 512), dram("xsr", BLOCKS, TILE, 512)
    SLOTS = dram("slots", NODES, 4)
    XE = dram("xe", 2 * BLOCKS, 128, COLS)
    X1 = dram("x1", NODE_CHUNKS + 2 * BLOCKS, 128, COLS)
    X2 = dram("x2", NODE_CHUNKS + 2 * BLOCKS, 128, COLS)
    GU, GD = dram("gu", 2 * BLOCKS, 128, COLS), dram("gd", BLOCKS, 128, COLS)
    X1D, X1F = dram("x1d", BLOCKS, 128, COLS), dram("x1f", BLOCKS, 128, COLS)
    TF, TC, UPD = (dram(n, BLOCKS, 128, COLS) for n in ("tf", "tc", "upd"))
    X2D, X2S, HD = (dram(n, BLOCKS, 128, COLS) for n in ("x2d", "x2s", "hd"))
    X3D, X3S, QS, QD = (dram(n, BLOCKS, 128, COLS) for n in ("x3d", "x3s", "qs", "qd"))
    TAB = [dram(f"tab{n}", EDGES, D) for n in range(5)]
    OV = [dram(f"ov{n}", BLOCKS, TILE, 512) for n in range(5)]
    ROWS = dram("rows", 2 * BLOCKS, len(ROW_NAMES), COLS)
    META_S = dram("meta_sorted", EDGES + 2, 4)
    EA_S = dram("ea_sorted", EDGES + 2, D)

    ctx = ExitStack()
    with ctx:
        def sb(name, shape, dt=F32):
            return ctx.enter_context(nc.sbuf_tensor(name, list(shape), dt))

        def sem(name):
            return ctx.enter_context(nc.semaphore(name))

        bank = [ctx.enter_context(nc.psum_tensor(f"bank{k}", [128, 512], F32)) for k in range(8)]

        ident, J, C, HALF = (sb(n, [128, 128]) for n in ("ident", "J", "C", "HALF"))
        MATS = ["w1a", "w1b", "w2a", "w2b", "w2ca", "w2cb", "srcf", "dstf", "nbrf", "srcc", "dstc",
                "nbrc", "wl2", "w31", "w32"]
        mats = sb("mats", [128, len(MATS), 128])
        M = {n: mats[:, k, :] for k, n in enumerate(MATS)}
        w2t_sb = sb("w2t_sb", [D, HID])
        CN = ["b1", "b2", "bf", "bc", "g1f", "g1c", "be1f", "be1c", "g2", "be2", "bl2", "g3", "be3",
              "b31", "b32", "cb2", "s1f", "t1f", "s1c", "t1c", "s2", "t2", "nt2",
              "ct2", "s3", "t3", "eps", "tmp0", "tmp1", "tmp2", "tmp3"]
        cols = sb("cols", [128, len(CN)])
        K = {n: cols[:, k:k + 1] for k, n in enumerate(CN)}
        nat_i = sb("nat_i", [NAT, 4, 250], I32)
        nat = sb("nat", [NAT, 12, 250])
        tiny = sb("tiny", [1, 4, NAT])
        carry_in = sb("carry_in", [NAT, 1])
        col = sb("col", [TILE, 4, 200])
        idx_src, idx_dst, idx_last = (sb(n, [TILE, 200], I32) for n in ("idx_src", "idx_dst", "idx_last"))
        idx_f = sb("idx_f", [TILE, 200])
        slot_rows = sb("slot_rows", [TILE, 200, 4])
        row_no = sb("row_no", [TILE, 200], I32)
        src_info = sb("src_info", [TILE, 200, 4])
        gat = sb("gat", [TILE, 4, TILES, D])
        gidx = sb("gidx", [TILE, 4, TILES], I32)
        grow = sb("grow", [TILE, 4, TILES, 4])
        bufs = sb("bufs", [128, 4 * CHUNK_BUFFERS, COLS])

        def buffers(names, rows=()):
            R = len(rows)
            views = {}
            for k, row in enumerate(rows):
                for name in row.split():
                    views[name] = bufs[:, k:4 * R:max(R, 1), :]
            views["rows"] = bufs[:, 0:4 * R, :].rearrange("p (u r) c -> p u r c", u=4) if R else None
            for k, entry in enumerate(names):
                for name in entry.split():
                    views[name] = bufs[:, 4 * (R + k):4 * (R + k) + 4, :]
            assert R + len(names) <= CHUNK_BUFFERS
            return views

        rows_in_all = sb("rows_in", [TILE, 2, 4, TILES, D])
        rows_in = [rows_in_all[:, k] for k in (0, 1)]
        default = rows_in_all[:, :, :, :, :].rearrange("p k u t f -> p (k u t f)")[:, 0:NODES // TILE * 4]\
            .rearrange("p (t c) -> p t c", c=4)
        rows_out = sb("rows_out", [TILE, 4, TILES, D])
        carry = sb("carry", [128, 1])
        viol = sb("viol", [NAT, 1])
        flag = sb("flag", [1, 1], I32)
        pad = sb("pad", [1, 4])
        key_col, edge_col = sb("key_col", [TILE, 1]), sb("edge_col", [TILE, 1])
        part, rank = sb("part", [TILE, PER]), sb("rank", [TILE, PER])
        arena = bufs[0:TILE, :, :].rearrange("p n c -> p (n c)")
        key_i, key_f, no_i, no_f = (arena[:, k * KEYS:(k + 1) * KEYS] for k in range(4))
        key_i, no_i, work = key_i.bitcast(I32), no_i.bitcast(I32), no_i
        own_i = arena[:, 4 * KEYS:4 * KEYS + 2 * PER].rearrange("p (k t) -> p k t", k=2).bitcast(I32)
        own_no = arena[:, 4 * KEYS + 2 * PER:4 * KEYS + 3 * PER].bitcast(I32)
        own_f = arena[:, 4 * KEYS + 3 * PER:4 * KEYS + 6 * PER].rearrange("p (k t) -> p k t", k=3)
        meta = src_info
        rank_i = idx_last
        meta_in = bufs[0:NAT, :, :].rearrange("p n c -> p (n c)")[:, 0:3000].rearrange("p (k c) -> p k c", k=3)
        stats = {n: sb(f"stats_{n}", [128, k, 6]) for n, k in
                 (("f", BLOCKS), ("c", BLOCKS), ("u", BLOCKS), ("n", NODE_CHUNKS), ("hd", BLOCKS), ("hu", BLOCKS))}
        mv = sb("mv", [128, 8, 2])
        mom = sb("mom", [128, 8, 2])
        hold = sb("hold", [128, 8])

        sems = Sems(sem)
        SIG = {"nabs": 1, "lsig": 2, "arg": 1, "sig": 1}
        LN = {"y": 1, "sq": 1, "var": 1, "lnv": 1, "rstd": 1, "out": 1}
        P_node0 = Phase(sems, NODE_CHUNKS, {"hid": 1, "relu0": 1, "relu1": 1, **LN}, {"ld": 1, "st": 1})
        P_e0 = Phase(sems, BLOCKS, {"tr": 1, "evs": 1, "evd": 1, "msg": 1, "scan": 4, "vec": 3, "hid": 1,
                                    "relu0": 1, "relu1": 1, "g": 1, "out": 1, "row": 1, "evrow": 1},
                     {"ld": 4, "st": 4})
        P_node0e = Phase(sems, 2 * BLOCKS, {"hid": 1, "relu0": 1, "relu1": 1, "g": 1, "evs": 1, **LN},
                         {"ld": 1, "st": 2})
        P_e1 = Phase(sems, BLOCKS, {"tr": 1, "msg": 2, "scan": 4, "vec": 3, **LN, "row": 1, "evrow": 1},
                     {"ld": 6, "st": 2})
        P_e2 = Phase(sems, BLOCKS, {"tr": 1, "evs": 1, "msg": 2, "vec": 1, "scan": 4, "t": 1, "evf": 1,
                                    "evc": 1, "bnf": 1, "bnc": 1}, {"ld": 7, "st": 4})
        P_e3 = Phase(sems, BLOCKS, {"act": 3, "msg": 2, **SIG, "vec": 2, "scan": 4, "out": 1, "bnf": 1}, {"ld": 4, "st": 1})
        P_e4 = Phase(sems, BLOCKS, {"msg": 1, "vec": 2, "act": 3, **LN, "row": 1, "evrow": 1}, {"ld": 2, "st": 2})
        P_node1 = Phase(sems, NODE_CHUNKS, {"vec": 2, "act": 3, **LN, "h": 1, "bnf": 1}, {"ld": 1, "st": 1})
        P_node1e = Phase(sems, 2 * BLOCKS, {"vec": 2, "act": 3, **LN}, {"ld": 1, "st": 1})
        P_e5 = Phase(sems, BLOCKS, {"tr": 1, "msg": 2, "scan": 4, "vec": 1, "h": 1, "evs": 1, "mask": 2,
                                    "bnf": 1, "bnc": 1}, {"ld": 6, "st": 2})
        P_e6 = Phase(sems, BLOCKS, {"act": 1, "vec": 1, **LN, "row": 1, "evrow": 1}, {"ld": 2, "st": 2})
        P_e6s = Phase(sems, BLOCKS, {"h": 1, "act": 1, "vec": 1, **LN}, {"ld": 1, "st": 1})
        NODE2 = {"h": 1, "act": 1, "vec": 1, **LN, "hid": 1, "relu0": 1, "g": 1, "z": 1, **SIG,
                 "add": 1, "y2": 1, "sq2": 1, "var2": 1, "lnv2": 1, "rstd2": 1, "out2": 1, "row": 1, "evrow": 1}
        P_node2 = Phase(sems, NODE2_EARLY, NODE2, {"ld": 1, "st": 1})
        P_e7 = Phase(sems, BLOCKS, {"tr": 1, "msg": 2, "hid": 1, "evs": 1, "evd": 1, "relu0": 1, "vec": 4,
                                    "scan": 4, "relu1": 1, "g": 1, "h": 1, "act": 1, "out": 1, "row": 1,
                                    "evrow": 1}, {"ld": 5, "st": 3})
        P_node2b = Phase(sems, NODE_CHUNKS - NODE2_EARLY, NODE2, {"ld": 1, "st": 1})
        P_e8 = Phase(sems, BLOCKS, {"tr": 1, "msg": 3, "scan": 4, "vec": 2, **SIG, "add": 1,
                                    **LN, "row": 1, "evrow": 1}, {"ld": 6})

        s_w, s_nat, s_def, s_rows = sem("s_w"), sem("s_nat"), sem("s_def"), sem("s_rows")
        s_const, s_dconst, s_setup, s_tcol, s_ccol = (sem(n) for n in
                                                      ("s_const", "s_dconst", "s_setup", "s_tcol", "s_ccol"))
        s_pe_small, s_dv_small, s_idx = sem("s_pe_small"), sem("s_dv_small"), sem("s_idx")
        s_info, s_ac_small = sem("s_info"), sem("s_ac_small")
        s_gcopy, s_gather = sem("s_gcopy"), [sem("s_gather0"), sem("s_gather1")]
        s_gstore = [sem("s_gstore0"), sem("s_gstore1")]
        s_scatter = [sem("s_scatter0"), sem("s_scatter1")]
        s_final = [sem(f"s_final{u}") for u in range(4)]
        s_iota = sem("s_iota")
        s_flag, s_own, s_keys, s_keys_used, s_rank, s_numbered, s_ranked = (sem(n) for n in (
            "s_flag", "s_own", "s_keys", "s_keys_used", "s_rank", "s_numbered", "s_ranked"))
        s_ea_in, s_rank_copy, s_sorted, s_meta, s_pad, s_ea = (sem(n) for n in (
            "s_ea_in", "s_rank_copy", "s_sorted", "s_meta", "s_pad", "s_ea"))
        s_passed_sp, s_passed_pool = sem("s_passed_sp"), sem("s_passed_pool")

        POOL = ["xd", "slot", "info", "xs", "ov0", "ov1", "ov2", "ov3", "ov4", "final"]
        per_slot = [(BLOCKS + 1 - u) // 2 for u in (0, 1)]
        GATHERS = [n for n in POOL if n not in ("slot", "final")]
        STORES = [n for n in GATHERS if n != "info"]

        def gather_base(name, half):
            return GATHERS.index(name) * (BLOCKS // 4 * 2 + BLOCKS % 4 * (1 - half)) * 16 * TILES

        def store_base(name, half):
            return STORES.index(name) * pairs_in(half) * 16

        def pairs_in(half):
            return (BLOCKS + 3 - 2 * half) // 4

        def gathered(eng, name, i, u):
            sems.wait(eng, s_gstore[u // 2], store_base(name, u // 2) + (i + 1) * 16)

        def scattered(eng, i, u):
            if not (isinstance(i, int) and i == 0):
                sems.wait(eng, s_final[u], i * (16 * TILES))

        PAIRS = Phase(sems, BLOCKS, {}, {}, slots=2)
        FOURS = Phase(sems, BLOCKS, {}, {})
        nodes = buffers(("in0", "in1", "a", "b", "c", "d", "e", "g", "h", "o0", "o1"))
        for P in (P_node0, P_node0e, P_e4, P_node1, P_node1e, P_e6, P_e6s, P_node2, P_node2b):
            P.B = nodes
        P_e0.B = buffers(("o1", "o2", "a", "e", "f g b", "c", "d", "o0"), ROW_SETS["e0"][1])
        P_e1.B = buffers(("in0 a", "in1", "in2", "e f b c", "d", "g", "o0"), ROW_SETS["e1"][1])
        P_e2.B = buffers(("in0", "in1 b", "a", "o3", "o0", "o1", "o2"), ROW_SETS["e2"][1])
        P_e3.B = buffers(("in0", "in1", "e g h", "f in3 in4", "g2 a", "b c d", "o1", "o0"), ROW_SETS["e3"][1])
        P_e5.B = buffers(("in0", "in1", "in2", "o0", "e b", "o1", "f", "g"), ROW_SETS["e3"][1])
        P_e7.B = buffers(("in0 a", "in1", "b g", "c f in4 in3 h o0", "d", "e", "o1"), ROW_SETS["e7"][1])
        P_e8.B = buffers(("in0 a g o1 e", "in1", "in2", "b h c in3 in4 f", "d", "g2", "o0"), ROW_SETS["e8"][1])
        block = ctx.enter_context(nc.Block())

        @block.sync
        def _(sp):
            def factors(P, which, u, blk):
                first, names = ROW_SETS[which]
                for h in (0, 1):
                    yield P.B["rows"][64 * h:64 * h + 64, u], \
                        ROWS[bass.ds(2 * blk + h, 1), first:first + len(names), :].to_broadcast([64, len(names), COLS])

            def store_factors(pairs):
                for k, name in pairs:
                    for r, other in enumerate(ROW_NAMES):
                        if other == name:
                            for a in (0, 1):
                                sp.dma_start(ROWS[:, r, 250 * a:250 * a + 250], nat[a::2, k, :]).then_inc(s_rows, 16)

            for k, off in enumerate((0, 1, 2)):
                sp.dma_start(nat_i[:, k, :], dstp[off:off + EDGES].rearrange("(a b) -> a b", a=NAT)).then_inc(s_nat, 16)
            sp.dma_start(nat_i[:, 3, :], src_in.rearrange("(a b) -> a b", a=NAT)).then_inc(s_nat, 16)
            sp.dma_start(nat[:, 11, :], ew.rearrange("(a b) -> a b", a=NAT)).then_inc(s_nat, 16)
            sems.passed[id(sp)] = s_passed_sp
            sp.wait_ge(s_dconst, 1)

            def twice(name, src):
                for h in (0, 1):
                    sp.dma_start(M[name][64 * h:64 * h + 64, 64 * h:64 * h + 64], src).then_inc(s_w, 16)

            sp.dma_start(M["w1a"][0:64, :], w1).then_inc(s_w, 16)
            sp.dma_start(M["w1b"][64:128, :], w1).then_inc(s_w, 16)
            sp.dma_start(M["w2a"][:, 0:64], w2).then_inc(s_w, 16)
            sp.dma_start(M["w2b"][:, 64:128], w2).then_inc(s_w, 16)
            sp.dma_start(w2t_sb[:, :], w2t).then_inc(s_w, 16)
            for part, o in (("f", 0), ("c", 64)):
                for k, name in enumerate(("src", "dst", "nbr")):
                    twice(name + part, wf[64 * k:64 * k + 64, o:o + 64])
            twice("wl2", wl2)
            twice("w31", w31t)
            twice("w32", w32t)

            def column(name, src):
                n = src.shape[0]
                for h in range(128 // n):
                    sp.dma_start(K[name][n * h:n * h + n, :], src.rearrange("(a o) -> a o", o=1)).then_inc(s_w, 16)

            for name, src in (("b1", b1), ("b2", b2), ("bf", bf[0:64]), ("bc", bf[64:128]), ("g1f", g1[0:64]),
                              ("g1c", g1[64:128]), ("be1f", be1[0:64]), ("be1c", be1[64:128]), ("g2", g2),
                              ("be2", be2), ("bl2", bl2), ("g3", g3), ("be3", be3), ("b31", b31), ("b32", b32)):
                column(name, src)
            sp.wait_ge(s_dconst, 6)
            sp.dma_start(SLOTS.rearrange("(p t) c -> p (t c)", p=TILE),
                         default[:, :, :].rearrange("p t c -> p (t c)")).then_inc(s_def, 16)
            sp.wait_ge(s_flag, 2)
            unsorted = sp.value_load(flag[0:1, 0:1])
            with sp.If(unsorted > 0):
                for k, row in enumerate((dstp[1:1 + EDGES], src_in)):
                    sp.dma_start(own_i[:, k, :], row.rearrange("(p t) -> p t", p=TILE)).then_inc(s_own, 16)
                sp.dma_start(own_f[:, 2, :], ew.rearrange("(p t) -> p t", p=TILE)).then_inc(s_own, 16)
                for r in (0, EDGES + 1):
                    sp.dma_start(META_S[r:r + 1, :], pad[:, :]).then_inc(s_pad, 16)
                for c in range(EDGES // KEYS):
                    if c:
                        sp.wait_ge(s_keys_used, c)
                    sp.dma_start(key_i, dstp[1 + c * KEYS:1 + (c + 1) * KEYS].rearrange("(o c) -> o c", o=1)
                                 .to_broadcast([TILE, KEYS])).then_inc(s_keys, 16)
                sp.wait_ge(s_sorted, BLOCKS * TILES * 2 * 16)
                sp.wait_ge(s_pad, 32)
                for off in (0, 1, 2):
                    sp.dma_start(meta_in[:, off, :], META_S[off:off + EDGES, :].rearrange("(a b) c -> a (b c)", a=NAT))\
                      .then_inc(s_meta, 16)
                sp.wait_ge(s_rank, SORT_END)
                sp.sem_inc(s_ea, 16)
            with sp.Else():
                sp.dma_start(EA_S[1:1 + EDGES, :], ea_in).then_inc(s_ea, 16)
            sp.wait_ge(s_setup, SETUP_ROWS)
            store_factors(((11, "w"), (4, "same"), (6, "more"), (10, "dinv")))

            def run(P, load, store, before=None):
                if before:
                    before()
                last = P.in_slot(0)

                def slots(i):
                    return range(min(P.slots, P.chunks - i * P.slots))

                def loads(i, us):
                    for u in us:
                        for dst, src in load(i, u):
                            sp.dma_start(dst, src).then_inc(P.s(f"ld{u}"), 16)

                def stores(i, us):
                    for u in us:
                        for dst, src in store(i, u):
                            sp.dma_start(dst, src).then_inc(P.s(f"st{u}"), 16)

                loads(0, slots(0))
                loads(1, slots(1))
                stores(0, slots(0))
                if last - 2 > 1:
                    with sp.Fori(1, last - 2) as i:
                        loads(i + 1, slots(0))
                        stores(i, slots(0))
                loads(last - 1, slots(last - 1))
                stores(last - 2, slots(0))
                stores(last - 1, slots(last - 1))

            def load(i, u):
                P_node0.free(sp, "y", i, u)
                yield P_node0.B["in0"][:, u, :], xt[P_node0.at(i, u), :, :]

            def store(i, u):
                P_node0.wait(sp, "out", P_node0.at(i, u))
                yield X1[P_node0.at(i, u), :, :], P_node0.B["o0"][:, u, :]
            run(P_node0, load, store)
            P_node0.all_done(sp)

            sp.wait_ge(s_info, INFO_ROWS)
            store_factors(((0, "keep"), (1, "sdinv"), (2, "wd")))
            sp.wait_ge(s_rows, 20 * 16)
            sp.wait_ge(s_def, 16)

            def load(i, u):
                n = P_e0.at(i, u)
                P_e0.free(sp, "out", i, u)
                gathered(sp, "xs", i, u)
                yield rows_in[0][:, u, :, :].rearrange("p t f -> p (t f)"), XSR[n, :, :]
                yield rows_in[1][:, u, :, :].rearrange("p t f -> p (t f)"), XDR[n, :, :]
                yield from factors(P_e0, "e0", u, n)

            def store(i, u):
                n = P_e0.at(i, u)
                P_e0.wait(sp, "evs", n)
                yield XE[n, :, :], P_e0.B["o1"][:, u, :]
                P_e0.wait(sp, "evd", n)
                yield XE[BLOCKS + n, :, :], P_e0.B["o2"][:, u, :]
                P_e0.wait(sp, "out", n)
                yield GD[n, :, :], P_e0.B["o0"][:, u, :]
                P_e0.wait(sp, "evrow", n)
                yield table(0, n), flat(u)

            def table(t, n):
                return TAB[t].rearrange("(k p t) f -> k p (t f)", p=TILE, t=TILES)[n, :, :]

            def flat(u):
                return rows_out[:, u, :, :].rearrange("p t f -> p (t f)")
            run(P_e0, load, store)
            P_e0.all_done(sp)

            def load(i, u):
                P_node0e.free(sp, "y", i, u)
                yield P_node0e.B["in0"][:, u, :], XE[P_node0e.at(i, u), :, :]

            def store(i, u):
                P_node0e.wait(sp, "evs", P_node0e.at(i, u))
                yield GU[P_node0e.at(i, u), :, :], P_node0e.B["o1"][:, u, :]
                P_node0e.wait(sp, "out", P_node0e.at(i, u))
                yield X1[P_node0e.at(i, u) + NODE_CHUNKS, :, :], P_node0e.B["o0"][:, u, :]
            run(P_node0e, load, store)
            P_node0e.all_done(sp)

            def load(i, u):
                n = P_e1.at(i, u)
                P_e1.free(sp, "vec", i, u)
                gathered(sp, "ov0", i, u)
                yield rows_in[0][:, u, :, :].rearrange("p t f -> p (t f)"), OV[0][n, :, :]
                yield P_e1.B["in0"][:, u, :], GU[n, :, :]
                yield P_e1.B["in1"][:, u, :], XE[BLOCKS + n, :, :]
                yield P_e1.B["in2"][:, u, :], GD[n, :, :]
                yield from factors(P_e1, "e1", u, n)

            def store(i, u):
                n = P_e1.at(i, u)
                P_e1.wait(sp, "out", n)
                yield X1D[n, :, :], P_e1.B["o0"][:, u, :]
                P_e1.wait(sp, "evrow", n)
                yield table(1, n), flat(u)
            run(P_e1, load, store)
            P_e1.all_done(sp)

            sp.wait_ge(s_ea, 16)

            def load(i, u):
                n = P_e2.at(i, u)
                k = BLOCKS - 1 - n
                P_e2.free(sp, "scan", i, u)
                gathered(sp, "ov1", i, u)
                yield rows_in[0][:, u, :, :].rearrange("p t f -> p (t f)"), OV[1][k, :, :]
                for h in (0, 1):
                    yield rows_in[1][:, u, h::2, :], \
                        EA_S[bass.ds(k * PACK + h * COLS + 1, COLS), :].rearrange("(t p) f -> p t f", p=TILE)
                yield P_e2.B["in0"][:, u, :], X1[k + NODE_CHUNKS, :, :]
                yield P_e2.B["in1"][:, u, :], X1D[k, :, :]
                yield from factors(P_e2, "e2", u, k)

            def store(i, u):
                n = P_e2.at(i, u)
                k = BLOCKS - 1 - n
                P_e2.wait(sp, "scan", n)
                yield X1F[k, :, :], P_e2.B["o0"][:, u, :]
                P_e2.wait(sp, "evf", n)
                yield TF[k, :, :], P_e2.B["o1"][:, u, :]
                P_e2.wait(sp, "evc", n)
                yield TC[k, :, :], P_e2.B["o2"][:, u, :]
                P_e2.wait(sp, "msg", n)
                yield X2S[k, :, :], P_e2.B["o3"][:, u, :]
            run(P_e2, load, store)
            P_e2.all_done(sp)

            def load(i, u):
                n = P_e3.at(i, u)
                P_e3.free(sp, "out", i, u)
                yield P_e3.B["in0"][:, u, :], TF[n, :, :]
                yield P_e3.B["in1"][:, u, :], TC[n, :, :]
                yield from factors(P_e3, "e3", u, n)

            def store(i, u):
                P_e3.wait(sp, "out", P_e3.at(i, u))
                yield UPD[P_e3.at(i, u), :, :], P_e3.B["o0"][:, u, :]
            run(P_e3, load, store)
            P_e3.all_done(sp)

            def load(i, u):
                P_e4.free(sp, "out", i, u)
                yield P_e4.B["in0"][:, u, :], X1F[P_e4.at(i, u), :, :]
                yield P_e4.B["in1"][:, u, :], UPD[P_e4.at(i, u), :, :]

            def store(i, u):
                P_e4.wait(sp, "out", P_e4.at(i, u))
                yield X2D[P_e4.at(i, u), :, :], P_e4.B["o0"][:, u, :]
                P_e4.wait(sp, "evrow", P_e4.at(i, u))
                yield table(2, P_e4.at(i, u)), flat(u)
            run(P_e4, load, store)
            P_e4.all_done(sp)

            def load(i, u):
                P_node1.free(sp, "out", i, u)
                yield P_node1.B["in0"][:, u, :], X1[P_node1.at(i, u), :, :]

            def store(i, u):
                P_node1.wait(sp, "out", P_node1.at(i, u))
                yield X2[P_node1.at(i, u), :, :], P_node1.B["o0"][:, u, :]
            run(P_node1, load, store)
            P_node1.all_done(sp)

            def load(i, u):
                P_node1e.free(sp, "out", i, u)
                yield P_node1e.B["in0"][:, u, :], X1[P_node1e.at(i, u) + NODE_CHUNKS, :, :]

            def store(i, u):
                P_node1e.wait(sp, "out", P_node1e.at(i, u))
                yield X2[P_node1e.at(i, u) + NODE_CHUNKS, :, :], P_node1e.B["o0"][:, u, :]
            run(P_node1e, load, store)
            P_node1e.all_done(sp)

            def load(i, u):
                n = P_e5.at(i, u)
                P_e5.free(sp, "mask", i, u)
                gathered(sp, "ov2", i, u)
                yield rows_in[0][:, u, :, :].rearrange("p t f -> p (t f)"), OV[2][n, :, :]
                yield P_e5.B["in0"][:, u, :], X2[n + NODE_CHUNKS, :, :]
                yield P_e5.B["in1"][:, u, :], X2D[n, :, :]
                yield P_e5.B["in2"][:, u, :], X2[n + NODE_CHUNKS + BLOCKS, :, :]
                yield from factors(P_e5, "e3", u, n)

            def store(i, u):
                n = P_e5.at(i, u)
                P_e5.wait(sp, "msg", n)
                yield X2S[n, :, :], P_e5.B["o0"][:, u, :]
                P_e5.wait(sp, "evs", n)
                yield HD[n, :, :], P_e5.B["o1"][:, u, :]
            run(P_e5, load, store)
            P_e5.all_done(sp)

            def load(i, u):
                P_e6.free(sp, "out", i, u)
                yield P_e6.B["in0"][:, u, :], HD[P_e6.at(i, u), :, :]
                yield P_e6.B["in1"][:, u, :], X2D[P_e6.at(i, u), :, :]

            def store(i, u):
                P_e6.wait(sp, "out", P_e6.at(i, u))
                yield X3D[P_e6.at(i, u), :, :], P_e6.B["o0"][:, u, :]
                P_e6.wait(sp, "evrow", P_e6.at(i, u))
                yield table(3, P_e6.at(i, u)), flat(u)
            run(P_e6, load, store)
            P_e6.all_done(sp)

            def load(i, u):
                P_e6s.free(sp, "out", i, u)
                yield P_e6s.B["in0"][:, u, :], X2S[P_e6s.at(i, u), :, :]

            def store(i, u):
                P_e6s.wait(sp, "out", P_e6s.at(i, u))
                yield X3S[P_e6s.at(i, u), :, :], P_e6s.B["o0"][:, u, :]
            run(P_e6s, load, store)
            P_e6s.all_done(sp)

            def node2(P, first):
                def load(i, u):
                    P.free(sp, "vec", i, u)
                    yield P.B["in0"][:, u, :], X2[P.at(i, u) + first, :, :]

                def store(i, u):
                    P.wait(sp, "evrow", P.at(i, u))
                    yield out.rearrange("(k p t) f -> k p (t f)", p=TILE, t=TILES)[P.at(i, u) + first, :, :], flat(u)
                run(P, load, store)
                P.all_done(sp)
            node2(P_node2, 0)

            def load(i, u):
                n = P_e7.at(i, u)
                P_e7.free(sp, "out", i, u)
                gathered(sp, "ov3", i, u)
                yield rows_in[0][:, u, :, :].rearrange("p t f -> p (t f)"), OV[3][n, :, :]
                yield P_e7.B["in0"][:, u, :], X3S[n, :, :]
                yield P_e7.B["in1"][:, u, :], X3D[n, :, :]
                yield from factors(P_e7, "e7", u, n)

            def store(i, u):
                n = P_e7.at(i, u)
                P_e7.wait(sp, "act", n)
                yield QS[n, :, :], P_e7.B["o1"][:, u, :]
                P_e7.wait(sp, "out", n)
                yield QD[n, :, :], P_e7.B["o0"][:, u, :]
                P_e7.wait(sp, "evrow", n)
                yield table(4, n), flat(u)
            run(P_e7, load, store)
            P_e7.all_done(sp)

            node2(P_node2b, NODE2_EARLY)

            def load(i, u):
                n = P_e8.at(i, u)
                P_e8.free(sp, "add", i, u)
                gathered(sp, "ov4", i, u)
                yield rows_in[0][:, u, :, :].rearrange("p t f -> p (t f)"), OV[4][n, :, :]
                yield P_e8.B["in0"][:, u, :], QS[n, :, :]
                yield P_e8.B["in1"][:, u, :], X3D[n, :, :]
                yield P_e8.B["in2"][:, u, :], QD[n, :, :]
                yield from factors(P_e8, "e8", u, n)

            run(P_e8, load, lambda i, u: ())
            for u in range(4):
                sp.wait_ge(s_final[u], FOURS.in_slot(u) * 16 * TILES)

        @block.gpsimd
        def _(po):
            po.memset(ident[:, :], 0.0).then_inc(s_const, 1)
            po.memset(HALF[:, :], 0.0).then_inc(s_const, 1)
            po.wait_ge(s_const, 2)
            po.affine_select(out=ident[:, :], in_=ident[:, :], compare_op=ALU.not_equal, fill=1.0, base=0,
                             pattern=[[-1, 128]], channel_multiplier=1).then_inc(s_const, 1)
            for k, base in enumerate((0, 64, -64)):
                po.affine_select(out=HALF[:, :], in_=HALF[:, :], compare_op=ALU.not_equal, fill=0.5, base=base,
                                 pattern=[[-1, 128]], channel_multiplier=1).then_inc(s_const, 1)
                po.wait_ge(s_const, 4 + k)
            po.iota(row_no[:, :].rearrange("p (k t) -> p k t", t=TILES), pattern=[[PACK, BLOCKS], [1, TILES]],
                    base=0, channel_multiplier=TILES).then_inc(s_iota, 1)
            po.wait_ge(s_iota, 1)
            po.tensor_copy(slot_rows[:, :, 0].bitcast(I32), row_no[:, :]).then_inc(s_iota, 1)
            po.memset(slot_rows[:, :, 1], 0.0).then_inc(s_iota, 1)
            po.memset(slot_rows[:, :, 3], 0.0).then_inc(s_iota, 1)
            po.wait_ge(s_iota, 4)
            sems.passed[id(po)] = s_passed_pool
            po.wait_ge(s_flag, 2)
            unsorted = po.value_load(flag[0:1, 0:1])
            with po.If(unsorted > 0):
                po.iota(no_i, pattern=[[1, KEYS]], base=0, channel_multiplier=0).then_inc(s_numbered, 1)
                po.iota(own_no, pattern=[[1, PER]], base=0, channel_multiplier=PER).then_inc(s_numbered, 1)
                po.wait_ge(s_ranked, 4)
                with po.Fori(0, BLOCKS) as i:
                    po.dma_start(gat[:, 0, :, :], ea_in.rearrange("(p t) f -> p t f", p=TILE)[:, bass.ds(i * TILES, TILES), :])\
                      .then_inc(s_ea_in, 16)
                    po.tensor_copy(gidx[:, 0, :], rank_i[:, bass.ds(i * TILES, TILES)]).then_inc(s_rank_copy, 1)
                    po.tensor_copy(grow[:, 0, :, :], meta[:, bass.ds(i * TILES, TILES), :]).then_inc(s_rank_copy, 1)
                    sems.wait(po, s_ea_in, i * 16 + 16)
                    sems.wait(po, s_rank_copy, i * 2 + 2)
                    for t in range(TILES):
                        for table, rows in ((EA_S, gat[:, 0, t, :]), (META_S, grow[:, 0, t, :])):
                            po.indirect_dma_start(
                                table, bass.IndirectOffsetOnAxis(ap=gidx[:, 0, t:t + 1], axis=0),
                                rows, None, bounds_check=EDGES + 1, oob_is_err=False).then_inc(s_sorted, 16)
                    sems.wait(po, s_sorted, i * (TILES * 32) + TILES * 32)
            po.end_ifs()
            po.wait_ge(s_idx, 4)

            copies = [0]

            def gather_pass(name, index, source, rows, bound, target, backwards=False):
                base = copies[0]
                skips = name.startswith("ov")

                def body(i, us):
                    pairs = [(half, us[2 * half:2 * half + 2]) for half in (0, 1) if us[2 * half:2 * half + 2]]
                    dst = grow if target is None else gat

                    def lowest(half, slots):
                        n = 4 * i + 2 * half
                        return BLOCKS - n - len(slots) if backwards else n

                    for half, slots in pairs:
                        pair = 2 * i + half
                        slot = slice(2 * half, 2 * half + len(slots))
                        if not (isinstance(i, int) and i == 0):
                            if target is None:
                                sems.wait(po, s_info, pair - 1)
                            else:
                                sems.wait(po, s_gstore[half], store_base(name, half) + i * 16)
                        po.tensor_copy(gidx[:, slot, :].rearrange("p u t -> p (u t)"),
                                       index(lowest(half, slots), len(slots))).then_inc(s_gcopy, 1)
                        if skips:
                            po.memset(dst[:, slot, :, :], 0.0).then_inc(s_gcopy, 1)
                        sems.wait(po, s_gcopy, base + (pair + 1) * (2 if skips else 1))
                        for u in slots:
                            for t in range(TILES):
                                at = t if target is None else 2 * (t % 4) + t // 4
                                po.indirect_dma_start(
                                    dst[:, u, at, :], None, source,
                                    bass.IndirectOffsetOnAxis(ap=gidx[:, u, t:t + 1], axis=0),
                                    bounds_check=bound, oob_is_err=False).then_inc(s_gather[half], 16)
                    for half, slots in pairs:
                        slot = slice(2 * half, 2 * half + len(slots))
                        sems.wait(po, s_gather[half],
                                  gather_base(name, half) + i * (32 * TILES) + 16 * TILES * len(slots))
                        block0 = lowest(half, slots)
                        if target is None:
                            po.tensor_copy(src_info[:, bass.ds(block0 * TILES, len(slots) * TILES), :],
                                           grow[:, slot, :, :].rearrange("p u t c -> p (u t) c")).then_inc(s_info, 1)
                        else:
                            po.dma_start(target[bass.ds(block0, len(slots)), :, :].rearrange("u p c -> p u c"),
                                         gat[:, slot, :, :].rearrange("p u t f -> p u (t f)"))\
                              .then_inc(s_gstore[half], 16)
                in_groups(po, FOURS, body)
                copies[0] += (2 if skips else 1) * PAIRS_OF_BLOCKS

            def all_stored(name):
                for half in (0, 1):
                    po.wait_ge(s_gstore[half], store_base(name, half) + pairs_in(half) * 16)

            gather_pass("xd", lambda k, m: idx_dst[:, bass.ds(k * TILES, m * TILES)], x, D, NODES - 1, XDR)
            all_stored("xd")
            po.wait_ge(s_def, 16)
            base = copies[0]

            def body(i, us):
                for u in us:
                    n = 2 * i + u
                    if not (isinstance(i, int) and i == 0):
                        sems.wait(po, s_scatter[u], i * (16 * TILES))
                    po.tensor_copy(gidx[:, u, :], idx_last[:, bass.ds(n * TILES, TILES)]).then_inc(s_gcopy, 1)
                    po.tensor_copy(grow[:, u, :, :], slot_rows[:, bass.ds(n * TILES, TILES), :]).then_inc(s_gcopy, 1)
                    sems.wait(po, s_gcopy, base + n * 2 + 2)
                    for t in range(TILES):
                        po.indirect_dma_start(
                            SLOTS, bass.IndirectOffsetOnAxis(ap=gidx[:, u, t:t + 1], axis=0),
                            grow[:, u, t, :], None, bounds_check=NODES - 1, oob_is_err=False)\
                          .then_inc(s_scatter[u], 16)
            in_groups(po, PAIRS, body)
            copies[0] += 2 * BLOCKS
            for u in (0, 1):
                po.wait_ge(s_scatter[u], per_slot[u] * 16 * TILES)
            gather_pass("info", lambda k, m: idx_src[:, bass.ds(k * TILES, m * TILES)], SLOTS, 4, NODES - 1, None)
            gather_pass("xs", lambda k, m: idx_src[:, bass.ds(k * TILES, m * TILES)], x, D, NODES - 1, XSR)
            all_stored("xs")
            for t, (P, back) in enumerate(((P_e0, False), (P_e1, True), (P_e4, False), (P_e6, False), (P_e7, False))):
                P.all_done(po)
                gather_pass(f"ov{t}", lambda k, m: src_info[:, bass.ds(k * TILES, m * TILES), 0].bitcast(I32),
                            TAB[t], D, EDGES - 1, OV[t], back)
                all_stored(f"ov{t}")
            P_node2.all_done(po)
            P_node2b.all_done(po)
            base = copies[0]

            def body(i, us):
                for u in us:
                    n = 4 * i + u
                    scattered(po, i, u)
                    po.tensor_copy(gidx[:, u, :], idx_last[:, bass.ds(n * TILES, TILES)]).then_inc(s_gcopy, 1)
                    sems.wait(po, s_gcopy, base + n + 1)
                    P_e8.wait(po, "evrow", n)
                    for t in range(TILES):
                        po.indirect_dma_start(
                            out, bass.IndirectOffsetOnAxis(ap=gidx[:, u, t:t + 1], axis=0),
                            rows_out[:, u, t, :], None, bounds_check=NODES - 1, oob_is_err=False)\
                          .then_inc(s_final[u], 16)
            in_groups(po, FOURS, body)

        def at_bank(P, u, k):
            return bank[8 // P.slots * u + k][:, 0:COLS]

        @block.tensor
        def _(pe):
            mm = nc.tensor.matmul

            def to_features(dst, rows):
                rows = rows.rearrange("p t f -> p (t f)")
                for j in range(4):
                    last = nc.tensor.transpose(dst[:, TILE * j:TILE * j + TILE], rows[:, 128 * j:128 * j + 128],
                                               ident[0:TILE, 0:TILE])
                return last

            def to_rows(dst, value):
                for j in range(4):
                    last = nc.tensor.transpose(dst[0:TILE, 128 * j:128 * j + 128], value[:, TILE * j:TILE * j + TILE],
                                               ident[:, :])
                return last

            def acc(dst, *pairs):
                for k, (w, v) in enumerate(pairs):
                    last = mm(dst, w, v, start=(k == 0), stop=(k == len(pairs) - 1))
                return last

            def one(dst, w, v):
                return mm(dst, w, v, start=True, stop=True)

            def hidden(P, u, buf):
                for h, name in enumerate(("w1a", "w1b")):
                    rows = slice(64 * h, 64 * h + 64)
                    last = one(at_bank(P, u, h), M[name][rows, :], P.B[buf][rows, u, :])
                return last

            def back(P, u, k, wa, wb, a, b, more=False):
                for h, name, buf in ((0, wa, a), (1, wb, b)):
                    rows = slice(64 * h, 64 * h + 64)
                    last = mm(at_bank(P, u, k)[rows, :], M[name][:, rows], P.B[buf][:, u, :], start=not more, stop=True)
                return last

            pe.wait_ge(s_const, 6)
            pe.wait_ge(s_setup, 3)
            one(bank[5][0:1, 0:1], viol[:, :], carry_in[:, :]).then_inc(s_flag, 1)
            pe.wait_ge(s_setup, SETUP_SCAN)
            one(bank[2][0:1, 0:NAT], nat[:, 8, 249:250], ident[0:NAT, 0:NAT])
            one(bank[3][0:1, 0:NAT], nat[:, 9, 249:250], ident[0:NAT, 0:NAT]).then_inc(s_pe_small, 1)
            pe.wait_ge(s_setup, SETUP_CARRY)
            one(bank[4][0:NAT, 0:1], tiny[:, 3, :], ident[0:1, 0:1]).then_inc(s_pe_small, 1)
            pe.wait_ge(s_setup, SETUP_ROWS)
            for q, k in enumerate((1, 3, 5, 10)):
                for par in (0, 1):
                    last = one(bank[q][0:TILE, 128 * par:128 * par + NAT], nat[:, k, TILE * par:TILE * par + TILE],
                               ident[0:NAT, 0:NAT])
            last.then_inc(s_tcol, 1)
            pe.wait_ge(s_ccol, 8)
            pe.wait_ge(s_w, WEIGHT_DMAS * 16)
            one(bank[0][:, 0:64], w2t_sb[:, :], C[0:64, 0:64])
            one(bank[1][:, 0:1], C[:, :], K["b2"]).then_inc(s_pe_small, 1)
            pe.wait_ge(s_dconst, CONST_END)

            def node0(P, with_g):
                def body(i, us):
                    for u in us:
                        P.landed(pe, "ld", i, u)
                        P.free(pe, "evs" if with_g else "out", i, u)
                        hidden(P, u, "in0").then_inc(P.s("hid"), 1)
                    for u in us:
                        P.wait(pe, "relu0", P.at(i, u))
                        P.wait(pe, "relu1", P.at(i, u))
                        mm(at_bank(P, u, 0), C[:, :], P.B["in0"][:, u, :], start=True, stop=False)
                        back(P, u, 0, "w2ca", "w2cb", "a", "b", more=True).then_inc(P.s("y"), 1)
                    for u in us:
                        variance(P, i, u, 1)
                    if with_g:
                        for u in us:
                            P.wait(pe, "out", P.at(i, u))
                            back(P, u, 0, "w2a", "w2b", "a", "b").then_inc(P.s("g"), 1)
                in_groups(pe, P, body)
                P.all_done(pe)

            def variance(P, i, u, k, sq="sq", var="var", lnv="lnv", buf="c"):
                P.free(pe, lnv, i, u)
                P.wait(pe, sq, P.at(i, u))
                one(at_bank(P, u, k), J[:, :], P.B[buf][:, u, :]).then_inc(P.s(var), 1)

            def rows_of(P, i, u, k, buf="o0", done="out"):
                P.free(pe, "evrow", i, u)
                P.wait(pe, done, P.at(i, u))
                to_rows(bank[8 // P.slots * u + k], P.B[buf][:, u, :]).then_inc(P.s("row"), 1)

            node0(P_node0, False)

            pe.wait_ge(s_info, PAIRS_OF_BLOCKS)
            for q, k in enumerate((1, 2)):
                for par in (0, 1):
                    last = one(bank[q][0:NAT, 128 * par:128 * par + TILE], src_info[:, par::2, k],
                               ident[0:TILE, 0:TILE])
            last.then_inc(s_pe_small, 1)
            pe.wait_ge(s_info, INFO_ROWS)

            def body(i, us):
                for u in us:
                    P_e0.landed(pe, "ld", i, u)
                    P_e0.free(pe, "evrow", i, u)
                    P_e0.free(pe, "out", i, u)
                    to_features(at_bank(P_e0, u, 0), rows_in[0][:, u])
                    to_features(at_bank(P_e0, u, 1), rows_in[1][:, u]).then_inc(P_e0.s("tr"), 1)
                for u in us:
                    P_e0.wait(pe, "vec", P_e0.at(i, u))
                    hidden(P_e0, u, "b").then_inc(P_e0.s("hid"), 1)
                for u in us:
                    P_e0.wait(pe, "relu0", P_e0.at(i, u))
                    P_e0.wait(pe, "relu1", P_e0.at(i, u))
                    back(P_e0, u, 0, "w2a", "w2b", "c", "d").then_inc(P_e0.s("g"), 1)
                for u in us:
                    rows_of(P_e0, i, u, 1)
            in_groups(pe, P_e0, body)
            P_e0.all_done(pe)

            node0(P_node0e, True)

            def body(i, us):
                for u in us:
                    P_e1.landed(pe, "ld", i, u)
                    P_e1.free(pe, "lnv", i, u)
                    to_features(at_bank(P_e1, u, 0), rows_in[0][:, u]).then_inc(P_e1.s("tr"), 1)
                for u in us:
                    P_e1.free(pe, "evrow", i, u)
                    P_e1.wait(pe, "vec", P_e1.at(i, u))
                    one(at_bank(P_e1, u, 1), C[:, :], P_e1.B["c"][:, u, :]).then_inc(P_e1.s("y"), 1)
                for u in us:
                    variance(P_e1, i, u, 0, buf="d")
                for u in us:
                    rows_of(P_e1, i, u, 1)
            in_groups(pe, P_e1, body)
            P_e1.all_done(pe)

            def body(i, us):
                for u in us:
                    P_e2.landed(pe, "ld", i, u)
                    P_e2.free(pe, "evf", i, u)
                    P_e2.free(pe, "evc", i, u)
                    to_features(at_bank(P_e2, u, 0), rows_in[0][:, u])
                    to_features(at_bank(P_e2, u, 1), rows_in[1][:, u]).then_inc(P_e2.s("tr"), 1)
                for u in us:
                    n = P_e2.at(i, u)
                    P_e2.wait(pe, "evs", n)
                    P_e2.wait(pe, "msg", n)
                    P_e2.wait(pe, "scan", n)
                    for k, part in ((0, "f"), (1, "c")):
                        last = acc(at_bank(P_e2, u, k), (M["src" + part], P_e2.B["o3"][:, u, :]), (M["dst" + part], P_e2.B["o0"][:, u, :]),
                                   (M["nbr" + part], P_e2.B["a"][:, u, :]))
                    last.then_inc(P_e2.s("t"), 1)
            in_groups(pe, P_e2, body)
            P_e2.all_done(pe)

            def halves_mean(want, k0, k1):
                pe.wait_ge(s_dv_small, want)
                one(bank[0][:, 0:2 * (k1 - k0)], HALF[:, :], mom[:, k0:k1, :].rearrange("p k c -> p (k c)"))\
                    .then_inc(s_pe_small, 1)

            halves_mean(STATS1, 0, 2)
            P_e3.all_done(pe)
            halves_mean(STATS2, 0, 1)
            pe.wait_ge(s_dv_small, STATS2B)
            one(bank[1][:, 0:1], C[:, :], K["t2"]).then_inc(s_pe_small, 1)

            def plain_ln(P, last=None, first=None):
                def body(i, us):
                    if first:
                        for u in us:
                            first(i, u)
                    for u in us:
                        P.free(pe, {"rows": "evrow", "h": "bnf", None: "out"}[last], i, u)
                        P.wait(pe, "vec", P.at(i, u))
                        one(at_bank(P, u, 0), C[:, :], P.B["c"][:, u, :]).then_inc(P.s("y"), 1)
                    for u in us:
                        variance(P, i, u, 1, buf="d")
                    for u in us:
                        if last == "rows":
                            rows_of(P, i, u, 0)
                        if last == "h":
                            P.wait(pe, "out", P.at(i, u))
                            one(at_bank(P, u, 0), M["wl2"], P.B["o0"][:, u, :]).then_inc(P.s("h"), 1)
                in_groups(pe, P, body)
                P.all_done(pe)

            plain_ln(P_e4, "rows")
            plain_ln(P_node1, "h")
            plain_ln(P_node1e)

            def body(i, us):
                for u in us:
                    P_e5.landed(pe, "ld", i, u)
                    P_e5.free(pe, "evs", i, u)
                    to_features(at_bank(P_e5, u, 0), rows_in[0][:, u]).then_inc(P_e5.s("tr"), 1)
                for u in us:
                    P_e5.free(pe, "mask", i, u)
                    P_e5.wait(pe, "vec", P_e5.at(i, u))
                    one(at_bank(P_e5, u, 0), M["wl2"], P_e5.B["b"][:, u, :])
                    one(at_bank(P_e5, u, 1), M["wl2"], P_e5.B["in2"][:, u, :]).then_inc(P_e5.s("h"), 1)
            in_groups(pe, P_e5, body)
            P_e5.all_done(pe)
            halves_mean(STATS3, 0, 3)

            plain_ln(P_e6, "rows")

            def first_h(P):
                def first(i, u):
                    P.landed(pe, "ld", i, u)
                    P.free(pe, "out", i, u)
                    one(at_bank(P, u, 0), M["wl2"], P.B["in0"][:, u, :]).then_inc(P.s("h"), 1)
                return first
            plain_ln(P_e6s, first=first_h(P_e6s))

            def node2(P):
                def body(i, us):
                    for u in us:
                        P.landed(pe, "ld", i, u)
                        P.free(pe, "evrow", i, u)
                        one(at_bank(P, u, 0), M["wl2"], P.B["in0"][:, u, :]).then_inc(P.s("h"), 1)
                    for u in us:
                        P.wait(pe, "vec", P.at(i, u))
                        one(at_bank(P, u, 1), C[:, :], P.B["b"][:, u, :]).then_inc(P.s("y"), 1)
                    for u in us:
                        variance(P, i, u, 0, buf="d")
                    for u in us:
                        P.wait(pe, "out", P.at(i, u))
                        one(at_bank(P, u, 0), M["w31"], P.B["o0"][:, u, :]).then_inc(P.s("hid"), 1)
                    for u in us:
                        P.wait(pe, "relu0", P.at(i, u))
                        one(at_bank(P, u, 1), M["w32"], P.B["a"][:, u, :]).then_inc(P.s("g"), 1)
                    for u in us:
                        P.wait(pe, "add", P.at(i, u))
                        one(at_bank(P, u, 0), C[:, :], P.B["o0"][:, u, :]).then_inc(P.s("y2"), 1)
                    for u in us:
                        variance(P, i, u, 1, "sq2", "var2", "lnv2", "g")
                    for u in us:
                        rows_of(P, i, u, 0, "o1", "out2")
                in_groups(pe, P, body)
                P.all_done(pe)
            node2(P_node2)

            P = P_e7

            def body(i, us):
                for u in us:
                    n = P.at(i, u)
                    P.landed(pe, "ld", i, u)
                    P.free(pe, "out", i, u)
                    to_features(at_bank(P, u, 0), rows_in[0][:, u]).then_inc(P.s("tr"), 1)
                for u in us:
                    n = P.at(i, u)
                    P.free(pe, "evrow", i, u)
                    P.wait(pe, "msg", n, 1 + 1)
                    one(at_bank(P, u, 1), M["w31"], P.B["a"][:, u, :])
                    one(at_bank(P, u, 0), M["w31"], P.B["in1"][:, u, :]).then_inc(P.s("hid"), 1)
                for u in us:
                    n = P.at(i, u)
                    P.wait(pe, "relu0", n)
                    one(at_bank(P, u, 1), M["w32"], P.B["d"][:, u, :]).then_inc(P.s("g"), 1)
                for u in us:
                    n = P.at(i, u)
                    P.wait(pe, "relu1", n)
                    one(at_bank(P, u, 0), M["w32"], P.B["h"][:, u, :]).then_inc(P.s("h"), 1)
                for u in us:
                    P.wait(pe, "act", P.at(i, u))
                    rows_of(P, i, u, 1)
            in_groups(pe, P, body)
            P.all_done(pe)

            node2(P_node2b)
            P = P_e8

            def body(i, us):
                for u in us:
                    P.landed(pe, "ld", i, u)
                    P.free(pe, "lnv", i, u)
                    to_features(at_bank(P, u, 0), rows_in[0][:, u]).then_inc(P.s("tr"), 1)
                for u in us:
                    P.free(pe, "evrow", i, u)
                    P.wait(pe, "add", P.at(i, u))
                    one(at_bank(P, u, 1), C[:, :], P.B["f"][:, u, :]).then_inc(P.s("y"), 1)
                for u in us:
                    variance(P, i, u, 0, buf="d")
                for u in us:
                    rows_of(P, i, u, 1)
            in_groups(pe, P, body)

        @block.scalar
        def _(ac):
            act = nc.scalar.activation

            def square(P, i, u, k, bias, buf="c", y="y", sq="sq", var="var"):
                P.free(ac, var, i, u)
                P.wait(ac, y, P.at(i, u))
                act(P.B[buf][:, u, :], at_bank(P, u, k), ACT.Square, bias=bias).then_inc(P.s(sq), 1)

            def rstd(P, i, u, k, buf="g", var="var", lnv="lnv", name="rstd", read="out"):
                P.free(ac, read, i, u)
                P.wait(ac, var, P.at(i, u))
                act(P.B[buf][:, u, :], at_bank(P, u, k), ACT.Ln, bias=K["eps"]).then_inc(P.s(lnv), 1)
                P.wait(ac, lnv, P.at(i, u))
                act(P.B[buf][:, u, :], P.B[buf][:, u, :], ACT.Exp, scale=-0.5).then_inc(P.s(name), 1)

            def small_rstd(want, col):
                ac.wait_ge(s_dv_small, want)
                act(col, col, ACT.Ln, bias=K["eps"]).then_inc(s_ac_small, 1)
                small[0] += 2
                ac.wait_ge(s_ac_small, small[0] - 1)
                act(col, col, ACT.Exp, scale=-0.5).then_inc(s_ac_small, 1)

            small = [0]

            def rows_evac(P, i, u, k, stored=True):
                if stored:
                    P.stored(ac, "st", i, u)
                P.wait(ac, "row", P.at(i, u))
                act(rows_out[:, u, :, :].rearrange("p (h j) f -> p j h f", h=2),
                    bank[8 // P.slots * u + k][0:TILE, :].rearrange("p (j h f) -> p j h f", j=4, h=2), ACT.Copy)\
                    .then_inc(P.s("evrow"), 1)

            def sigmoid_log(P, i, u, out, z):
                n = P.at(i, u)
                P.free(ac, "sig", i, u)
                P.wait(ac, "nabs", n)
                act(out, z, ACT.Exp).then_inc(P.s("lsig"), 1)
                P.wait(ac, "lsig", n, 1)
                act(out, out, ACT.Ln, bias=1.0).then_inc(P.s("lsig"), 1)

            def sigmoid_end(P, i, u, out, arg, used):
                P.free(ac, used, i, u)
                P.wait(ac, "arg", P.at(i, u))
                act(out, arg, ACT.Exp).then_inc(P.s("sig"), 1)

            def node0(P, with_g):
                def body(i, us):
                    for u in us:
                        P.free(ac, "y", i, u)
                        if with_g:
                            P.free(ac, "g", i, u)
                        P.wait(ac, "hid", P.at(i, u))
                        act(P.B["a"][:, u, :], at_bank(P, u, 0), ACT.Relu, bias=K["b1"]).then_inc(P.s("relu0"), 1)
                    for u in us:
                        square(P, i, u, 0, K["cb2"])
                    for u in us:
                        rstd(P, i, u, 1)
                    if with_g:
                        for u in us:
                            P.stored(ac, "st", i, u)
                            P.wait(ac, "g", P.at(i, u))
                            act(P.B["o1"][:, u, :], at_bank(P, u, 0), ACT.Copy).then_inc(P.s("evs"), 1)
                in_groups(ac, P, body)
                P.all_done(ac)

            ac.preload_act_table_set("natural_log_exp_and_others")
            ac.wait_ge(s_setup, SETUP_CARRY + 2)
            act(nat[:, 10, :], nat[:, 7, :], ACT.Ln, bias=1.0).then_inc(s_setup, 1)
            ac.wait_ge(s_setup, SETUP_CARRY + 3)
            act(nat[:, 10, :], nat[:, 10, :], ACT.Exp, scale=-0.5).then_inc(s_setup, 1)
            ac.wait_ge(s_dconst, CONST_END)
            node0(P_node0, False)

            def body(i, us):
                for u in us:
                    P_e0.stored(ac, "st", i, u)
                    P_e0.wait(ac, "tr", P_e0.at(i, u))
                    act(P_e0.B["o1"][:, u, :], at_bank(P_e0, u, 0), ACT.Copy).then_inc(P_e0.s("evs"), 1)
                for u in us:
                    P_e0.free(ac, "g", i, u)
                    P_e0.wait(ac, "hid", P_e0.at(i, u))
                    act(P_e0.B["c"][:, u, :], at_bank(P_e0, u, 0), ACT.Relu, bias=K["b1"]).then_inc(P_e0.s("relu0"), 1)
                for u in us:
                    rows_evac(P_e0, i, u, 1)
            in_groups(ac, P_e0, body)
            P_e0.all_done(ac)

            node0(P_node0e, True)

            def body(i, us):
                for u in us:
                    square(P_e1, i, u, 1, K["cb2"], "d")
                for u in us:
                    rstd(P_e1, i, u, 0)
                for u in us:
                    rows_evac(P_e1, i, u, 1)
            in_groups(ac, P_e1, body)
            P_e1.all_done(ac)

            def body(i, us):
                for u in us:
                    P_e2.free(ac, "t", i, u)
                    P_e2.wait(ac, "tr", P_e2.at(i, u))
                    act(P_e2.B["a"][:, u, :], at_bank(P_e2, u, 1), ACT.Copy).then_inc(P_e2.s("evs"), 1)
                for u in us:
                    P_e2.stored(ac, "st", i, u)
                    P_e2.wait(ac, "t", P_e2.at(i, u))
                    act(P_e2.B["o1"][:, u, :], at_bank(P_e2, u, 0), ACT.Identity, bias=K["bf"]).then_inc(P_e2.s("evf"), 1)
                    act(P_e2.B["o2"][:, u, :], at_bank(P_e2, u, 1), ACT.Identity, bias=K["bc"]).then_inc(P_e2.s("evc"), 1)
            in_groups(ac, P_e2, body)
            P_e2.all_done(ac)
            small_rstd(STATS1 + 3, K["tmp1"])
            small_rstd(STATS1 + 8, K["tmp1"])
            ac.wait_ge(s_dv_small, STATS1B)

            def body(i, us):
                for u in us:
                    n = P_e3.at(i, u)
                    P_e3.landed(ac, "ld", i, u)
                    P_e3.free(ac, "vec", i, u)
                    act(P_e3.B["b"][:, u, :], P_e3.B["in1"][:, u, :], ACT.Abs, scale=K["s1c"], bias=K["t1c"]).then_inc(P_e3.s("act"), 1)
                    P_e3.wait(ac, "act", n, 1)
                    act(P_e3.B["c"][:, u, :], P_e3.B["b"][:, u, :], ACT.Exp, scale=-1.0).then_inc(P_e3.s("act"), 1)
                    P_e3.wait(ac, "act", n, 2)
                    act(P_e3.B["d"][:, u, :], P_e3.B["c"][:, u, :], ACT.Ln, bias=1.0).then_inc(P_e3.s("act"), 1)
                    sigmoid_log(P_e3, i, u, P_e3.B["a"][:, u, :], P_e3.B["g2"][:, u, :])
                for u in us:
                    sigmoid_end(P_e3, i, u, P_e3.B["in4"][:, u, :], P_e3.B["in3"][:, u, :], "vec")
            in_groups(ac, P_e3, body)
            P_e3.all_done(ac)
            small_rstd(STATS2 + 3, K["tmp1"])
            ac.wait_ge(s_dv_small, STATS2C)

            def soft(P, source, ready, rows=None):
                def body(i, us):
                    for u in us:
                        n = P.at(i, u)
                        ready(i, u)
                        P.free(ac, "vec", i, u)
                        act(P.B["a"][:, u, :], P.B[source][:, u, :], ACT.Abs, bias=K["t2"]).then_inc(P.s("act"), 1)
                        P.wait(ac, "act", n, 1)
                        act(P.B["a"][:, u, :], P.B["a"][:, u, :], ACT.Exp, scale=-1.0).then_inc(P.s("act"), 1)
                        P.wait(ac, "act", n, 2)
                        act(P.B["a"][:, u, :], P.B["a"][:, u, :], ACT.Ln, bias=1.0).then_inc(P.s("act"), 1)
                    for u in us:
                        square(P, i, u, 0, K["ct2"], "d")
                    for u in us:
                        rstd(P, i, u, 1)
                    if rows:
                        for u in us:
                            rows_evac(P, i, u, 0)
                in_groups(ac, P, body)
                P.all_done(ac)
            soft(P_e4, "e", lambda i, u: P_e4.wait(ac, "msg", P_e4.at(i, u)), True)
            soft(P_node1, "in0", lambda i, u: P_node1.landed(ac, "ld", i, u))
            soft(P_node1e, "in0", lambda i, u: P_node1e.landed(ac, "ld", i, u))

            def body(i, us):
                for u in us:
                    P_e5.stored(ac, "st", i, u)
                    P_e5.wait(ac, "h", P_e5.at(i, u))
                    act(P_e5.B["o1"][:, u, :], at_bank(P_e5, u, 0), ACT.Copy).then_inc(P_e5.s("evs"), 1)
            in_groups(ac, P_e5, body)
            P_e5.all_done(ac)
            small_rstd(STATS3 + 5, K["tmp1"])
            ac.wait_ge(s_dv_small, STATS3B)

            def relu_bn(P, source, ready, rows=None):
                def body(i, us):
                    for u in us:
                        ready(i, u)
                        P.free(ac, "vec", i, u)
                        act(P.B["a"][:, u, :], source(u), ACT.Relu, scale=K["s3"], bias=K["t3"]).then_inc(P.s("act"), 1)
                    for u in us:
                        square(P, i, u, 0, 0.0, "d")
                    for u in us:
                        rstd(P, i, u, 1)
                    if rows:
                        for u in us:
                            rows_evac(P, i, u, 0)
                in_groups(ac, P, body)
                P.all_done(ac)
            relu_bn(P_e6, lambda u: P_e6.B["in0"][:, u, :], lambda i, u: P_e6.landed(ac, "ld", i, u), True)
            relu_bn(P_e6s, lambda u: at_bank(P_e6s, u, 0), lambda i, u: P_e6s.wait(ac, "h", P_e6s.at(i, u)))

            def node2(P):
                def body(i, us):
                    for u in us:
                        P.wait(ac, "h", P.at(i, u))
                        P.free(ac, "vec", i, u)
                        act(P.B["b"][:, u, :], at_bank(P, u, 0), ACT.Relu, scale=K["s3"], bias=K["t3"]).then_inc(P.s("act"), 1)
                    for u in us:
                        square(P, i, u, 1, 0.0, "d")
                    for u in us:
                        rstd(P, i, u, 0, "h")
                    for u in us:
                        sigmoid_log(P, i, u, P.B["in1"][:, u, :], P.B["in1"][:, u, :])
                    for u in us:
                        sigmoid_end(P, i, u, P.B["e"][:, u, :], P.B["e"][:, u, :], "add")
                    for u in us:
                        square(P, i, u, 0, 0.0, "g", "y2", "sq2", "var2")
                    for u in us:
                        rstd(P, i, u, 1, "c", "var2", "lnv2", "rstd2", "out2")
                    for u in us:
                        rows_evac(P, i, u, 0)
                in_groups(ac, P, body)
                P.all_done(ac)
            node2(P_node2)

            P = P_e7

            def body(i, us):
                for u in us:
                    n = P.at(i, u)
                    P.wait(ac, "hid", n)
                    P.free(ac, "vec", i, u)
                    act(P.B["b"][:, u, :], at_bank(P, u, 1), ACT.Identity, bias=K["b31"]).then_inc(P.s("evs"), 1)
                    P.stored(ac, "st", i, u)
                    act(P.B["c"][:, u, :], at_bank(P, u, 0), ACT.Identity, bias=K["b31"]).then_inc(P.s("evd"), 1)
                    P.free(ac, "g", i, u)
                    act(P.B["d"][:, u, :], at_bank(P, u, 1), ACT.Relu, bias=K["b31"]).then_inc(P.s("relu0"), 1)
                for u in us:
                    P.wait(ac, "g", P.at(i, u))
                    act(P.B["o1"][:, u, :], at_bank(P, u, 1), ACT.Identity, bias=K["b32"]).then_inc(P.s("act"), 1)
                for u in us:
                    rows_evac(P, i, u, 1)
            in_groups(ac, P, body)
            P.all_done(ac)

            node2(P_node2b)
            P = P_e8

            def body(i, us):
                for u in us:
                    sigmoid_log(P, i, u, P.B["o1"][:, u, :], P.B["o1"][:, u, :])
                for u in us:
                    sigmoid_end(P, i, u, P.B["in4"][:, u, :], P.B["in3"][:, u, :], "add")
                for u in us:
                    square(P, i, u, 1, 0.0, "d")
                for u in us:
                    rstd(P, i, u, 0, "g2")
                for u in us:
                    scattered(ac, i, u)
                    rows_evac(P, i, u, 1, stored=False)
            in_groups(ac, P, body)

        @block.vector
        def _(dv):
            v = nc.vector
            marks = {}
            count = [0]

            def const(ins):
                ins.then_inc(s_dconst, 1)
                count[0] += 1
                dv.wait_ge(s_dconst, count[0])

            const(v.memset(mats[:, :, :], 0.0))
            const(v.memset(J[:, :], 0.0))
            v.memset(J[0:64, 0:64], 1.0 / D)
            v.memset(default[:, :, 0].bitcast(I32), SKIP)
            v.memset(default[:, :, 3], 0.0)
            const(v.memset(J[64:128, 64:128], 1.0 / D))
            v.memset(pad[:, :], -1.0)
            v.memset(carry_in[:, :], 1.0)
            const(v.memset(default[:, :, 1:3], 1.0))
            dv.wait_ge(s_const, 6)
            const(v.tensor_tensor(C[:, :], ident[:, :], J[:, :], ALU.subtract))
            v.memset(K["eps"], EPS)
            const(v.memset(carry[:, :], 0.0))

            def sort_edges():
                done = [0]

                def by_own(ins):
                    ins.then_inc(s_rank, 1)
                    done[0] += 1
                    dv.wait_ge(s_rank, done[0])

                dv.wait_ge(s_own, 48)
                dv.wait_ge(s_numbered, 2)
                by_own(v.tensor_copy(own_f[:, 0:2, :], own_i))
                by_own(v.tensor_copy(idx_f[:, :], own_no))
                v.memset(meta[:, :, 3], 0.0)
                by_own(v.memset(rank[:, :], 1.0))
                by_own(v.tensor_copy(no_f, no_i))
                for c in range(EDGES // KEYS):
                    dv.wait_ge(s_keys, 16 * c + 16)
                    by_own(v.tensor_copy(key_f, key_i))
                    dv.sem_inc(s_keys_used, 1)
                    base = done[0]
                    with dv.Fori(0, PER) as t:
                        def looped(k, ins):
                            ins.then_inc(s_rank, 1)
                            dv.wait_ge(s_rank, t * 6 + (base + k))
                        looped(1, v.tensor_copy(key_col[:, :], own_f[:, 0, bass.ds(t, 1)]))
                        looped(2, v.tensor_copy(edge_col[:, :], idx_f[:, bass.ds(t, 1)]))
                        looped(3, v.tensor_scalar(work, no_f, edge_col[:, 0:1], None, ALU.is_lt))
                        looped(4, v.scalar_tensor_tensor(out=work, in0=key_f, scalar=key_col[:, 0:1], in1=work,
                                                         op0=ALU.is_equal, op1=ALU.mult))
                        looped(5, v.scalar_tensor_tensor(out=work, in0=key_f, scalar=key_col[:, 0:1], in1=work,
                                                         op0=ALU.is_lt, op1=ALU.add))
                        looped(6, v.reduce_sum(part[:, bass.ds(t, 1)], work, mybir.AxisListType.X))
                    done[0] += PER * 6
                    by_own(v.tensor_tensor(rank[:, :], rank[:, :], part[:, :], ALU.add))
                    by_own(v.tensor_scalar(idx_f[:, :], idx_f[:, :], -float(KEYS), None, ALU.add))
                    by_own(v.memset(part[:, :], 0.0))
                assert done[0] == SORT_RANKED, done
                v.tensor_copy(rank_i[:, :], rank[:, :]).then_inc(s_ranked, 1)
                for k in range(3):
                    v.tensor_copy(meta[:, :, k], own_f[:, k, :]).then_inc(s_ranked, 1)
                dv.wait_ge(s_ranked, 4)
                dv.wait_ge(s_meta, 48)
                for k in range(3):
                    by_own(v.tensor_copy(nat[:, k, :], meta_in[:, k, 0::4]))
                by_own(v.tensor_copy(nat[:, 3, :], meta_in[:, 1, 1::4]))
                by_own(v.tensor_copy(nat[:, 11, :], meta_in[:, 1, 2::4]))

            steps = [0]

            def step(ins):
                ins.then_inc(s_setup, 1)
                steps[0] += 1
                dv.wait_ge(s_setup, steps[0])

            dv.wait_ge(s_nat, 5 * 16)
            step(v.tensor_copy(nat[:, 0:4, :], nat_i[:, :, :]))
            step(v.tensor_tensor(nat[:, 4, :], nat[:, 1, :], nat[:, 2, :], ALU.is_gt))
            step(v.reduce_sum(viol[:, :], nat[:, 4, :], mybir.AxisListType.X))
            dv.wait_ge(s_flag, 1)
            v.tensor_scalar(flag[:, :], bank[5][0:1, 0:1], 1.0, None, ALU.subtract).then_inc(s_flag, 1)
            dv.wait_ge(s_flag, 2)
            unsorted = dv.value_load(flag[0:1, 0:1])
            with dv.If(unsorted > 0):
                sort_edges()
            dv.end_ifs()
            dv.wait_ge(s_setup, 3)
            step(v.tensor_tensor(nat[:, 4, :], nat[:, 1, :], nat[:, 0, :], ALU.is_equal))
            step(v.tensor_tensor(nat[:, 5, :], nat[:, 1, :], nat[:, 2, :], ALU.not_equal))
            step(v.tensor_tensor(nat[:, 6, :], nat[:, 1, :], nat[:, 2, :], ALU.is_equal))
            step(v.memset(nat[:, 7, :], 1.0))
            step(v.tensor_tensor_scan(out=nat[:, 8, :], data0=nat[:, 4, :], data1=nat[:, 7, :], initial=0.0,
                                      op0=ALU.mult, op1=ALU.add))
            step(v.memset(nat[:, 7, :], 0.0))
            step(v.tensor_tensor_scan(out=nat[:, 9, :], data0=nat[:, 4, :], data1=nat[:, 7, :], initial=1.0,
                                      op0=ALU.mult, op1=ALU.add))
            assert steps[0] == SETUP_SCAN
            dv.wait_ge(s_pe_small, 1)
            step(v.tensor_copy(tiny[:, 0, :], bank[2][0:1, 0:NAT]))
            step(v.tensor_copy(tiny[:, 1, :], bank[3][0:1, 0:NAT]))
            step(v.tensor_tensor_scan(out=tiny[:, 2, :], data0=tiny[:, 1, :], data1=tiny[:, 0, :], initial=0.0,
                                      op0=ALU.mult, op1=ALU.add))
            step(v.memset(tiny[:, 3, 0:1], 0.0))
            step(v.tensor_copy(tiny[:, 3, 1:NAT], tiny[:, 2, 0:NAT - 1]))
            assert steps[0] == SETUP_CARRY
            dv.wait_ge(s_pe_small, 2)
            step(v.tensor_copy(carry_in[:, :], bank[4][0:NAT, 0:1]))
            step(v.scalar_tensor_tensor(out=nat[:, 7, :], in0=nat[:, 9, :], scalar=carry_in[:, 0:1],
                                        in1=nat[:, 8, :], op0=ALU.mult, op1=ALU.add))
            steps[0] += 2
            dv.wait_ge(s_setup, steps[0])
            step(v.tensor_tensor(nat[:, 0, :], nat[:, 10, :], nat[:, 10, :], ALU.mult))
            step(v.scalar_tensor_tensor(out=nat[:, 0, :], in0=nat[:, 7, :], scalar=1.0, in1=nat[:, 0, :],
                                        op0=ALU.add, op1=ALU.mult))
            step(v.tensor_scalar(nat[:, 0, :], nat[:, 0, :], -0.5, 1.5, ALU.mult, ALU.add))
            step(v.tensor_tensor(nat[:, 10, :], nat[:, 10, :], nat[:, 0, :], ALU.mult))
            assert steps[0] == SETUP_ROWS
            dv.wait_ge(s_tcol, 1)
            ccol = [0]

            def cstep(ins, wait=False):
                ins.then_inc(s_ccol, 1)
                ccol[0] += 1
                if wait:
                    dv.wait_ge(s_ccol, ccol[0])

            for q in range(4):
                for par in (0, 1):
                    cstep(v.tensor_copy(col[:, q, par::2], bank[q][0:TILE, 128 * par:128 * par + NAT]))
            dv.wait_ge(s_ccol, 8)
            v.tensor_copy(idx_dst[:, :], col[:, 0, :]).then_inc(s_idx, 1)
            v.tensor_copy(idx_src[:, :], col[:, 1, :]).then_inc(s_idx, 1)
            v.tensor_copy(slot_rows[:, :, 2], col[:, 3, :]).then_inc(s_idx, 1)
            cstep(v.tensor_scalar(idx_f[:, :], col[:, 2, :], -float(SKIP), float(SKIP), ALU.mult, ALU.add), True)
            cstep(v.tensor_tensor(idx_f[:, :], idx_f[:, :], col[:, 0, :], ALU.add), True)
            v.tensor_copy(idx_last[:, :], idx_f[:, :]).then_inc(s_idx, 1)
            dv.wait_ge(s_pe_small, 3)
            v.tensor_copy(M["w2ca"][:, 0:64], bank[0][:, 0:64])
            v.tensor_copy(M["w2cb"][:, 64:128], bank[0][:, 0:64])
            const(v.tensor_copy(K["cb2"], bank[1][:, 0:1]))
            assert count[0] == CONST_END

            def own(P, step, n, ins, part=None):
                ins.then_inc(P.s(step), 1)
                P.wait(dv, step, n, part)

            def normed(P, i, u, ky, bias, out="o0", stored=True, rs="g"):
                P.wait(dv, "rstd", P.at(i, u))
                if stored:
                    P.stored(dv, "st", i, u)
                if bias is None:
                    ins = v.tensor_tensor(P.B[out][:, u, :], at_bank(P, u, ky), P.B[rs][:, u, :], ALU.mult)
                else:
                    ins = v.scalar_tensor_tensor(out=P.B[out][:, u, :], in0=at_bank(P, u, ky), scalar=bias,
                                                 in1=P.B[rs][:, u, :], op0=ALU.add, op1=ALU.mult)
                ins.then_inc(P.s("out"), 1)

            def neg_abs(P, i, u, out, z):
                P.free(dv, "lsig", i, u)
                v.scalar_tensor_tensor(out=out, in0=z, scalar=-1.0, in1=z, op0=ALU.mult, op1=ALU.min)\
                 .then_inc(P.s("nabs"), 1)

            def sigmoid_arg(P, i, u, out, z, log):
                P.free(dv, "sig", i, u)
                P.wait(dv, "lsig", P.at(i, u))
                v.scalar_tensor_tensor(out=out, in0=z, scalar=0.0, in1=log, op0=ALU.min, op1=ALU.subtract)\
                 .then_inc(P.s("arg"), 1)

            def relu_hidden(P, i, u, k, buf):
                v.tensor_scalar(P.B[buf][:, u, :], at_bank(P, u, k), K["b1"], 0.0, ALU.add, ALU.max).then_inc(P.s("relu1"), 1)

            def node0(P, with_g):
                def body(i, us):
                    for u in us:
                        P.free(dv, "y", i, u)
                        if with_g:
                            P.free(dv, "g", i, u)
                        P.wait(dv, "hid", P.at(i, u))
                        relu_hidden(P, i, u, 1, "b")
                    for u in us:
                        normed(P, i, u, 0, K["cb2"])
                in_groups(dv, P, body)
                P.all_done(dv)

            node0(P_node0, False)

            dv.wait_ge(s_info, PAIRS_OF_BLOCKS)
            dv.wait_ge(s_pe_small, 4)
            dv.wait_ge(s_rows, 12 * 16)
            for q in (0, 1):
                for par in (0, 1):
                    v.tensor_copy(nat[:, q, TILE * par:TILE * par + TILE],
                                  bank[q][0:NAT, 128 * par:128 * par + TILE]).then_inc(s_info, 1)
            dv.wait_ge(s_info, PAIRS_OF_BLOCKS + 4)
            v.tensor_tensor(nat[:, 2, :], nat[:, 1, :], nat[:, 11, :], ALU.mult).then_inc(s_info, 1)

            def scan(P, n, u, out, same, msg):
                def part(k, ins):
                    own(P, "scan", n, ins, k)
                for h in (0, 1):
                    lo, hi = slice(64 * h, 64 * h + 64), slice(64 - 64 * h, 128 - 64 * h)
                    part(2 * h + 1, v.tensor_tensor_scan(out=out[lo, u, :], data0=same[lo, u, :], data1=msg[lo, u, :],
                                                         initial=carry[lo, 0:1], op0=ALU.mult, op1=ALU.add))
                    part(2 * h + 2, v.tensor_copy(carry[hi, 0:1], out[lo, u, COLS - 1:COLS]))

            def tt(out, a, b, op):
                return v.tensor_tensor(out, a, b, op)

            def body(i, us):
                for u in us:
                    n = P_e0.at(i, u)
                    P_e0.landed(dv, "ld", i, u)
                    P_e0.stored(dv, "st", i, u)
                    P_e0.wait(dv, "tr", n)
                    own(P_e0, "evd", n, v.tensor_copy(P_e0.B["o2"][:, u, :], at_bank(P_e0, u, 1)))
                    P_e0.wait(dv, "evs", n)
                    own(P_e0, "msg", n, tt(P_e0.B["a"][:, u, :], P_e0.B["o1"][:, u, :], P_e0.B["wts"][:, u, :], ALU.mult))
                    scan(P_e0, n, u, P_e0.B["e"], P_e0.B["same"], P_e0.B["a"])
                    P_e0.free(dv, "hid", i, u)
                    own(P_e0, "vec", n, tt(P_e0.B["f"][:, u, :], P_e0.B["o2"][:, u, :], P_e0.B["dinv"][:, u, :], ALU.mult), 1)
                    own(P_e0, "vec", n, tt(P_e0.B["g"][:, u, :], P_e0.B["f"][:, u, :], P_e0.B["e"][:, u, :], ALU.add), 2)
                    tt(P_e0.B["b"][:, u, :], P_e0.B["g"][:, u, :], P_e0.B["dinv"][:, u, :], ALU.mult).then_inc(P_e0.s("vec"), 1)
                for u in us:
                    P_e0.free(dv, "g", i, u)
                    P_e0.wait(dv, "hid", P_e0.at(i, u))
                    relu_hidden(P_e0, i, u, 1, "d")
                for u in us:
                    P_e0.wait(dv, "g", P_e0.at(i, u))
                    tt(P_e0.B["o0"][:, u, :], at_bank(P_e0, u, 0), P_e0.B["dinv"][:, u, :], ALU.mult).then_inc(P_e0.s("out"), 1)
            in_groups(dv, P_e0, body)
            P_e0.all_done(dv)

            def clear_carry(k):
                v.memset(carry[:, :], 0.0).then_inc(s_dconst, 1)
                dv.wait_ge(s_dconst, CONST_END + k)
            node0(P_node0e, True)
            clear_carry(1)

            def overlay(P, i, u, out):
                n = P.at(i, u)
                P.landed(dv, "ld", i, u)
                own(P, "msg", n, tt(P.B["in0"][:, u, :], P.B["in0"][:, u, :], P.B["keep"][:, u, :], ALU.mult), 1)
                P.wait(dv, "tr", n)
                own(P, "msg", n, tt(out[:, u, :], P.B["in0"][:, u, :], at_bank(P, u, 0), ALU.add), 2)

            def body(i, us):
                for u in us:
                    n = P_e1.at(i, u)
                    overlay(P_e1, i, u, P_e1.B["a"])
                    P_e1.free(dv, "y", i, u)
                    scan(P_e1, n, u, P_e1.B["e"], P_e1.B["same"], P_e1.B["a"])
                    own(P_e1, "vec", n, tt(P_e1.B["f"][:, u, :], P_e1.B["e"][:, u, :], P_e1.B["in2"][:, u, :], ALU.add), 1)
                    own(P_e1, "vec", n, tt(P_e1.B["b"][:, u, :], P_e1.B["f"][:, u, :], P_e1.B["dinv"][:, u, :], ALU.mult), 2)
                    tt(P_e1.B["c"][:, u, :], P_e1.B["b"][:, u, :], P_e1.B["in1"][:, u, :], ALU.add).then_inc(P_e1.s("vec"), 1)
                for u in us:
                    normed(P_e1, i, u, 1, K["cb2"])
            in_groups(dv, P_e1, body)
            P_e1.all_done(dv)
            clear_carry(2)

            def body(i, us):
                P = P_e2
                for u in us:
                    n = P_e2.at(i, u)
                    P.stored(dv, "st", i, u)
                    P.free(dv, "t", i, u)
                    overlay(P, i, u, P_e2.B["o3"])
                    own(P, "vec", n, v.scalar_tensor_tensor(out=P_e2.B["b"][:, u, :], in0=P_e2.B["more"][:, u, :], scalar=0.0,
                                                            in1=P_e2.B["in1"][:, u, :], op0=ALU.is_equal, op1=ALU.mult))
                    for q, h in enumerate((1, 0)):
                        lo, hi = slice(64 * h, 64 * h + 64), slice(64 - 64 * h, 128 - 64 * h)
                        own(P, "scan", n, v.tensor_tensor_scan(
                            out=P_e2.B["o0"][lo, u, ::-1], data0=P_e2.B["more"][lo, u, ::-1], data1=P_e2.B["b"][lo, u, ::-1],
                            initial=carry[lo, 0:1], op0=ALU.mult, op1=ALU.add), 2 * q + 1)
                        own(P, "scan", n, v.tensor_copy(carry[hi, 0:1], P_e2.B["o0"][lo, u, 0:1]), 2 * q + 2)
                for u in us:
                    n = P_e2.at(i, u)
                    P.wait(dv, "evf", n)
                    v.bn_stats(stats["f"][:, bass.ds(n, 1), :], P_e2.B["o1"][:, u, :]).then_inc(P.s("bnf"), 1)
                    P.wait(dv, "evc", n)
                    v.bn_stats(stats["c"][:, bass.ds(n, 1), :], P_e2.B["o2"][:, u, :]).then_inc(P.s("bnc"), 1)
            in_groups(dv, P_e2, body)
            P_e2.all_done(dv)

            small = [0]

            def sm(ins):
                ins.then_inc(s_dv_small, 1)
                small[0] += 1
                dv.wait_ge(s_dv_small, small[0])

            def moments(names):
                for k, name in enumerate(names):
                    sm(v.bn_aggr(mv[:, k, :], stats[name][:, :, :]))
                    sm(v.tensor_copy(mom[:, k, 0:1], mv[:, k, 0:1]))
                    sm(v.scalar_tensor_tensor(out=mom[:, k, 1:2], in0=mv[:, k, 0:1], scalar=mv[:, k, 0:1],
                                              in1=mv[:, k, 1:2], op0=ALU.mult, op1=ALU.add))

            roots = [0]

            def affine(mean, square, gain, shift, s, t):
                sm(v.tensor_tensor(K["tmp0"], mean, mean, ALU.mult))
                sm(v.tensor_tensor(K["tmp1"], square, K["tmp0"], ALU.subtract))
                roots[0] += 2
                dv.wait_ge(s_ac_small, roots[0])
                sm(v.tensor_tensor(s, gain, K["tmp1"], ALU.mult))
                sm(v.tensor_tensor(K["tmp0"], mean, s, ALU.mult))
                sm(v.tensor_tensor(t, shift, K["tmp0"], ALU.subtract))

            moments(("f", "c"))
            assert small[0] == STATS1
            dv.wait_ge(s_pe_small, 5)
            sm(v.tensor_copy(hold[:, 0:4], bank[0][:, 0:4]))
            affine(hold[:, 0:1], hold[:, 1:2], K["g1f"], K["be1f"], K["s1f"], K["t1f"])
            affine(hold[:, 2:3], hold[:, 3:4], K["g1c"], K["be1c"], K["s1c"], K["t1c"])
            assert small[0] == STATS1B, small
            clear_carry(3)

            def body(i, us):
                P = P_e3
                for u in us:
                    n = P_e3.at(i, u)
                    P.landed(dv, "ld", i, u)
                    own(P, "msg", n, v.tensor_scalar(P_e3.B["e"][:, u, :], P_e3.B["in1"][:, u, :], K["s1c"], K["t1c"],
                                                     ALU.mult, ALU.add), 1)
                    own(P, "msg", n, v.tensor_scalar(P_e3.B["f"][:, u, :], P_e3.B["in0"][:, u, :], K["s1f"], K["t1f"],
                                                     ALU.mult, ALU.add), 2)
                    neg_abs(P, i, u, P_e3.B["g2"][:, u, :], P_e3.B["f"][:, u, :])
                for u in us:
                    sigmoid_arg(P, i, u, P_e3.B["in3"][:, u, :], P_e3.B["f"][:, u, :], P_e3.B["a"][:, u, :])
                for u in us:
                    P.wait(dv, "sig", P_e3.at(i, u))
                    n = P_e3.at(i, u)
                    P.wait(dv, "act", n)
                    own(P, "vec", n, v.scalar_tensor_tensor(out=P_e3.B["g"][:, u, :], in0=P_e3.B["e"][:, u, :], scalar=0.0,
                                                            in1=P_e3.B["d"][:, u, :], op0=ALU.max, op1=ALU.add), 1)
                    own(P, "vec", n, tt(P_e3.B["h"][:, u, :], P_e3.B["g"][:, u, :], P_e3.B["in4"][:, u, :], ALU.mult), 2)
                    scan(P, n, u, P_e3.B["o1"], P_e3.B["same"], P_e3.B["h"])
                    P.stored(dv, "st", i, u)
                    own(P, "out", n, v.scalar_tensor_tensor(out=P_e3.B["o0"][:, u, :], in0=P_e3.B["more"][:, u, :], scalar=0.0,
                                                            in1=P_e3.B["o1"][:, u, :], op0=ALU.is_equal, op1=ALU.mult))
                    v.bn_stats(stats["u"][:, bass.ds(n, 1), :], P_e3.B["o0"][:, u, :]).then_inc(P.s("bnf"), 1)
            in_groups(dv, P_e3, body)
            P_e3.all_done(dv)

            moments(("u",))
            assert small[0] == STATS2, small
            dv.wait_ge(s_pe_small, 6)
            sm(v.tensor_scalar(hold[:, 0:2], bank[0][:, 0:2], float(EDGES) / NODES, None, ALU.mult))
            affine(hold[:, 0:1], hold[:, 1:2], K["g2"], K["be2"], K["s2"], K["t2"])
            sm(v.tensor_scalar(K["nt2"], K["t2"], -1.0, None, ALU.mult))
            assert small[0] == STATS2B, small
            dv.wait_ge(s_pe_small, 7)
            sm(v.tensor_copy(K["ct2"], bank[1][:, 0:1]))
            assert small[0] == STATS2C

            def body(i, us):
                P = P_e4
                for u in us:
                    P.landed(dv, "ld", i, u)
                    P.free(dv, "act", i, u)
                    v.scalar_tensor_tensor(out=P.B["e"][:, u, :], in0=P.B["in1"][:, u, :], scalar=K["s2"],
                                           in1=P.B["in0"][:, u, :], op0=ALU.mult, op1=ALU.add).then_inc(P.s("msg"), 1)
                for u in us:
                    n = P.at(i, u)
                    P.wait(dv, "act", n)
                    own(P, "vec", n, v.scalar_tensor_tensor(out=P.B["h"][:, u, :], in0=P.B["e"][:, u, :], scalar=K["nt2"],
                                                            in1=P.B["a"][:, u, :], op0=ALU.max, op1=ALU.add), 1)
                    P.free(dv, "y", i, u)
                    tt(P.B["c"][:, u, :], P.B["h"][:, u, :], P.B["in0"][:, u, :], ALU.add).then_inc(P.s("vec"), 1)
                for u in us:
                    normed(P, i, u, 0, K["ct2"])
            in_groups(dv, P_e4, body)
            P_e4.all_done(dv)

            def soft(P, stat):
                def body(i, us):
                    for u in us:
                        n = P.at(i, u)
                        P.landed(dv, "ld", i, u)
                        P.wait(dv, "act", n)
                        own(P, "vec", n, v.scalar_tensor_tensor(out=P.B["h"][:, u, :], in0=P.B["in0"][:, u, :],
                                                                scalar=K["nt2"], in1=P.B["a"][:, u, :],
                                                                op0=ALU.max, op1=ALU.add), 1)
                        P.free(dv, "y", i, u)
                        tt(P.B["c"][:, u, :], P.B["h"][:, u, :], P.B["in0"][:, u, :], ALU.add).then_inc(P.s("vec"), 1)
                    for u in us:
                        if stat:
                            P.free(dv, "h", i, u)
                        normed(P, i, u, 0, K["ct2"])
                    if stat:
                        for u in us:
                            n = P.at(i, u)
                            P.wait(dv, "h", n)
                            v.bn_stats(stats["n"][:, bass.ds(n, 1), :], at_bank(P, u, 0)).then_inc(P.s("bnf"), 1)
                in_groups(dv, P, body)
                P.all_done(dv)
            soft(P_node1, True)
            soft(P_node1e, False)
            clear_carry(4)

            def body(i, us):
                P = P_e5
                for u in us:
                    n = P_e5.at(i, u)
                    P.stored(dv, "st", i, u)
                    overlay(P, i, u, P_e5.B["o0"])
                    P.free(dv, "h", i, u)
                    scan(P, n, u, P_e5.B["e"], P_e5.B["same"], P_e5.B["o0"])
                    tt(P_e5.B["b"][:, u, :], P_e5.B["e"][:, u, :], P_e5.B["in1"][:, u, :], ALU.add).then_inc(P.s("vec"), 1)
                for u in us:
                    n = P_e5.at(i, u)
                    P.wait(dv, "evs", n)
                    for k, (buf, name, done) in enumerate((("f", "hd", "bnf"), ("g", "hu", "bnc"))):
                        own(P, "mask", n, v.scalar_tensor_tensor(out=P_e5.B[buf][:, u, :], in0=P_e5.B["more"][:, u, :], scalar=0.0,
                                                                 in1=(P_e5.B["o1"][:, u, :], at_bank(P_e5, u, 1))[k], op0=ALU.is_equal, op1=ALU.mult), k + 1)
                        v.bn_stats(stats[name][:, bass.ds(n, 1), :], P_e5.B[buf][:, u, :]).then_inc(P.s(done), 1)
            in_groups(dv, P_e5, body)
            P_e5.all_done(dv)

            moments(("n", "hd", "hu"))
            assert small[0] == STATS3, small
            dv.wait_ge(s_pe_small, 8)
            sm(v.tensor_copy(hold[:, 0:6], bank[0][:, 0:6]))
            sm(v.tensor_tensor(hold[:, 2:4], hold[:, 2:4], hold[:, 4:6], ALU.subtract))
            sm(v.scalar_tensor_tensor(out=hold[:, 6:8], in0=hold[:, 2:4], scalar=float(EDGES) / NODES,
                                      in1=hold[:, 0:2], op0=ALU.mult, op1=ALU.add))
            affine(hold[:, 6:7], hold[:, 7:8], K["g3"], K["be3"], K["s3"], K["t3"])
            sm(v.tensor_tensor(K["tmp2"], hold[:, 6:7], K["bl2"], ALU.add))
            sm(v.tensor_tensor(K["tmp2"], K["bl2"], K["tmp2"], ALU.subtract))
            sm(v.tensor_tensor(K["tmp2"], K["tmp2"], K["s3"], ALU.mult))
            sm(v.tensor_tensor(K["t3"], K["be3"], K["tmp2"], ALU.add))
            assert small[0] == STATS3B, small

            def relu_bn(P, x2):
                def body(i, us):
                    for u in us:
                        P.landed(dv, "ld", i, u)
                        P.free(dv, "y", i, u)
                        P.wait(dv, "act", P.at(i, u))
                        tt(P.B["c"][:, u, :], P.B["a"][:, u, :], P.B[x2][:, u, :], ALU.add).then_inc(P.s("vec"), 1)
                    for u in us:
                        normed(P, i, u, 0, None)
                in_groups(dv, P, body)
                P.all_done(dv)
            relu_bn(P_e6, "in1")
            relu_bn(P_e6s, "in0")

            def node2(P):
                def body(i, us):
                    for u in us:
                        P.landed(dv, "ld", i, u)
                        P.wait(dv, "act", P.at(i, u))
                        tt(P.B["b"][:, u, :], P.B["b"][:, u, :], P.B["in0"][:, u, :], ALU.add).then_inc(P.s("vec"), 1)
                    for u in us:
                        P.wait(dv, "rstd", P.at(i, u))
                        tt(P.B["o0"][:, u, :], at_bank(P, u, 1), P.B["h"][:, u, :], ALU.mult).then_inc(P.s("out"), 1)
                    for u in us:
                        P.wait(dv, "hid", P.at(i, u))
                        P.free(dv, "g", i, u)
                        v.tensor_scalar(P.B["a"][:, u, :], at_bank(P, u, 0), K["b31"], 0.0, ALU.add, ALU.max).then_inc(P.s("relu0"), 1)
                    for u in us:
                        P.wait(dv, "g", P.at(i, u))
                        own(P, "z", P.at(i, u), v.tensor_scalar(P.B["e"][:, u, :], at_bank(P, u, 1), K["b32"], None, ALU.add))
                        neg_abs(P, i, u, P.B["in1"][:, u, :], P.B["e"][:, u, :])
                    for u in us:
                        sigmoid_arg(P, i, u, P.B["e"][:, u, :], P.B["e"][:, u, :], P.B["in1"][:, u, :])
                    for u in us:
                        P.free(dv, "y2", i, u)
                        P.wait(dv, "sig", P.at(i, u))
                        tt(P.B["o0"][:, u, :], P.B["e"][:, u, :], P.B["o0"][:, u, :], ALU.add).then_inc(P.s("add"), 1)
                    for u in us:
                        P.wait(dv, "rstd2", P.at(i, u))
                        tt(P.B["o1"][:, u, :], at_bank(P, u, 0), P.B["c"][:, u, :], ALU.mult).then_inc(P.s("out2"), 1)
                in_groups(dv, P, body)
                P.all_done(dv)
            node2(P_node2)
            clear_carry(5)

            P = P_e7

            def body(i, us):
                for u in us:
                    n = P.at(i, u)
                    overlay(P, i, u, P.B["a"])
                for u in us:
                    n = P.at(i, u)
                    P.wait(dv, "evs", n)
                    own(P, "vec", n, tt(P.B["g"][:, u, :], P.B["b"][:, u, :], P.B["wts"][:, u, :], ALU.mult), 1)
                    scan(P, n, u, P.B["e"], P.B["same"], P.B["g"])
                    P.wait(dv, "evd", n)
                    own(P, "vec", n, tt(P.B["f"][:, u, :], P.B["c"][:, u, :], P.B["dinv"][:, u, :], ALU.mult), 2)
                    own(P, "vec", n, tt(P.B["in4"][:, u, :], P.B["f"][:, u, :], P.B["e"][:, u, :], ALU.add), 3)
                    own(P, "vec", n, tt(P.B["in3"][:, u, :], P.B["in4"][:, u, :], P.B["dinv"][:, u, :], ALU.mult), 4)
                    v.tensor_scalar(P.B["h"][:, u, :], P.B["in3"][:, u, :], 0.0, None, ALU.max).then_inc(P.s("relu1"), 1)
                for u in us:
                    n = P.at(i, u)
                    P.wait(dv, "h", n)
                    P.stored(dv, "st", i, u)
                    v.scalar_tensor_tensor(out=P.B["o0"][:, u, :], in0=at_bank(P, u, 0), scalar=K["b32"], in1=P.B["dinv"][:, u, :],
                                           op0=ALU.add, op1=ALU.mult).then_inc(P.s("out"), 1)
            in_groups(dv, P, body)
            P.all_done(dv)
            clear_carry(6)

            node2(P_node2b)
            P = P_e8

            def body(i, us):
                for u in us:
                    n = P.at(i, u)
                    overlay(P, i, u, P.B["a"])
                    own(P, "msg", n, tt(P.B["g"][:, u, :], P.B["a"][:, u, :], P.B["wts"][:, u, :], ALU.mult), 3)
                    P.free(dv, "y", i, u)
                    scan(P, n, u, P.B["b"], P.B["same"], P.B["g"])
                    own(P, "vec", n, tt(P.B["h"][:, u, :], P.B["b"][:, u, :], P.B["in2"][:, u, :], ALU.add), 1)
                    own(P, "vec", n, tt(P.B["c"][:, u, :], P.B["h"][:, u, :], P.B["dinv"][:, u, :], ALU.mult), 2)
                    neg_abs(P, i, u, P.B["o1"][:, u, :], P.B["c"][:, u, :])
                for u in us:
                    sigmoid_arg(P, i, u, P.B["in3"][:, u, :], P.B["c"][:, u, :], P.B["e"][:, u, :])
                for u in us:
                    n = P.at(i, u)
                    P.wait(dv, "sig", n)
                    tt(P.B["f"][:, u, :], P.B["in4"][:, u, :], P.B["in1"][:, u, :], ALU.add).then_inc(P.s("add"), 1)
                for u in us:
                    P.free(dv, "row", i, u)
                    normed(P, i, u, 1, None, stored=False, rs="g2")
            in_groups(dv, P, body)


KEYS, PER = 5000, EDGES // TILE
SORT_KEYS = 1 + PER * 6 + 3
SORT_RANKED = 4 + EDGES // KEYS * SORT_KEYS
SORT_END = SORT_RANKED + 5

WEIGHT_DMAS = 5 + 12 + 6 + 1 + 2 * 14
CONST_END = 7
SETUP_SCAN, SETUP_CARRY, SETUP_ROWS = 10, 15, 23
PAIRS_OF_BLOCKS = (BLOCKS + 1) // 2
INFO_ROWS = PAIRS_OF_BLOCKS + 5
STATS1 = 6
STATS1B = STATS1 + 1 + 10
STATS2 = STATS1B + 3
STATS2B = STATS2 + 1 + 5 + 1
STATS2C = STATS2B + 1
STATS3 = STATS2C + 9
STATS3B = STATS3 + 3 + 5 + 4

ROW_NAMES = ["sdinv", "dinv", "same", "keep", "more", "wd", "dinv", "same", "keep", "w"]
ROW_SETS = {"e0": (0, ("sdinv wts", "dinv", "same")), "e1": (1, ("dinv", "same", "keep")), "e2": (3, ("keep", "more")),
            "e3": (2, ("same", "keep", "more")), "e7": (5, ("wd wts", "dinv", "same", "keep")),
            "e8": (6, ("dinv", "same", "keep", "w wts"))}

_ARGS = ["xt", "x", "src", "dstp", "ea", "ew", "w1", "w2", "w2t", "b1", "b2", "wf", "bf", "g1", "be1", "g2",
         "be2", "wl2", "bl2", "g3", "be3", "w31t", "b31", "w32t", "b32"]


def kernel(**inputs):
    import concourse.bacc as _bacc
    from concourse import mybir as _mybir
    from concourse.bass_utils import run_bass_kernel_spmd as _run

    a = {k: np.asarray(v) for k, v in inputs.items()}
    x = a["x"]
    arrays = {
        "xt": x.reshape(NODE_CHUNKS, TILE, 2, 4, D).transpose(0, 2, 4, 3, 1).reshape(NODE_CHUNKS, 128, COLS),
        "x": x, "src": a["src"],
        "dstp": np.concatenate([np.full(1, -1, a["dst"].dtype), a["dst"], np.full(1, -1, a["dst"].dtype)]),
        "ea": a["edge_attr_64"], "ew": a["edge_weight1"].reshape(-1),
        "w1": a["L0_gnn_W1"], "w2": a["L0_gnn_W2"], "w2t": a["L0_gnn_W2"].T, "b1": a["L0_gnn_b1"],
        "b2": a["L0_gnn_b2"], "wf": a["L1_gnn_W_full"], "bf": a["L1_gnn_b_full"], "g1": a["L1_gnn_bn1_g"],
        "be1": a["L1_gnn_bn1_b"], "g2": a["L1_gnn_bn2_g"], "be2": a["L1_gnn_bn2_b"], "wl2": a["L2_gnn_W"],
        "bl2": a["L2_gnn_b"], "g3": a["L2_gnn_gamma"], "be3": a["L2_gnn_beta"], "w31t": a["L3_gnn_W1"].T,
        "b31": a["L3_gnn_b1"], "w32t": a["L3_gnn_W2"].T, "b32": a["L3_gnn_b2"],
    }
    nc = _bacc.Bacc("TRN2", target_bir_lowering=False, num_devices=1)
    feed, args = {}, []
    for name in _ARGS:
        v = np.ascontiguousarray(arrays[name])
        feed[f"in_{name}"] = v
        args.append(nc.dram_tensor(f"in_{name}", v.shape, _mybir.dt.from_np(v.dtype), kind="ExternalInput").ap())
    args.append(nc.dram_tensor("out_0", (NODES, D), _mybir.dt.float32, kind="ExternalOutput").ap())
    gnn(nc, *args)
    r = _run(nc, [feed], core_ids=[0])
    return r.results[0]["out_0"]
```

```python
import numpy as np
import concourse.bass as bass
import concourse.mybir as mybir
from contextlib import ExitStack

F32 = mybir.dt.float32
I32 = mybir.dt.int32
ALU = mybir.AluOpType
ACT = mybir.ActivationFunctionType

NODES, EDGES, D, HID = 100000, 25000, 64, 128
COLS = 500
PACK = 2 * COLS
TILE = 125
TILES = PACK // TILE
NODE_CHUNKS = NODES // PACK
BLOCKS = EDGES // PACK
NODE2_EARLY = 32
CHUNK_BUFFERS = 11
NAT = 100
SKIP = 1 << 20
EPS = 1e-5


class Sems:

    def __init__(self, make):
        self.make, self.sem, self.total = make, {}, {}
        self.passed = {}

    def wait(self, eng, sem, value):
        eng.wait_ge(sem, value)
        if not isinstance(value, int) and id(eng) in self.passed:
            eng.sem_inc(self.passed[id(eng)], 1)

    def get(self, name):
        if name not in self.sem:
            self.sem[name], self.total[name] = self.make(name), 0
        return self.sem[name]


class Phase:

    def __init__(self, sems, chunks, steps, dmas, slots=4):
        self.chunks, self.sems, self.steps, self.dmas = chunks, sems, steps, dmas
        self.slots = slots
        self.base = {}
        for name, count in steps.items():
            sems.get(name)
            self.base[name] = sems.total[name]
            sems.total[name] += chunks * count
        for name, count in dmas.items():
            for u in range(slots):
                slot = f"{name}{u}"
                sems.get(slot)
                self.base[slot] = sems.total[slot]
                sems.total[slot] += self.in_slot(u) * 16 * count
        self.ends = [(sems.sem[n], self.base[n] + chunks * c) for n, c in steps.items()]
        self.ends += [(sems.sem[f"{n}{u}"], self.base[f"{n}{u}"] + self.in_slot(u) * 16 * c)
                      for n, c in dmas.items() for u in range(slots)]

    def in_slot(self, u):
        return (self.chunks + self.slots - 1 - u) // self.slots

    def at(self, i, u):
        return self.slots * i + u

    def s(self, name):
        return self.sems.sem[name]

    def wait(self, eng, step, n, part=None):
        q = self.steps[step]
        part = q if part is None else part
        self.sems.wait(eng, self.s(step), self.base[step] + n * q + part)

    def free(self, eng, step, i, u):
        if not (isinstance(i, int) and i == 0):
            self.wait(eng, step, self.at(i, u) - self.slots)

    def landed(self, eng, dma, i, u):
        slot = f"{dma}{u}"
        self.sems.wait(eng, self.s(slot), self.base[slot] + (i + 1) * (16 * self.dmas[dma]))

    def stored(self, eng, dma, i, u):
        if not (isinstance(i, int) and i == 0):
            slot = f"{dma}{u}"
            self.sems.wait(eng, self.s(slot), self.base[slot] + i * (16 * self.dmas[dma]))

    def all_done(self, eng):
        for sem, value in self.ends:
            if value:
                eng.wait_ge(sem, value)


def in_groups(eng, P, body):
    body(0, range(P.slots))
    if P.chunks // P.slots > 1:
        with eng.Fori(1, P.chunks // P.slots) as i:
            body(i, range(P.slots))
    if P.chunks % P.slots:
        body(P.chunks // P.slots, range(P.chunks % P.slots))


def in_groups_ahead(eng, P, first, body):
    groups = P.chunks // P.slots
    assert P.chunks % P.slots == 0
    for u in range(P.slots):
        first(0, u)
    body(0, range(P.slots), True)
    with eng.Fori(1, groups - 1) as i:
        body(i, range(P.slots), True)
    body(groups - 1, range(P.slots), False)


def in_turn(eng, P, stages):
    groups, rest = P.chunks // 4, P.chunks % 4

    def turns(i, before, slots):
        for u in slots:
            for lag, stage in stages:
                if u - lag >= 0:
                    stage(i, u - lag)
                elif before is not None:
                    stage(before, u - lag + 4)

    turns(0, None, range(4))
    turns(1, 0, range(4))
    with eng.Fori(2, groups) as i:
        turns(i, i - 1, range(4))
    turns(groups, groups - 1, range(rest))
    for u in range(rest, rest + max(lag for lag, _ in stages)):
        for lag, stage in stages:
            if u - lag < rest and lag:
                stage(*((groups, u - lag) if u - lag >= 0 else (groups - 1, u - lag + 4)))


def gnn(nc, xt, x, src_in, dstp, ea_in, ew, w1, w2, w2t, b1, b2, wf, bf, g1, be1, g2, be2,
        wl2, bl2, g3, be3, w31t, b31, w32t, b32, out):
    def dram(name, *shape):
        return nc.dram_tensor(name, list(shape), F32).ap()

    XDR, XSR = dram("xdr", BLOCKS, TILE, 512), dram("xsr", BLOCKS, TILE, 512)
    SLOTS = dram("slots", NODES, 4)
    XE = dram("xe", 2 * BLOCKS, 128, COLS)
    X1 = dram("x1", NODE_CHUNKS + 2 * BLOCKS, 128, COLS)
    X2 = dram("x2", NODE_CHUNKS + 2 * BLOCKS, 128, COLS)
    GU, GD = dram("gu", 2 * BLOCKS, 128, COLS), dram("gd", BLOCKS, 128, COLS)
    X1D, X1F = dram("x1d", BLOCKS, 128, COLS), dram("x1f", BLOCKS, 128, COLS)
    TF, TC, UPD = (dram(n, BLOCKS, 128, COLS) for n in ("tf", "tc", "upd"))
    X2D, X2S, HD = (dram(n, BLOCKS, 128, COLS) for n in ("x2d", "x2s", "hd"))
    X3D, X3S, QS, QD = (dram(n, BLOCKS, 128, COLS) for n in ("x3d", "x3s", "qs", "qd"))
    TAB = [dram(f"tab{n}", EDGES, D) for n in range(5)]
    OV = [dram(f"ov{n}", BLOCKS, TILE, 512) for n in range(5)]
    ROWS = dram("rows", 2 * BLOCKS, len(ROW_NAMES), COLS)
    META_S = dram("meta_sorted", EDGES + 2, 4)
    EA_S = dram("ea_sorted", EDGES + 2, D)

    ctx = ExitStack()
    with ctx:
        def sb(name, shape, dt=F32):
            return ctx.enter_context(nc.sbuf_tensor(name, list(shape), dt))

        def sem(name):
            return ctx.enter_context(nc.semaphore(name))

        bank = [ctx.enter_context(nc.psum_tensor(f"bank{k}", [128, 512], F32)) for k in range(8)]

        ident, J, C, HALF = (sb(n, [128, 128]) for n in ("ident", "J", "C", "HALF"))
        MATS = ["w1a", "w1b", "w2a", "w2b", "w2ca", "w2cb", "srcf", "dstf", "nbrf", "srcc", "dstc",
                "nbrc", "wl2", "w31", "w32"]
        mats = sb("mats", [128, len(MATS), 128])
        M = {n: mats[:, k, :] for k, n in enumerate(MATS)}
        w2t_sb = sb("w2t_sb", [D, HID])
        CN = ["b1", "b2", "bf", "bc", "g1f", "g1c", "be1f", "be1c", "g2", "be2", "bl2", "g3", "be3",
              "b31", "b32", "cb2", "s1f", "t1f", "s1c", "t1c", "s2", "t2", "nt2",
              "ct2", "s3", "t3", "eps", "tmp0", "tmp1", "tmp2", "tmp3"]
        cols = sb("cols", [128, len(CN)])
        K = {n: cols[:, k:k + 1] for k, n in enumerate(CN)}
        nat_i = sb("nat_i", [NAT, 4, 250], I32)
        nat = sb("nat", [NAT, 12, 250])
        tiny = sb("tiny", [1, 4, NAT])
        carry_in = sb("carry_in", [NAT, 1])
        col = sb("col", [TILE, 4, 200])
        idx_src, idx_dst, idx_last = (sb(n, [TILE, 200], I32) for n in ("idx_src", "idx_dst", "idx_last"))
        idx_f = sb("idx_f", [TILE, 200])
        slot_rows = sb("slot_rows", [TILE, 200, 4])
        row_no = sb("row_no", [TILE, 200], I32)
        src_info = sb("src_info", [TILE, 200, 4])
        gat = sb("gat", [TILE, 4, TILES, D])
        gidx = sb("gidx", [TILE, 4, TILES], I32)
        grow = sb("grow", [TILE, 4, TILES, 4])
        bufs = sb("bufs", [128, 4 * CHUNK_BUFFERS, COLS])

        def buffers(names, rows=()):
            R = len(rows)
            views = {}
            for k, row in enumerate(rows):
                for name in row.split():
                    views[name] = bufs[:, k:4 * R:max(R, 1), :]
            views["rows"] = bufs[:, 0:4 * R, :].rearrange("p (u r) c -> p u r c", u=4) if R else None
            for k, entry in enumerate(names):
                for name in entry.split():
                    views[name] = bufs[:, 4 * (R + k):4 * (R + k) + 4, :]
            assert R + len(names) <= CHUNK_BUFFERS
            return views

        rows_in_all = sb("rows_in", [TILE, 2, 4, TILES, D])
        rows_in = [rows_in_all[:, k] for k in (0, 1)]
        default = rows_in_all[:, :, :, :, :].rearrange("p k u t f -> p (k u t f)")[:, 0:NODES // TILE * 4]\
            .rearrange("p (t c) -> p t c", c=4)
        rows_out = sb("rows_out", [TILE, 4, TILES, D])
        carry = sb("carry", [128, 1])
        viol = sb("viol", [NAT, 1])
        flag = sb("flag", [1, 1], I32)
        pad = sb("pad", [1, 4])
        key_col, edge_col = sb("key_col", [TILE, 1]), sb("edge_col", [TILE, 1])
        part, rank = sb("part", [TILE, PER]), sb("rank", [TILE, PER])
        arena = bufs[0:TILE, :, :].rearrange("p n c -> p (n c)")
        key_i, key_f, no_i, no_f = (arena[:, k * KEYS:(k + 1) * KEYS] for k in range(4))
        key_i, no_i, work = key_i.bitcast(I32), no_i.bitcast(I32), no_i
        own_i = arena[:, 4 * KEYS:4 * KEYS + 2 * PER].rearrange("p (k t) -> p k t", k=2).bitcast(I32)
        own_no = arena[:, 4 * KEYS + 2 * PER:4 * KEYS + 3 * PER].bitcast(I32)
        own_f = arena[:, 4 * KEYS + 3 * PER:4 * KEYS + 6 * PER].rearrange("p (k t) -> p k t", k=3)
        meta = src_info
        rank_i = idx_last
        meta_in = bufs[0:NAT, :, :].rearrange("p n c -> p (n c)")[:, 0:3000].rearrange("p (k c) -> p k c", k=3)
        stats = {n: sb(f"stats_{n}", [128, k, 6]) for n, k in
                 (("f", BLOCKS), ("c", BLOCKS), ("u", BLOCKS), ("n", NODE_CHUNKS), ("hd", BLOCKS), ("hu", BLOCKS))}
        mv = sb("mv", [128, 8, 2])
        mom = sb("mom", [128, 8, 2])
        hold = sb("hold", [128, 8])

        sems = Sems(sem)
        SIG = {"nabs": 1, "lsig": 2, "arg": 1, "sig": 1}
        LN = {"y": 1, "sq": 1, "var": 1, "lnv": 1, "rstd": 1, "out": 1}
        P_node0 = Phase(sems, NODE_CHUNKS, {"hid": 1, "relu0": 1, "relu1": 1, **LN}, {"ld": 1, "st": 1})
        P_e0 = Phase(sems, BLOCKS, {"tr": 1, "evs": 1, "evd": 1, "msg": 1, "scan": 4, "vec": 3, "hid": 1,
                                    "relu0": 1, "relu1": 1, "g": 1, "out": 1, "row": 1, "evrow": 1},
                     {"ld": 4, "st": 4})
        P_node0e = Phase(sems, 2 * BLOCKS, {"hid": 1, "relu0": 1, "relu1": 1, "g": 1, "evs": 1, **LN},
                         {"ld": 1, "st": 2})
        P_e1 = Phase(sems, BLOCKS, {"tr": 1, "msg": 2, "scan": 4, "vec": 3, **LN, "row": 1, "evrow": 1},
                     {"ld": 6, "st": 2})
        P_e2 = Phase(sems, BLOCKS, {"tr": 1, "evs": 1, "msg": 2, "vec": 1, "scan": 4, "t": 1, "evf": 1,
                                    "evc": 1, "bnf": 1, "bnc": 1}, {"ld": 7, "st": 4})
        P_e3 = Phase(sems, BLOCKS, {"act": 3, "msg": 2, **SIG, "vec": 2, "scan": 4, "out": 1, "bnf": 1}, {"ld": 4, "st": 1})
        P_e4 = Phase(sems, BLOCKS, {"msg": 1, "vec": 2, "act": 3, **LN, "row": 1, "evrow": 1}, {"ld": 2, "st": 2})
        P_node1 = Phase(sems, NODE_CHUNKS, {"vec": 2, "act": 3, **LN, "h": 1, "bnf": 1}, {"ld": 1, "st": 1})
        P_node1e = Phase(sems, 2 * BLOCKS, {"vec": 2, "act": 3, **LN}, {"ld": 1, "st": 1})
        P_e5 = Phase(sems, BLOCKS, {"tr": 1, "msg": 2, "scan": 4, "vec": 1, "h": 1, "evs": 1, "mask": 2,
                                    "bnf": 1, "bnc": 1}, {"ld": 6, "st": 2})
        P_e6 = Phase(sems, BLOCKS, {"act": 1, "vec": 1, **LN, "row": 1, "evrow": 1}, {"ld": 2, "st": 2})
        P_e6s = Phase(sems, BLOCKS, {"h": 1, "act": 1, "vec": 1, **LN}, {"ld": 1, "st": 1})
        NODE2 = {"h": 1, "act": 1, "vec": 1, **LN, "hid": 1, "relu0": 1, "g": 1, "z": 1, **SIG,
                 "add": 1, "y2": 1, "sq2": 1, "var2": 1, "lnv2": 1, "rstd2": 1, "out2": 1, "row": 1, "evrow": 1}
        P_node2 = Phase(sems, NODE2_EARLY, NODE2, {"ld": 1, "st": 1})
        P_e7 = Phase(sems, BLOCKS, {"tr": 1, "msg": 2, "hid": 1, "evs": 1, "evd": 1, "relu0": 1, "vec": 4,
                                    "scan": 4, "relu1": 1, "g": 1, "h": 1, "act": 1, "out": 1, "row": 1,
                                    "evrow": 1}, {"ld": 5, "st": 3})
        P_node2b = Phase(sems, NODE_CHUNKS - NODE2_EARLY, NODE2, {"ld": 1, "st": 1})
        P_e8 = Phase(sems, BLOCKS, {"tr": 1, "msg": 3, "scan": 4, "vec": 2, **SIG, "add": 1,
                                    **LN, "row": 1, "evrow": 1}, {"ld": 6})

        s_w, s_nat, s_def, s_rows = sem("s_w"), sem("s_nat"), sem("s_def"), sem("s_rows")
        s_const, s_dconst, s_setup, s_tcol, s_ccol = (sem(n) for n in
                                                      ("s_const", "s_dconst", "s_setup", "s_tcol", "s_ccol"))
        s_pe_small, s_dv_small, s_idx = sem("s_pe_small"), sem("s_dv_small"), sem("s_idx")
        s_info, s_ac_small = sem("s_info"), sem("s_ac_small")
        s_gcopy, s_gather = sem("s_gcopy"), [sem("s_gather0"), sem("s_gather1")]
        s_gstore = [sem("s_gstore0"), sem("s_gstore1")]
        s_scatter = [sem("s_scatter0"), sem("s_scatter1")]
        s_final = [sem(f"s_final{u}") for u in range(4)]
        s_iota = sem("s_iota")
        s_flag, s_own, s_keys, s_keys_used, s_rank, s_numbered, s_ranked = (sem(n) for n in (
            "s_flag", "s_own", "s_keys", "s_keys_used", "s_rank", "s_numbered", "s_ranked"))
        s_ea_in, s_rank_copy, s_sorted, s_meta, s_pad, s_ea = (sem(n) for n in (
            "s_ea_in", "s_rank_copy", "s_sorted", "s_meta", "s_pad", "s_ea"))
        s_passed_sp, s_passed_pool = sem("s_passed_sp"), sem("s_passed_pool")

        POOL = ["xd", "slot", "info", "xs", "ov0", "ov1", "ov2", "ov3", "ov4", "final"]
        per_slot = [(BLOCKS + 1 - u) // 2 for u in (0, 1)]
        GATHERS = [n for n in POOL if n not in ("slot", "final")]
        STORES = [n for n in GATHERS if n != "info"]

        def gather_base(name, half):
            return GATHERS.index(name) * (BLOCKS // 4 * 2 + BLOCKS % 4 * (1 - half)) * 16 * TILES

        def store_base(name, half):
            return STORES.index(name) * pairs_in(half) * 16

        def pairs_in(half):
            return (BLOCKS + 3 - 2 * half) // 4

        def gathered(eng, name, i, u):
            sems.wait(eng, s_gstore[u // 2], store_base(name, u // 2) + (i + 1) * 16)

        def scattered(eng, i, u):
            if not (isinstance(i, int) and i == 0):
                sems.wait(eng, s_final[u], i * (16 * TILES))

        PAIRS = Phase(sems, BLOCKS, {}, {}, slots=2)
        FOURS = Phase(sems, BLOCKS, {}, {})
        nodes = buffers(("in0", "in1", "a", "b", "c", "d", "e", "g", "h", "o0", "o1"))
        for P in (P_node0, P_node0e, P_e4, P_node1, P_node1e, P_e6, P_e6s, P_node2, P_node2b):
            P.B = nodes
        P_e0.B = buffers(("o1", "o2", "a", "e", "f g b", "c", "d", "o0"), ROW_SETS["e0"][1])
        P_e1.B = buffers(("in0 a", "in1", "in2", "e f b c", "d", "g", "o0"), ROW_SETS["e1"][1])
        P_e2.B = buffers(("in0", "in1 b", "a", "o3", "o0", "o1", "o2"), ROW_SETS["e2"][1])
        P_e3.B = buffers(("in0", "in1", "e g h", "f in3 in4", "g2 a", "b c d", "o1", "o0"), ROW_SETS["e3"][1])
        P_e5.B = buffers(("in0", "in1", "in2", "o0", "e b", "o1", "f", "g"), ROW_SETS["e3"][1])
        P_e7.B = buffers(("in0 a", "in1", "b g", "c f in4 in3 h o0", "d", "e", "o1"), ROW_SETS["e7"][1])
        P_e8.B = buffers(("in0 a g o1 e", "in1", "in2", "b h c in3 in4 f", "d", "g2", "o0"), ROW_SETS["e8"][1])
        block = ctx.enter_context(nc.Block())

        @block.sync
        def _(sp):
            def factors(P, which, u, blk):
                first, names = ROW_SETS[which]
                for h in (0, 1):
                    yield P.B["rows"][64 * h:64 * h + 64, u], \
                        ROWS[bass.ds(2 * blk + h, 1), first:first + len(names), :].to_broadcast([64, len(names), COLS])

            def store_factors(pairs):
                for k, name in pairs:
                    for r, other in enumerate(ROW_NAMES):
                        if other == name:
                            for a in (0, 1):
                                sp.dma_start(ROWS[:, r, 250 * a:250 * a + 250], nat[a::2, k, :]).then_inc(s_rows, 16)

            for k, off in enumerate((0, 1, 2)):
                sp.dma_start(nat_i[:, k, :], dstp[off:off + EDGES].rearrange("(a b) -> a b", a=NAT)).then_inc(s_nat, 16)
            sp.dma_start(nat_i[:, 3, :], src_in.rearrange("(a b) -> a b", a=NAT)).then_inc(s_nat, 16)
            sp.dma_start(nat[:, 11, :], ew.rearrange("(a b) -> a b", a=NAT)).then_inc(s_nat, 16)
            sems.passed[id(sp)] = s_passed_sp
            sp.wait_ge(s_dconst, 1)

            def twice(name, src):
                for h in (0, 1):
                    sp.dma_start(M[name][64 * h:64 * h + 64, 64 * h:64 * h + 64], src).then_inc(s_w, 16)

            sp.dma_start(M["w1a"][0:64, :], w1).then_inc(s_w, 16)
            sp.dma_start(M["w1b"][64:128, :], w1).then_inc(s_w, 16)
            sp.dma_start(M["w2a"][:, 0:64], w2).then_inc(s_w, 16)
            sp.dma_start(M["w2b"][:, 64:128], w2).then_inc(s_w, 16)
            sp.dma_start(w2t_sb[:, :], w2t).then_inc(s_w, 16)
            for part, o in (("f", 0), ("c", 64)):
                for k, name in enumerate(("src", "dst", "nbr")):
                    twice(name + part, wf[64 * k:64 * k + 64, o:o + 64])
            twice("wl2", wl2)
            twice("w31", w31t)
            twice("w32", w32t)

            def column(name, src):
                n = src.shape[0]
                for h in range(128 // n):
                    sp.dma_start(K[name][n * h:n * h + n, :], src.rearrange("(a o) -> a o", o=1)).then_inc(s_w, 16)

            for name, src in (("b1", b1), ("b2", b2), ("bf", bf[0:64]), ("bc", bf[64:128]), ("g1f", g1[0:64]),
                              ("g1c", g1[64:128]), ("be1f", be1[0:64]), ("be1c", be1[64:128]), ("g2", g2),
                              ("be2", be2), ("bl2", bl2), ("g3", g3), ("be3", be3), ("b31", b31), ("b32", b32)):
                column(name, src)
            sp.wait_ge(s_dconst, 6)
            sp.dma_start(SLOTS.rearrange("(p t) c -> p (t c)", p=TILE),
                         default[:, :, :].rearrange("p t c -> p (t c)")).then_inc(s_def, 16)
            sp.wait_ge(s_flag, 2)
            unsorted = sp.value_load(flag[0:1, 0:1])
            with sp.If(unsorted > 0):
                for k, row in enumerate((dstp[1:1 + EDGES], src_in)):
                    sp.dma_start(own_i[:, k, :], row.rearrange("(p t) -> p t", p=TILE)).then_inc(s_own, 16)
                sp.dma_start(own_f[:, 2, :], ew.rearrange("(p t) -> p t", p=TILE)).then_inc(s_own, 16)
                for r in (0, EDGES + 1):
                    sp.dma_start(META_S[r:r + 1, :], pad[:, :]).then_inc(s_pad, 16)
                for c in range(EDGES // KEYS):
                    if c:
                        sp.wait_ge(s_keys_used, c)
                    sp.dma_start(key_i, dstp[1 + c * KEYS:1 + (c + 1) * KEYS].rearrange("(o c) -> o c", o=1)
                                 .to_broadcast([TILE, KEYS])).then_inc(s_keys, 16)
                sp.wait_ge(s_sorted, BLOCKS * TILES * 2 * 16)
                sp.wait_ge(s_pad, 32)
                for off in (0, 1, 2):
                    sp.dma_start(meta_in[:, off, :], META_S[off:off + EDGES, :].rearrange("(a b) c -> a (b c)", a=NAT))\
                      .then_inc(s_meta, 16)
                sp.wait_ge(s_rank, SORT_END)
                sp.sem_inc(s_ea, 16)
            with sp.Else():
                sp.dma_start(EA_S[1:1 + EDGES, :], ea_in).then_inc(s_ea, 16)
            sp.wait_ge(s_setup, SETUP_ROWS)
            store_factors(((11, "w"), (4, "same"), (6, "more"), (10, "dinv")))

            def run_groups(P, load, store):
                last = P.in_slot(0)

                def slots(i):
                    return range(min(4, P.chunks - i * 4))

                def loads(i, us):
                    for u in us:
                        for dst, src in load(i, u):
                            sp.dma_start(dst, src).then_inc(P.s(f"ld{u}"), 16)

                def stores(i, us):
                    for u in us:
                        for dst, src in store(i, u):
                            sp.dma_start(dst, src).then_inc(P.s(f"st{u}"), 16)

                loads(0, slots(0))
                loads(1, slots(1))
                stores(0, slots(0))
                with sp.Fori(1, last - 2) as i:
                    loads(i + 1, slots(0))
                    stores(i, slots(0))
                loads(last - 1, slots(last - 1))
                stores(last - 2, slots(0))
                stores(last - 1, slots(last - 1))

            def run(P, load, store):
                groups = P.chunks // 4

                def loads(i, u):
                    for dst, src in load(i, u):
                        sp.dma_start(dst, src).then_inc(P.s(f"ld{u}"), 16)

                def stores(i, u):
                    for dst, src in store(i, u):
                        sp.dma_start(dst, src).then_inc(P.s(f"st{u}"), 16)

                def known(k):
                    if k >= 2:
                        stores(*divmod(k - 2, 4))
                    if k + 3 < P.chunks:
                        loads(*divmod(k + 3, 4))

                for k in (0, 1, 2):
                    loads(0, k)
                for k in range(8):
                    known(k)
                with sp.Fori(2, groups - 1) as i:
                    for u in range(4):
                        stores(*((i, u - 2) if u >= 2 else (i - 1, u + 2)))
                        loads(*((i, 3) if u == 0 else (i + 1, u - 1)))
                for k in range(4 * (groups - 1), P.chunks + 2):
                    known(k)

            def load(i, u):
                P_node0.free(sp, "y", i, u)
                yield P_node0.B["in0"][:, u, :], xt[P_node0.at(i, u), :, :]

            def store(i, u):
                P_node0.wait(sp, "out", P_node0.at(i, u))
                yield X1[P_node0.at(i, u), :, :], P_node0.B["o0"][:, u, :]
            run_groups(P_node0, load, store)
            P_node0.all_done(sp)

            sp.wait_ge(s_info, INFO_ROWS)
            store_factors(((0, "keep"), (1, "sdinv"), (2, "wd")))
            sp.wait_ge(s_rows, 20 * 16)
            sp.wait_ge(s_def, 16)

            def load(i, u):
                n = P_e0.at(i, u)
                P_e0.free(sp, "out", i, u)
                gathered(sp, "xs", i, u)
                yield rows_in[0][:, u, :, :].rearrange("p t f -> p (t f)"), XSR[n, :, :]
                yield rows_in[1][:, u, :, :].rearrange("p t f -> p (t f)"), XDR[n, :, :]
                yield from factors(P_e0, "e0", u, n)

            def store(i, u):
                n = P_e0.at(i, u)
                P_e0.wait(sp, "evs", n)
                yield XE[n, :, :], P_e0.B["o1"][:, u, :]
                P_e0.wait(sp, "evd", n)
                yield XE[BLOCKS + n, :, :], P_e0.B["o2"][:, u, :]
                P_e0.wait(sp, "out", n)
                yield GD[n, :, :], P_e0.B["o0"][:, u, :]
                P_e0.wait(sp, "evrow", n)
                yield table(0, n), flat(u)

            def table(t, n):
                return TAB[t].rearrange("(k p t) f -> k p (t f)", p=TILE, t=TILES)[n, :, :]

            def flat(u):
                return rows_out[:, u, :, :].rearrange("p t f -> p (t f)")
            run(P_e0, load, store)
            P_e0.all_done(sp)

            def load(i, u):
                P_node0e.free(sp, "y", i, u)
                yield P_node0e.B["in0"][:, u, :], XE[P_node0e.at(i, u), :, :]

            def store(i, u):
                P_node0e.wait(sp, "evs", P_node0e.at(i, u))
                yield GU[P_node0e.at(i, u), :, :], P_node0e.B["o1"][:, u, :]
                P_node0e.wait(sp, "out", P_node0e.at(i, u))
                yield X1[P_node0e.at(i, u) + NODE_CHUNKS, :, :], P_node0e.B["o0"][:, u, :]
            run_groups(P_node0e, load, store)
            P_node0e.all_done(sp)

            def load(i, u):
                n = P_e1.at(i, u)
                P_e1.free(sp, "vec", i, u)
                gathered(sp, "ov0", i, u)
                yield rows_in[0][:, u, :, :].rearrange("p t f -> p (t f)"), OV[0][n, :, :]
                yield P_e1.B["in0"][:, u, :], GU[n, :, :]
                yield P_e1.B["in1"][:, u, :], XE[BLOCKS + n, :, :]
                yield P_e1.B["in2"][:, u, :], GD[n, :, :]
                yield from factors(P_e1, "e1", u, n)

            def store(i, u):
                n = P_e1.at(i, u)
                P_e1.wait(sp, "out", n)
                yield X1D[n, :, :], P_e1.B["o0"][:, u, :]
                P_e1.wait(sp, "evrow", n)
                yield table(1, n), flat(u)
            run(P_e1, load, store)
            P_e1.all_done(sp)

            sp.wait_ge(s_ea, 16)

            def load(i, u):
                n = P_e2.at(i, u)
                k = BLOCKS - 1 - n
                P_e2.free(sp, "scan", i, u)
                gathered(sp, "ov1", i, u)
                yield rows_in[0][:, u, :, :].rearrange("p t f -> p (t f)"), OV[1][k, :, :]
                for h in (0, 1):
                    yield rows_in[1][:, u, h::2, :], \
                        EA_S[bass.ds(k * PACK + h * COLS + 1, COLS), :].rearrange("(t p) f -> p t f", p=TILE)
                yield P_e2.B["in0"][:, u, :], X1[k + NODE_CHUNKS, :, :]
                yield P_e2.B["in1"][:, u, :], X1D[k, :, :]
                yield from factors(P_e2, "e2", u, k)

            def store(i, u):
                n = P_e2.at(i, u)
                k = BLOCKS - 1 - n
                P_e2.wait(sp, "scan", n)
                yield X1F[k, :, :], P_e2.B["o0"][:, u, :]
                P_e2.wait(sp, "evf", n)
                yield TF[k, :, :], P_e2.B["o1"][:, u, :]
                P_e2.wait(sp, "evc", n)
                yield TC[k, :, :], P_e2.B["o2"][:, u, :]
                P_e2.wait(sp, "msg", n)
                yield X2S[k, :, :], P_e2.B["o3"][:, u, :]
            run(P_e2, load, store)
            P_e2.all_done(sp)

            def load(i, u):
                n = P_e3.at(i, u)
                P_e3.free(sp, "out", i, u)
                yield P_e3.B["in0"][:, u, :], TF[n, :, :]
                yield P_e3.B["in1"][:, u, :], TC[n, :, :]
                yield from factors(P_e3, "e3", u, n)

            def store(i, u):
                P_e3.wait(sp, "out", P_e3.at(i, u))
                yield UPD[P_e3.at(i, u), :, :], P_e3.B["o0"][:, u, :]
            run(P_e3, load, store)
            P_e3.all_done(sp)

            def load(i, u):
                P_e4.free(sp, "vec", i, u)
                yield P_e4.B["in0"][:, u, :], X1F[P_e4.at(i, u), :, :]
                yield P_e4.B["in1"][:, u, :], UPD[P_e4.at(i, u), :, :]

            def store(i, u):
                P_e4.wait(sp, "out", P_e4.at(i, u))
                yield X2D[P_e4.at(i, u), :, :], P_e4.B["o0"][:, u, :]
                P_e4.wait(sp, "evrow", P_e4.at(i, u))
                yield table(2, P_e4.at(i, u)), flat(u)
            run_groups(P_e4, load, store)
            P_e4.all_done(sp)

            def load(i, u):
                P_node1.free(sp, "vec", i, u)
                yield P_node1.B["in0"][:, u, :], X1[P_node1.at(i, u), :, :]

            def store(i, u):
                P_node1.wait(sp, "out", P_node1.at(i, u))
                yield X2[P_node1.at(i, u), :, :], P_node1.B["o0"][:, u, :]
            run_groups(P_node1, load, store)
            P_node1.all_done(sp)

            def load(i, u):
                P_node1e.free(sp, "vec", i, u)
                yield P_node1e.B["in0"][:, u, :], X1[P_node1e.at(i, u) + NODE_CHUNKS, :, :]

            def store(i, u):
                P_node1e.wait(sp, "out", P_node1e.at(i, u))
                yield X2[P_node1e.at(i, u) + NODE_CHUNKS, :, :], P_node1e.B["o0"][:, u, :]
            run_groups(P_node1e, load, store)
            P_node1e.all_done(sp)

            def load(i, u):
                n = P_e5.at(i, u)
                P_e5.free(sp, "mask", i, u)
                gathered(sp, "ov2", i, u)
                yield rows_in[0][:, u, :, :].rearrange("p t f -> p (t f)"), OV[2][n, :, :]
                yield P_e5.B["in0"][:, u, :], X2[n + NODE_CHUNKS, :, :]
                yield P_e5.B["in1"][:, u, :], X2D[n, :, :]
                yield P_e5.B["in2"][:, u, :], X2[n + NODE_CHUNKS + BLOCKS, :, :]
                yield from factors(P_e5, "e3", u, n)

            def store(i, u):
                n = P_e5.at(i, u)
                P_e5.wait(sp, "msg", n)
                yield X2S[n, :, :], P_e5.B["o0"][:, u, :]
                P_e5.wait(sp, "evs", n)
                yield HD[n, :, :], P_e5.B["o1"][:, u, :]
            run(P_e5, load, store)
            P_e5.all_done(sp)

            def load(i, u):
                P_e6.free(sp, "vec", i, u)
                yield P_e6.B["in0"][:, u, :], HD[P_e6.at(i, u), :, :]
                yield P_e6.B["in1"][:, u, :], X2D[P_e6.at(i, u), :, :]

            def store(i, u):
                P_e6.wait(sp, "out", P_e6.at(i, u))
                yield X3D[P_e6.at(i, u), :, :], P_e6.B["o0"][:, u, :]
                P_e6.wait(sp, "evrow", P_e6.at(i, u))
                yield table(3, P_e6.at(i, u)), flat(u)
            run_groups(P_e6, load, store)
            P_e6.all_done(sp)

            def load(i, u):
                P_e6s.free(sp, "vec", i, u)
                yield P_e6s.B["in0"][:, u, :], X2S[P_e6s.at(i, u), :, :]

            def store(i, u):
                P_e6s.wait(sp, "out", P_e6s.at(i, u))
                yield X3S[P_e6s.at(i, u), :, :], P_e6s.B["o0"][:, u, :]
            run_groups(P_e6s, load, store)
            P_e6s.all_done(sp)

            def node2(P, first):
                def load(i, u):
                    P.free(sp, "vec", i, u)
                    yield P.B["in0"][:, u, :], X2[P.at(i, u) + first, :, :]

                def store(i, u):
                    P.wait(sp, "evrow", P.at(i, u))
                    yield out.rearrange("(k p t) f -> k p (t f)", p=TILE, t=TILES)[P.at(i, u) + first, :, :], flat(u)
                run_groups(P, load, store)
                P.all_done(sp)
            node2(P_node2, 0)

            def load(i, u):
                n = P_e7.at(i, u)
                P_e7.free(sp, "out", i, u)
                gathered(sp, "ov3", i, u)
                yield rows_in[0][:, u, :, :].rearrange("p t f -> p (t f)"), OV[3][n, :, :]
                yield P_e7.B["in0"][:, u, :], X3S[n, :, :]
                yield P_e7.B["in1"][:, u, :], X3D[n, :, :]
                yield from factors(P_e7, "e7", u, n)

            def store(i, u):
                n = P_e7.at(i, u)
                P_e7.wait(sp, "act", n)
                yield QS[n, :, :], P_e7.B["o1"][:, u, :]
                P_e7.wait(sp, "out", n)
                yield QD[n, :, :], P_e7.B["o0"][:, u, :]
                P_e7.wait(sp, "evrow", n)
                yield table(4, n), flat(u)
            run(P_e7, load, store)
            P_e7.all_done(sp)

            node2(P_node2b, NODE2_EARLY)

            def load(i, u):
                n = P_e8.at(i, u)
                P_e8.free(sp, "add", i, u)
                gathered(sp, "ov4", i, u)
                yield rows_in[0][:, u, :, :].rearrange("p t f -> p (t f)"), OV[4][n, :, :]
                yield P_e8.B["in0"][:, u, :], QS[n, :, :]
                yield P_e8.B["in1"][:, u, :], X3D[n, :, :]
                yield P_e8.B["in2"][:, u, :], QD[n, :, :]
                yield from factors(P_e8, "e8", u, n)

            run(P_e8, load, lambda i, u: ())
            for u in range(4):
                sp.wait_ge(s_final[u], FOURS.in_slot(u) * 16 * TILES)

        @block.gpsimd
        def _(po):
            po.memset(ident[:, :], 0.0).then_inc(s_const, 1)
            po.memset(HALF[:, :], 0.0).then_inc(s_const, 1)
            po.wait_ge(s_const, 2)
            po.affine_select(out=ident[:, :], in_=ident[:, :], compare_op=ALU.not_equal, fill=1.0, base=0,
                             pattern=[[-1, 128]], channel_multiplier=1).then_inc(s_const, 1)
            for k, base in enumerate((0, 64, -64)):
                po.affine_select(out=HALF[:, :], in_=HALF[:, :], compare_op=ALU.not_equal, fill=0.5, base=base,
                                 pattern=[[-1, 128]], channel_multiplier=1).then_inc(s_const, 1)
                po.wait_ge(s_const, 4 + k)
            po.iota(row_no[:, :].rearrange("p (k t) -> p k t", t=TILES), pattern=[[PACK, BLOCKS], [1, TILES]],
                    base=0, channel_multiplier=TILES).then_inc(s_iota, 1)
            po.wait_ge(s_iota, 1)
            po.tensor_copy(slot_rows[:, :, 0].bitcast(I32), row_no[:, :]).then_inc(s_iota, 1)
            po.memset(slot_rows[:, :, 1], 0.0).then_inc(s_iota, 1)
            po.memset(slot_rows[:, :, 3], 0.0).then_inc(s_iota, 1)
            po.wait_ge(s_iota, 4)
            sems.passed[id(po)] = s_passed_pool
            po.wait_ge(s_flag, 2)
            unsorted = po.value_load(flag[0:1, 0:1])
            with po.If(unsorted > 0):
                po.iota(no_i, pattern=[[1, KEYS]], base=0, channel_multiplier=0).then_inc(s_numbered, 1)
                po.iota(own_no, pattern=[[1, PER]], base=0, channel_multiplier=PER).then_inc(s_numbered, 1)
                po.wait_ge(s_ranked, 4)
                with po.Fori(0, BLOCKS) as i:
                    po.dma_start(gat[:, 0, :, :], ea_in.rearrange("(p t) f -> p t f", p=TILE)[:, bass.ds(i * TILES, TILES), :])\
                      .then_inc(s_ea_in, 16)
                    po.tensor_copy(gidx[:, 0, :], rank_i[:, bass.ds(i * TILES, TILES)]).then_inc(s_rank_copy, 1)
                    po.tensor_copy(grow[:, 0, :, :], meta[:, bass.ds(i * TILES, TILES), :]).then_inc(s_rank_copy, 1)
                    sems.wait(po, s_ea_in, i * 16 + 16)
                    sems.wait(po, s_rank_copy, i * 2 + 2)
                    for t in range(TILES):
                        for table, rows in ((EA_S, gat[:, 0, t, :]), (META_S, grow[:, 0, t, :])):
                            po.indirect_dma_start(
                                table, bass.IndirectOffsetOnAxis(ap=gidx[:, 0, t:t + 1], axis=0),
                                rows, None, bounds_check=EDGES + 1, oob_is_err=False).then_inc(s_sorted, 16)
                    sems.wait(po, s_sorted, i * (TILES * 32) + TILES * 32)
            po.end_ifs()
            po.wait_ge(s_idx, 4)

            copies = [0]

            def gather_pass(name, index, source, rows, bound, target, backwards=False):
                base = copies[0]
                skips = name.startswith("ov")

                def body(i, us):
                    pairs = [(half, us[2 * half:2 * half + 2]) for half in (0, 1) if us[2 * half:2 * half + 2]]
                    dst = grow if target is None else gat

                    def lowest(half, slots):
                        n = 4 * i + 2 * half
                        return BLOCKS - n - len(slots) if backwards else n

                    for half, slots in pairs:
                        pair = 2 * i + half
                        slot = slice(2 * half, 2 * half + len(slots))
                        if not (isinstance(i, int) and i == 0):
                            if target is None:
                                sems.wait(po, s_info, pair - 1)
                            else:
                                sems.wait(po, s_gstore[half], store_base(name, half) + i * 16)
                        po.tensor_copy(gidx[:, slot, :].rearrange("p u t -> p (u t)"),
                                       index(lowest(half, slots), len(slots))).then_inc(s_gcopy, 1)
                        if skips:
                            po.memset(dst[:, slot, :, :], 0.0).then_inc(s_gcopy, 1)
                        sems.wait(po, s_gcopy, base + (pair + 1) * (2 if skips else 1))
                        for u in slots:
                            for t in range(TILES):
                                at = t if target is None else 2 * (t % 4) + t // 4
                                po.indirect_dma_start(
                                    dst[:, u, at, :], None, source,
                                    bass.IndirectOffsetOnAxis(ap=gidx[:, u, t:t + 1], axis=0),
                                    bounds_check=bound, oob_is_err=False).then_inc(s_gather[half], 16)
                    for half, slots in pairs:
                        slot = slice(2 * half, 2 * half + len(slots))
                        sems.wait(po, s_gather[half],
                                  gather_base(name, half) + i * (32 * TILES) + 16 * TILES * len(slots))
                        block0 = lowest(half, slots)
                        if target is None:
                            po.tensor_copy(src_info[:, bass.ds(block0 * TILES, len(slots) * TILES), :],
                                           grow[:, slot, :, :].rearrange("p u t c -> p (u t) c")).then_inc(s_info, 1)
                        else:
                            po.dma_start(target[bass.ds(block0, len(slots)), :, :].rearrange("u p c -> p u c"),
                                         gat[:, slot, :, :].rearrange("p u t f -> p u (t f)"))\
                              .then_inc(s_gstore[half], 16)
                in_groups(po, FOURS, body)
                copies[0] += (2 if skips else 1) * PAIRS_OF_BLOCKS

            def all_stored(name):
                for half in (0, 1):
                    po.wait_ge(s_gstore[half], store_base(name, half) + pairs_in(half) * 16)

            gather_pass("xd", lambda k, m: idx_dst[:, bass.ds(k * TILES, m * TILES)], x, D, NODES - 1, XDR)
            all_stored("xd")
            po.wait_ge(s_def, 16)
            base = copies[0]

            def body(i, us):
                for u in us:
                    n = 2 * i + u
                    if not (isinstance(i, int) and i == 0):
                        sems.wait(po, s_scatter[u], i * (16 * TILES))
                    po.tensor_copy(gidx[:, u, :], idx_last[:, bass.ds(n * TILES, TILES)]).then_inc(s_gcopy, 1)
                    po.tensor_copy(grow[:, u, :, :], slot_rows[:, bass.ds(n * TILES, TILES), :]).then_inc(s_gcopy, 1)
                    sems.wait(po, s_gcopy, base + n * 2 + 2)
                    for t in range(TILES):
                        po.indirect_dma_start(
                            SLOTS, bass.IndirectOffsetOnAxis(ap=gidx[:, u, t:t + 1], axis=0),
                            grow[:, u, t, :], None, bounds_check=NODES - 1, oob_is_err=False)\
                          .then_inc(s_scatter[u], 16)
            in_groups(po, PAIRS, body)
            copies[0] += 2 * BLOCKS
            for u in (0, 1):
                po.wait_ge(s_scatter[u], per_slot[u] * 16 * TILES)
            gather_pass("info", lambda k, m: idx_src[:, bass.ds(k * TILES, m * TILES)], SLOTS, 4, NODES - 1, None)
            gather_pass("xs", lambda k, m: idx_src[:, bass.ds(k * TILES, m * TILES)], x, D, NODES - 1, XSR)
            all_stored("xs")
            for t, (P, back) in enumerate(((P_e0, False), (P_e1, True), (P_e4, False), (P_e6, False), (P_e7, False))):
                P.all_done(po)
                gather_pass(f"ov{t}", lambda k, m: src_info[:, bass.ds(k * TILES, m * TILES), 0].bitcast(I32),
                            TAB[t], D, EDGES - 1, OV[t], back)
                all_stored(f"ov{t}")
            P_node2.all_done(po)
            P_node2b.all_done(po)
            base = copies[0]

            def body(i, us):
                for u in us:
                    n = 4 * i + u
                    scattered(po, i, u)
                    po.tensor_copy(gidx[:, u, :], idx_last[:, bass.ds(n * TILES, TILES)]).then_inc(s_gcopy, 1)
                    sems.wait(po, s_gcopy, base + n + 1)
                    P_e8.wait(po, "evrow", n)
                    for t in range(TILES):
                        po.indirect_dma_start(
                            out, bass.IndirectOffsetOnAxis(ap=gidx[:, u, t:t + 1], axis=0),
                            rows_out[:, u, t, :], None, bounds_check=NODES - 1, oob_is_err=False)\
                          .then_inc(s_final[u], 16)
            in_groups(po, FOURS, body)

        def at_bank(P, u, k):
            return bank[8 // P.slots * u + k][:, 0:COLS]

        @block.tensor
        def _(pe):
            mm = nc.tensor.matmul

            def to_features(dst, rows):
                rows = rows.rearrange("p t f -> p (t f)")
                for j in range(4):
                    last = nc.tensor.transpose(dst[:, TILE * j:TILE * j + TILE], rows[:, 128 * j:128 * j + 128],
                                               ident[0:TILE, 0:TILE])
                return last

            def to_rows(dst, value):
                for j in range(4):
                    last = nc.tensor.transpose(dst[0:TILE, 128 * j:128 * j + 128], value[:, TILE * j:TILE * j + TILE],
                                               ident[:, :])
                return last

            def acc(dst, *pairs):
                for k, (w, v) in enumerate(pairs):
                    last = mm(dst, w, v, start=(k == 0), stop=(k == len(pairs) - 1))
                return last

            def one(dst, w, v):
                return mm(dst, w, v, start=True, stop=True)

            def hidden(P, u, buf):
                for h, name in enumerate(("w1a", "w1b")):
                    rows = slice(64 * h, 64 * h + 64)
                    last = one(at_bank(P, u, h), M[name][rows, :], P.B[buf][rows, u, :])
                return last

            def back(P, u, k, wa, wb, a, b, more=False):
                for h, name, buf in ((0, wa, a), (1, wb, b)):
                    rows = slice(64 * h, 64 * h + 64)
                    last = mm(at_bank(P, u, k)[rows, :], M[name][:, rows], P.B[buf][:, u, :], start=not more, stop=True)
                return last

            pe.wait_ge(s_const, 6)
            pe.wait_ge(s_setup, 3)
            one(bank[5][0:1, 0:1], viol[:, :], carry_in[:, :]).then_inc(s_flag, 1)
            pe.wait_ge(s_setup, SETUP_SCAN)
            one(bank[2][0:1, 0:NAT], nat[:, 8, 249:250], ident[0:NAT, 0:NAT])
            one(bank[3][0:1, 0:NAT], nat[:, 9, 249:250], ident[0:NAT, 0:NAT]).then_inc(s_pe_small, 1)
            pe.wait_ge(s_setup, SETUP_CARRY)
            one(bank[4][0:NAT, 0:1], tiny[:, 3, :], ident[0:1, 0:1]).then_inc(s_pe_small, 1)
            pe.wait_ge(s_setup, SETUP_ROWS)
            for q, k in enumerate((1, 3, 5, 10)):
                for par in (0, 1):
                    last = one(bank[q][0:TILE, 128 * par:128 * par + NAT], nat[:, k, TILE * par:TILE * par + TILE],
                               ident[0:NAT, 0:NAT])
            last.then_inc(s_tcol, 1)
            pe.wait_ge(s_ccol, 8)
            pe.wait_ge(s_w, WEIGHT_DMAS * 16)
            one(bank[0][:, 0:64], w2t_sb[:, :], C[0:64, 0:64])
            one(bank[1][:, 0:1], C[:, :], K["b2"]).then_inc(s_pe_small, 1)
            pe.wait_ge(s_dconst, CONST_END)

            def node0(P, with_g):
                def body(i, us):
                    for u in us:
                        P.landed(pe, "ld", i, u)
                        P.free(pe, "evs" if with_g else "out", i, u)
                        hidden(P, u, "in0").then_inc(P.s("hid"), 1)
                    for u in us:
                        P.wait(pe, "relu0", P.at(i, u))
                        P.wait(pe, "relu1", P.at(i, u))
                        mm(at_bank(P, u, 0), C[:, :], P.B["in0"][:, u, :], start=True, stop=False)
                        back(P, u, 0, "w2ca", "w2cb", "a", "b", more=True).then_inc(P.s("y"), 1)
                    for u in us:
                        variance(P, i, u, 1)
                    if with_g:
                        for u in us:
                            P.wait(pe, "out", P.at(i, u))
                            back(P, u, 0, "w2a", "w2b", "a", "b").then_inc(P.s("g"), 1)
                in_groups(pe, P, body)
                P.all_done(pe)

            def variance(P, i, u, k, sq="sq", var="var", lnv="lnv", buf="c"):
                P.free(pe, lnv, i, u)
                P.wait(pe, sq, P.at(i, u))
                one(at_bank(P, u, k), J[:, :], P.B[buf][:, u, :]).then_inc(P.s(var), 1)

            def rows_of(P, i, u, k, buf="o0", done="out"):
                P.free(pe, "evrow", i, u)
                P.wait(pe, done, P.at(i, u))
                to_rows(bank[8 // P.slots * u + k], P.B[buf][:, u, :]).then_inc(P.s("row"), 1)

            node0(P_node0, False)

            pe.wait_ge(s_info, PAIRS_OF_BLOCKS)
            for q, k in enumerate((1, 2)):
                for par in (0, 1):
                    last = one(bank[q][0:NAT, 128 * par:128 * par + TILE], src_info[:, par::2, k],
                               ident[0:TILE, 0:TILE])
            last.then_inc(s_pe_small, 1)
            pe.wait_ge(s_info, INFO_ROWS)

            def tr(i, u):
                P_e0.landed(pe, "ld", i, u)
                P_e0.free(pe, "evrow", i, u)
                P_e0.free(pe, "out", i, u)
                to_features(at_bank(P_e0, u, 0), rows_in[0][:, u])
                to_features(at_bank(P_e0, u, 1), rows_in[1][:, u]).then_inc(P_e0.s("tr"), 1)

            def hid(i, u):
                P_e0.wait(pe, "vec", P_e0.at(i, u))
                hidden(P_e0, u, "b").then_inc(P_e0.s("hid"), 1)

            def g(i, u):
                P_e0.wait(pe, "relu0", P_e0.at(i, u))
                P_e0.wait(pe, "relu1", P_e0.at(i, u))
                back(P_e0, u, 0, "w2a", "w2b", "c", "d").then_inc(P_e0.s("g"), 1)

            def rows(i, u):
                rows_of(P_e0, i, u, 1)

            in_turn(pe, P_e0, [(0, tr), (1, hid), (2, g), (3, rows)])
            P_e0.all_done(pe)

            node0(P_node0e, True)

            def tr(i, u):
                P_e1.landed(pe, "ld", i, u)
                P_e1.free(pe, "lnv", i, u)
                to_features(at_bank(P_e1, u, 0), rows_in[0][:, u]).then_inc(P_e1.s("tr"), 1)

            def y(i, u):
                P_e1.free(pe, "evrow", i, u)
                P_e1.wait(pe, "vec", P_e1.at(i, u))
                one(at_bank(P_e1, u, 1), C[:, :], P_e1.B["c"][:, u, :]).then_inc(P_e1.s("y"), 1)

            def var(i, u):
                variance(P_e1, i, u, 0, buf="d")

            def rows(i, u):
                rows_of(P_e1, i, u, 1)

            in_turn(pe, P_e1, [(0, tr), (1, y), (1, var), (2, rows)])
            P_e1.all_done(pe)

            def tr(i, u):
                P_e2.landed(pe, "ld", i, u)
                P_e2.free(pe, "evf", i, u)
                P_e2.free(pe, "evc", i, u)
                to_features(at_bank(P_e2, u, 0), rows_in[0][:, u])
                to_features(at_bank(P_e2, u, 1), rows_in[1][:, u]).then_inc(P_e2.s("tr"), 1)

            def t(i, u):
                n = P_e2.at(i, u)
                P_e2.wait(pe, "evs", n)
                P_e2.wait(pe, "msg", n)
                P_e2.wait(pe, "scan", n)
                for k, part in ((0, "f"), (1, "c")):
                    last = acc(at_bank(P_e2, u, k), (M["src" + part], P_e2.B["o3"][:, u, :]), (M["dst" + part], P_e2.B["o0"][:, u, :]),
                               (M["nbr" + part], P_e2.B["a"][:, u, :]))
                last.then_inc(P_e2.s("t"), 1)

            in_turn(pe, P_e2, [(0, tr), (1, t)])
            P_e2.all_done(pe)

            def halves_mean(want, k0, k1):
                pe.wait_ge(s_dv_small, want)
                one(bank[0][:, 0:2 * (k1 - k0)], HALF[:, :], mom[:, k0:k1, :].rearrange("p k c -> p (k c)"))\
                    .then_inc(s_pe_small, 1)

            halves_mean(STATS1, 0, 2)
            P_e3.all_done(pe)
            halves_mean(STATS2, 0, 1)
            pe.wait_ge(s_dv_small, STATS2B)
            one(bank[1][:, 0:1], C[:, :], K["t2"]).then_inc(s_pe_small, 1)

            def plain_ln(P, last=None, first=None):
                def body(i, us):
                    if first:
                        for u in us:
                            first(i, u)
                    for u in us:
                        P.free(pe, {"rows": "evrow", "h": "bnf", None: "out"}[last], i, u)
                        P.wait(pe, "vec", P.at(i, u))
                        one(at_bank(P, u, 0), C[:, :], P.B["c"][:, u, :]).then_inc(P.s("y"), 1)
                    for u in us:
                        variance(P, i, u, 1, buf="d")
                    for u in us:
                        if last == "rows":
                            rows_of(P, i, u, 0)
                        if last == "h":
                            P.wait(pe, "out", P.at(i, u))
                            one(at_bank(P, u, 0), M["wl2"], P.B["o0"][:, u, :]).then_inc(P.s("h"), 1)
                in_groups(pe, P, body)
                P.all_done(pe)

            plain_ln(P_e4, "rows")
            plain_ln(P_node1, "h")
            plain_ln(P_node1e)

            def tr(i, u):
                P_e5.landed(pe, "ld", i, u)
                P_e5.free(pe, "evs", i, u)
                to_features(at_bank(P_e5, u, 0), rows_in[0][:, u]).then_inc(P_e5.s("tr"), 1)

            def h(i, u):
                P_e5.free(pe, "mask", i, u)
                P_e5.wait(pe, "vec", P_e5.at(i, u))
                one(at_bank(P_e5, u, 0), M["wl2"], P_e5.B["b"][:, u, :])
                one(at_bank(P_e5, u, 1), M["wl2"], P_e5.B["in2"][:, u, :]).then_inc(P_e5.s("h"), 1)

            in_turn(pe, P_e5, [(0, tr), (1, h)])
            P_e5.all_done(pe)
            halves_mean(STATS3, 0, 3)

            plain_ln(P_e6, "rows")

            def first_h(P):
                def first(i, u):
                    P.landed(pe, "ld", i, u)
                    P.free(pe, "out", i, u)
                    one(at_bank(P, u, 0), M["wl2"], P.B["in0"][:, u, :]).then_inc(P.s("h"), 1)
                return first
            plain_ln(P_e6s, first=first_h(P_e6s))

            def node2(P):
                def h(i, u):
                    P.landed(pe, "ld", i, u)
                    one(at_bank(P, u, 0), M["wl2"], P.B["in0"][:, u, :]).then_inc(P.s("h"), 1)

                def body(i, us, more):
                    for u in us:
                        P.free(pe, "evrow", i, u)
                        P.wait(pe, "vec", P.at(i, u))
                        one(at_bank(P, u, 1), C[:, :], P.B["b"][:, u, :]).then_inc(P.s("y"), 1)
                    for u in us:
                        variance(P, i, u, 0, buf="d")
                    for u in us:
                        P.wait(pe, "out", P.at(i, u))
                        one(at_bank(P, u, 0), M["w31"], P.B["o0"][:, u, :]).then_inc(P.s("hid"), 1)
                    for u in us:
                        P.wait(pe, "relu0", P.at(i, u))
                        one(at_bank(P, u, 1), M["w32"], P.B["a"][:, u, :]).then_inc(P.s("g"), 1)
                    if more:
                        for u in us:
                            h(i + 1, u)
                    for u in us:
                        if more:
                            P.wait(pe, "act", P.at(i + 1, u))
                        P.wait(pe, "add", P.at(i, u))
                        one(at_bank(P, u, 0), C[:, :], P.B["o0"][:, u, :]).then_inc(P.s("y2"), 1)
                    for u in us:
                        variance(P, i, u, 1, "sq2", "var2", "lnv2", "g")
                    for u in us:
                        rows_of(P, i, u, 0, "o1", "out2")
                in_groups_ahead(pe, P, h, body)
                P.all_done(pe)
            node2(P_node2)

            P = P_e7

            def tr(i, u):
                n = P_e7.at(i, u)
                P_e7.landed(pe, "ld", i, u)
                P_e7.free(pe, "out", i, u)
                to_features(at_bank(P_e7, u, 0), rows_in[0][:, u]).then_inc(P_e7.s("tr"), 1)

            def hid(i, u):
                n = P_e7.at(i, u)
                P_e7.free(pe, "evrow", i, u)
                P_e7.wait(pe, "msg", n, 1 + 1)
                one(at_bank(P_e7, u, 1), M["w31"], P_e7.B["a"][:, u, :])
                one(at_bank(P_e7, u, 0), M["w31"], P_e7.B["in1"][:, u, :]).then_inc(P_e7.s("hid"), 1)

            def g(i, u):
                n = P_e7.at(i, u)
                P_e7.wait(pe, "relu0", n)
                one(at_bank(P_e7, u, 1), M["w32"], P_e7.B["d"][:, u, :]).then_inc(P_e7.s("g"), 1)

            def h(i, u):
                n = P_e7.at(i, u)
                P_e7.wait(pe, "relu1", n)
                one(at_bank(P_e7, u, 0), M["w32"], P_e7.B["h"][:, u, :]).then_inc(P_e7.s("h"), 1)

            def rows(i, u):
                P_e7.wait(pe, "act", P_e7.at(i, u))
                rows_of(P_e7, i, u, 1)

            in_turn(pe, P_e7, [(0, tr), (2, h), (1, g), (0, hid), (3, rows)])
            P.all_done(pe)

            node2(P_node2b)
            P = P_e8

            def tr(i, u):
                P_e8.landed(pe, "ld", i, u)
                P_e8.free(pe, "lnv", i, u)
                to_features(at_bank(P_e8, u, 0), rows_in[0][:, u]).then_inc(P_e8.s("tr"), 1)

            def y(i, u):
                P_e8.free(pe, "evrow", i, u)
                P_e8.wait(pe, "add", P_e8.at(i, u))
                one(at_bank(P_e8, u, 1), C[:, :], P_e8.B["f"][:, u, :]).then_inc(P_e8.s("y"), 1)

            def var(i, u):
                variance(P_e8, i, u, 0, buf="d")

            def rows(i, u):
                rows_of(P_e8, i, u, 1)

            in_turn(pe, P_e8, [(0, tr), (2, y), (2, var), (3, rows)])

        @block.scalar
        def _(ac):
            act = nc.scalar.activation

            def square(P, i, u, k, bias, buf="c", y="y", sq="sq", var="var"):
                P.free(ac, var, i, u)
                P.wait(ac, y, P.at(i, u))
                act(P.B[buf][:, u, :], at_bank(P, u, k), ACT.Square, bias=bias).then_inc(P.s(sq), 1)

            def rstd(P, i, u, k, buf="g", var="var", lnv="lnv", name="rstd", read="out"):
                P.free(ac, read, i, u)
                P.wait(ac, var, P.at(i, u))
                act(P.B[buf][:, u, :], at_bank(P, u, k), ACT.Ln, bias=K["eps"]).then_inc(P.s(lnv), 1)
                P.wait(ac, lnv, P.at(i, u))
                act(P.B[buf][:, u, :], P.B[buf][:, u, :], ACT.Exp, scale=-0.5).then_inc(P.s(name), 1)

            def small_rstd(want, col):
                ac.wait_ge(s_dv_small, want)
                act(col, col, ACT.Ln, bias=K["eps"]).then_inc(s_ac_small, 1)
                small[0] += 2
                ac.wait_ge(s_ac_small, small[0] - 1)
                act(col, col, ACT.Exp, scale=-0.5).then_inc(s_ac_small, 1)

            small = [0]

            def rows_evac(P, i, u, k, stored=True):
                if stored:
                    P.stored(ac, "st", i, u)
                P.wait(ac, "row", P.at(i, u))
                act(rows_out[:, u, :, :].rearrange("p (h j) f -> p j h f", h=2),
                    bank[8 // P.slots * u + k][0:TILE, :].rearrange("p (j h f) -> p j h f", j=4, h=2), ACT.Copy)\
                    .then_inc(P.s("evrow"), 1)

            def sigmoid_log(P, i, u, out, z):
                n = P.at(i, u)
                P.free(ac, "sig", i, u)
                P.wait(ac, "nabs", n)
                act(out, z, ACT.Exp).then_inc(P.s("lsig"), 1)
                P.wait(ac, "lsig", n, 1)
                act(out, out, ACT.Ln, bias=1.0).then_inc(P.s("lsig"), 1)

            def sigmoid_end(P, i, u, out, arg, used):
                P.free(ac, used, i, u)
                P.wait(ac, "arg", P.at(i, u))
                act(out, arg, ACT.Exp).then_inc(P.s("sig"), 1)

            def node0(P, with_g):
                def body(i, us):
                    for u in us:
                        P.free(ac, "y", i, u)
                        if with_g:
                            P.free(ac, "g", i, u)
                        P.wait(ac, "hid", P.at(i, u))
                        act(P.B["a"][:, u, :], at_bank(P, u, 0), ACT.Relu, bias=K["b1"]).then_inc(P.s("relu0"), 1)
                    for u in us:
                        square(P, i, u, 0, K["cb2"])
                    for u in us:
                        rstd(P, i, u, 1)
                    if with_g:
                        for u in us:
                            P.stored(ac, "st", i, u)
                            P.wait(ac, "g", P.at(i, u))
                            act(P.B["o1"][:, u, :], at_bank(P, u, 0), ACT.Copy).then_inc(P.s("evs"), 1)
                in_groups(ac, P, body)
                P.all_done(ac)

            ac.preload_act_table_set("natural_log_exp_and_others")
            ac.wait_ge(s_setup, SETUP_CARRY + 2)
            act(nat[:, 10, :], nat[:, 7, :], ACT.Ln, bias=1.0).then_inc(s_setup, 1)
            ac.wait_ge(s_setup, SETUP_CARRY + 3)
            act(nat[:, 10, :], nat[:, 10, :], ACT.Exp, scale=-0.5).then_inc(s_setup, 1)
            ac.wait_ge(s_dconst, CONST_END)
            node0(P_node0, False)

            def ev(i, u):
                P_e0.stored(ac, "st", i, u)
                P_e0.wait(ac, "tr", P_e0.at(i, u))
                act(P_e0.B["o1"][:, u, :], at_bank(P_e0, u, 0), ACT.Copy).then_inc(P_e0.s("evs"), 1)

            def relu(i, u):
                P_e0.free(ac, "g", i, u)
                P_e0.wait(ac, "hid", P_e0.at(i, u))
                act(P_e0.B["c"][:, u, :], at_bank(P_e0, u, 0), ACT.Relu, bias=K["b1"]).then_inc(P_e0.s("relu0"), 1)

            def evrow(i, u):
                rows_evac(P_e0, i, u, 1)

            in_turn(ac, P_e0, [(0, ev), (1, relu), (3, evrow)])
            P_e0.all_done(ac)

            node0(P_node0e, True)

            def sq(i, u):
                square(P_e1, i, u, 1, K["cb2"], "d")

            def root(i, u):
                rstd(P_e1, i, u, 0)

            def evrow(i, u):
                rows_evac(P_e1, i, u, 1)

            in_turn(ac, P_e1, [(1, sq), (1, root), (2, evrow)])
            P_e1.all_done(ac)

            def ea_rows(i, u):
                P_e2.free(ac, "t", i, u)
                P_e2.wait(ac, "tr", P_e2.at(i, u))
                act(P_e2.B["a"][:, u, :], at_bank(P_e2, u, 1), ACT.Copy).then_inc(P_e2.s("evs"), 1)

            def ev(i, u):
                P_e2.stored(ac, "st", i, u)
                P_e2.wait(ac, "t", P_e2.at(i, u))
                act(P_e2.B["o1"][:, u, :], at_bank(P_e2, u, 0), ACT.Identity, bias=K["bf"]).then_inc(P_e2.s("evf"), 1)
                act(P_e2.B["o2"][:, u, :], at_bank(P_e2, u, 1), ACT.Identity, bias=K["bc"]).then_inc(P_e2.s("evc"), 1)

            in_turn(ac, P_e2, [(0, ea_rows), (1, ev)])
            P_e2.all_done(ac)
            small_rstd(STATS1 + 3, K["tmp1"])
            small_rstd(STATS1 + 8, K["tmp1"])
            ac.wait_ge(s_dv_small, STATS1B)

            def logs(i, u):
                n = P_e3.at(i, u)
                P_e3.landed(ac, "ld", i, u)
                P_e3.free(ac, "vec", i, u)
                act(P_e3.B["b"][:, u, :], P_e3.B["in1"][:, u, :], ACT.Abs, scale=K["s1c"], bias=K["t1c"]).then_inc(P_e3.s("act"), 1)
                P_e3.wait(ac, "act", n, 1)
                act(P_e3.B["c"][:, u, :], P_e3.B["b"][:, u, :], ACT.Exp, scale=-1.0).then_inc(P_e3.s("act"), 1)
                P_e3.wait(ac, "act", n, 2)
                act(P_e3.B["d"][:, u, :], P_e3.B["c"][:, u, :], ACT.Ln, bias=1.0).then_inc(P_e3.s("act"), 1)
                sigmoid_log(P_e3, i, u, P_e3.B["a"][:, u, :], P_e3.B["g2"][:, u, :])

            def end(i, u):
                sigmoid_end(P_e3, i, u, P_e3.B["in4"][:, u, :], P_e3.B["in3"][:, u, :], "vec")

            in_turn(ac, P_e3, [(1, end), (0, logs)])
            P_e3.all_done(ac)
            small_rstd(STATS2 + 3, K["tmp1"])
            ac.wait_ge(s_dv_small, STATS2C)

            def soft(P, source, ready, rows=None):
                def body(i, us):
                    for u in us:
                        n = P.at(i, u)
                        ready(i, u)
                        P.free(ac, "vec", i, u)
                        act(P.B["a"][:, u, :], P.B[source][:, u, :], ACT.Abs, bias=K["t2"]).then_inc(P.s("act"), 1)
                        P.wait(ac, "act", n, 1)
                        act(P.B["a"][:, u, :], P.B["a"][:, u, :], ACT.Exp, scale=-1.0).then_inc(P.s("act"), 1)
                        P.wait(ac, "act", n, 2)
                        act(P.B["a"][:, u, :], P.B["a"][:, u, :], ACT.Ln, bias=1.0).then_inc(P.s("act"), 1)
                    for u in us:
                        square(P, i, u, 0, K["ct2"], "d")
                    for u in us:
                        rstd(P, i, u, 1)
                    if rows:
                        for u in us:
                            rows_evac(P, i, u, 0)
                in_groups(ac, P, body)
                P.all_done(ac)
            soft(P_e4, "e", lambda i, u: P_e4.wait(ac, "msg", P_e4.at(i, u)), True)
            soft(P_node1, "in0", lambda i, u: P_node1.landed(ac, "ld", i, u))
            soft(P_node1e, "in0", lambda i, u: P_node1e.landed(ac, "ld", i, u))

            def ev(i, u):
                P_e5.stored(ac, "st", i, u)
                P_e5.wait(ac, "h", P_e5.at(i, u))
                act(P_e5.B["o1"][:, u, :], at_bank(P_e5, u, 0), ACT.Copy).then_inc(P_e5.s("evs"), 1)

            in_turn(ac, P_e5, [(1, ev)])
            P_e5.all_done(ac)
            small_rstd(STATS3 + 5, K["tmp1"])
            ac.wait_ge(s_dv_small, STATS3B)

            def relu_bn(P, source, ready, rows=None):
                def body(i, us):
                    for u in us:
                        ready(i, u)
                        P.free(ac, "vec", i, u)
                        act(P.B["a"][:, u, :], source(u), ACT.Relu, scale=K["s3"], bias=K["t3"]).then_inc(P.s("act"), 1)
                    for u in us:
                        square(P, i, u, 0, 0.0, "d")
                    for u in us:
                        rstd(P, i, u, 1)
                    if rows:
                        for u in us:
                            rows_evac(P, i, u, 0)
                in_groups(ac, P, body)
                P.all_done(ac)
            relu_bn(P_e6, lambda u: P_e6.B["in0"][:, u, :], lambda i, u: P_e6.landed(ac, "ld", i, u), True)
            relu_bn(P_e6s, lambda u: at_bank(P_e6s, u, 0), lambda i, u: P_e6s.wait(ac, "h", P_e6s.at(i, u)))

            def node2(P):
                def relu(i, u):
                    P.wait(ac, "h", P.at(i, u))
                    P.free(ac, "vec", i, u)
                    act(P.B["b"][:, u, :], at_bank(P, u, 0), ACT.Relu, scale=K["s3"], bias=K["t3"]).then_inc(P.s("act"), 1)

                def body(i, us, more):
                    for u in us:
                        square(P, i, u, 1, 0.0, "d")
                    for u in us:
                        rstd(P, i, u, 0, "h")
                    for u in us:
                        sigmoid_log(P, i, u, P.B["in1"][:, u, :], P.B["in1"][:, u, :])
                    if more:
                        for u in us:
                            relu(i + 1, u)
                    for u in us:
                        sigmoid_end(P, i, u, P.B["e"][:, u, :], P.B["e"][:, u, :], "add")
                    for u in us:
                        square(P, i, u, 0, 0.0, "g", "y2", "sq2", "var2")
                    for u in us:
                        rstd(P, i, u, 1, "c", "var2", "lnv2", "rstd2", "out2")
                    for u in us:
                        rows_evac(P, i, u, 0)
                in_groups_ahead(ac, P, relu, body)
                P.all_done(ac)
            node2(P_node2)

            P = P_e7

            def ev(i, u):
                n = P_e7.at(i, u)
                P_e7.wait(ac, "hid", n)
                P_e7.free(ac, "vec", i, u)
                act(P_e7.B["b"][:, u, :], at_bank(P_e7, u, 1), ACT.Identity, bias=K["b31"]).then_inc(P_e7.s("evs"), 1)
                P_e7.stored(ac, "st", i, u)
                act(P_e7.B["c"][:, u, :], at_bank(P_e7, u, 0), ACT.Identity, bias=K["b31"]).then_inc(P_e7.s("evd"), 1)
                P_e7.free(ac, "g", i, u)
                act(P_e7.B["d"][:, u, :], at_bank(P_e7, u, 1), ACT.Relu, bias=K["b31"]).then_inc(P_e7.s("relu0"), 1)

            def end(i, u):
                P_e7.wait(ac, "g", P_e7.at(i, u))
                act(P_e7.B["o1"][:, u, :], at_bank(P_e7, u, 1), ACT.Identity, bias=K["b32"]).then_inc(P_e7.s("act"), 1)

            def evrow(i, u):
                rows_evac(P_e7, i, u, 1)

            in_turn(ac, P_e7, [(1, end), (3, evrow), (0, ev)])
            P.all_done(ac)

            node2(P_node2b)
            P = P_e8

            def log(i, u):
                sigmoid_log(P_e8, i, u, P_e8.B["o1"][:, u, :], P_e8.B["o1"][:, u, :])

            def end(i, u):
                sigmoid_end(P_e8, i, u, P_e8.B["in4"][:, u, :], P_e8.B["in3"][:, u, :], "add")

            def sq(i, u):
                square(P_e8, i, u, 1, 0.0, "d")

            def root(i, u):
                rstd(P_e8, i, u, 0, "g2")

            def evrow(i, u):
                scattered(ac, i, u)
                rows_evac(P_e8, i, u, 1, stored=False)

            in_turn(ac, P_e8, [(1, end), (2, sq), (2, root), (3, evrow), (0, log)])

        @block.vector
        def _(dv):
            v = nc.vector
            count = [0]

            def const(ins):
                ins.then_inc(s_dconst, 1)
                count[0] += 1
                dv.wait_ge(s_dconst, count[0])

            const(v.memset(mats[:, :, :], 0.0))
            const(v.memset(J[:, :], 0.0))
            v.memset(J[0:64, 0:64], 1.0 / D)
            v.memset(default[:, :, 0].bitcast(I32), SKIP)
            v.memset(default[:, :, 3], 0.0)
            const(v.memset(J[64:128, 64:128], 1.0 / D))
            v.memset(pad[:, :], -1.0)
            v.memset(carry_in[:, :], 1.0)
            const(v.memset(default[:, :, 1:3], 1.0))
            dv.wait_ge(s_const, 6)
            const(v.tensor_tensor(C[:, :], ident[:, :], J[:, :], ALU.subtract))
            v.memset(K["eps"], EPS)
            const(v.memset(carry[:, :], 0.0))

            def sort_edges():
                done = [0]

                def by_own(ins):
                    ins.then_inc(s_rank, 1)
                    done[0] += 1
                    dv.wait_ge(s_rank, done[0])

                dv.wait_ge(s_own, 48)
                dv.wait_ge(s_numbered, 2)
                by_own(v.tensor_copy(own_f[:, 0:2, :], own_i))
                by_own(v.tensor_copy(idx_f[:, :], own_no))
                v.memset(meta[:, :, 3], 0.0)
                by_own(v.memset(rank[:, :], 1.0))
                by_own(v.tensor_copy(no_f, no_i))
                for c in range(EDGES // KEYS):
                    dv.wait_ge(s_keys, 16 * c + 16)
                    by_own(v.tensor_copy(key_f, key_i))
                    dv.sem_inc(s_keys_used, 1)
                    base = done[0]
                    with dv.Fori(0, PER) as t:
                        def looped(k, ins):
                            ins.then_inc(s_rank, 1)
                            dv.wait_ge(s_rank, t * 6 + (base + k))
                        looped(1, v.tensor_copy(key_col[:, :], own_f[:, 0, bass.ds(t, 1)]))
                        looped(2, v.tensor_copy(edge_col[:, :], idx_f[:, bass.ds(t, 1)]))
                        looped(3, v.tensor_scalar(work, no_f, edge_col[:, 0:1], None, ALU.is_lt))
                        looped(4, v.scalar_tensor_tensor(out=work, in0=key_f, scalar=key_col[:, 0:1], in1=work,
                                                         op0=ALU.is_equal, op1=ALU.mult))
                        looped(5, v.scalar_tensor_tensor(out=work, in0=key_f, scalar=key_col[:, 0:1], in1=work,
                                                         op0=ALU.is_lt, op1=ALU.add))
                        looped(6, v.reduce_sum(part[:, bass.ds(t, 1)], work, mybir.AxisListType.X))
                    done[0] += PER * 6
                    by_own(v.tensor_tensor(rank[:, :], rank[:, :], part[:, :], ALU.add))
                    by_own(v.tensor_scalar(idx_f[:, :], idx_f[:, :], -float(KEYS), None, ALU.add))
                    by_own(v.memset(part[:, :], 0.0))
                assert done[0] == SORT_RANKED, done
                v.tensor_copy(rank_i[:, :], rank[:, :]).then_inc(s_ranked, 1)
                for k in range(3):
                    v.tensor_copy(meta[:, :, k], own_f[:, k, :]).then_inc(s_ranked, 1)
                dv.wait_ge(s_ranked, 4)
                dv.wait_ge(s_meta, 48)
                for k in range(3):
                    by_own(v.tensor_copy(nat[:, k, :], meta_in[:, k, 0::4]))
                by_own(v.tensor_copy(nat[:, 3, :], meta_in[:, 1, 1::4]))
                by_own(v.tensor_copy(nat[:, 11, :], meta_in[:, 1, 2::4]))

            steps = [0]

            def step(ins):
                ins.then_inc(s_setup, 1)
                steps[0] += 1
                dv.wait_ge(s_setup, steps[0])

            dv.wait_ge(s_nat, 5 * 16)
            step(v.tensor_copy(nat[:, 0:4, :], nat_i[:, :, :]))
            step(v.tensor_tensor(nat[:, 4, :], nat[:, 1, :], nat[:, 2, :], ALU.is_gt))
            step(v.reduce_sum(viol[:, :], nat[:, 4, :], mybir.AxisListType.X))
            dv.wait_ge(s_flag, 1)
            v.tensor_scalar(flag[:, :], bank[5][0:1, 0:1], 1.0, None, ALU.subtract).then_inc(s_flag, 1)
            dv.wait_ge(s_flag, 2)
            unsorted = dv.value_load(flag[0:1, 0:1])
            with dv.If(unsorted > 0):
                sort_edges()
            dv.end_ifs()
            dv.wait_ge(s_setup, 3)
            step(v.tensor_tensor(nat[:, 4, :], nat[:, 1, :], nat[:, 0, :], ALU.is_equal))
            step(v.tensor_tensor(nat[:, 5, :], nat[:, 1, :], nat[:, 2, :], ALU.not_equal))
            step(v.tensor_tensor(nat[:, 6, :], nat[:, 1, :], nat[:, 2, :], ALU.is_equal))
            step(v.memset(nat[:, 7, :], 1.0))
            step(v.tensor_tensor_scan(out=nat[:, 8, :], data0=nat[:, 4, :], data1=nat[:, 7, :], initial=0.0,
                                      op0=ALU.mult, op1=ALU.add))
            step(v.memset(nat[:, 7, :], 0.0))
            step(v.tensor_tensor_scan(out=nat[:, 9, :], data0=nat[:, 4, :], data1=nat[:, 7, :], initial=1.0,
                                      op0=ALU.mult, op1=ALU.add))
            assert steps[0] == SETUP_SCAN
            dv.wait_ge(s_pe_small, 1)
            step(v.tensor_copy(tiny[:, 0, :], bank[2][0:1, 0:NAT]))
            step(v.tensor_copy(tiny[:, 1, :], bank[3][0:1, 0:NAT]))
            step(v.tensor_tensor_scan(out=tiny[:, 2, :], data0=tiny[:, 1, :], data1=tiny[:, 0, :], initial=0.0,
                                      op0=ALU.mult, op1=ALU.add))
            step(v.memset(tiny[:, 3, 0:1], 0.0))
            step(v.tensor_copy(tiny[:, 3, 1:NAT], tiny[:, 2, 0:NAT - 1]))
            assert steps[0] == SETUP_CARRY
            dv.wait_ge(s_pe_small, 2)
            step(v.tensor_copy(carry_in[:, :], bank[4][0:NAT, 0:1]))
            step(v.scalar_tensor_tensor(out=nat[:, 7, :], in0=nat[:, 9, :], scalar=carry_in[:, 0:1],
                                        in1=nat[:, 8, :], op0=ALU.mult, op1=ALU.add))
            steps[0] += 2
            dv.wait_ge(s_setup, steps[0])
            step(v.tensor_tensor(nat[:, 0, :], nat[:, 10, :], nat[:, 10, :], ALU.mult))
            step(v.scalar_tensor_tensor(out=nat[:, 0, :], in0=nat[:, 7, :], scalar=1.0, in1=nat[:, 0, :],
                                        op0=ALU.add, op1=ALU.mult))
            step(v.tensor_scalar(nat[:, 0, :], nat[:, 0, :], -0.5, 1.5, ALU.mult, ALU.add))
            step(v.tensor_tensor(nat[:, 10, :], nat[:, 10, :], nat[:, 0, :], ALU.mult))
            assert steps[0] == SETUP_ROWS
            dv.wait_ge(s_tcol, 1)
            ccol = [0]

            def cstep(ins, wait=False):
                ins.then_inc(s_ccol, 1)
                ccol[0] += 1
                if wait:
                    dv.wait_ge(s_ccol, ccol[0])

            for q in range(4):
                for par in (0, 1):
                    cstep(v.tensor_copy(col[:, q, par::2], bank[q][0:TILE, 128 * par:128 * par + NAT]))
            dv.wait_ge(s_ccol, 8)
            v.tensor_copy(idx_dst[:, :], col[:, 0, :]).then_inc(s_idx, 1)
            v.tensor_copy(idx_src[:, :], col[:, 1, :]).then_inc(s_idx, 1)
            v.tensor_copy(slot_rows[:, :, 2], col[:, 3, :]).then_inc(s_idx, 1)
            cstep(v.tensor_scalar(idx_f[:, :], col[:, 2, :], -float(SKIP), float(SKIP), ALU.mult, ALU.add), True)
            cstep(v.tensor_tensor(idx_f[:, :], idx_f[:, :], col[:, 0, :], ALU.add), True)
            v.tensor_copy(idx_last[:, :], idx_f[:, :]).then_inc(s_idx, 1)
            dv.wait_ge(s_pe_small, 3)
            v.tensor_copy(M["w2ca"][:, 0:64], bank[0][:, 0:64])
            v.tensor_copy(M["w2cb"][:, 64:128], bank[0][:, 0:64])
            const(v.tensor_copy(K["cb2"], bank[1][:, 0:1]))
            assert count[0] == CONST_END

            def own(P, step, n, ins, part=None):
                ins.then_inc(P.s(step), 1)
                P.wait(dv, step, n, part)

            def normed(P, i, u, ky, bias, out="o0", stored=True, rs="g"):
                P.wait(dv, "rstd", P.at(i, u))
                if stored:
                    P.stored(dv, "st", i, u)
                if bias is None:
                    ins = v.tensor_tensor(P.B[out][:, u, :], at_bank(P, u, ky), P.B[rs][:, u, :], ALU.mult)
                else:
                    ins = v.scalar_tensor_tensor(out=P.B[out][:, u, :], in0=at_bank(P, u, ky), scalar=bias,
                                                 in1=P.B[rs][:, u, :], op0=ALU.add, op1=ALU.mult)
                ins.then_inc(P.s("out"), 1)

            def neg_abs(P, i, u, out, z):
                P.free(dv, "lsig", i, u)
                v.scalar_tensor_tensor(out=out, in0=z, scalar=-1.0, in1=z, op0=ALU.mult, op1=ALU.min)\
                 .then_inc(P.s("nabs"), 1)

            def sigmoid_arg(P, i, u, out, z, log):
                P.free(dv, "sig", i, u)
                P.wait(dv, "lsig", P.at(i, u))
                v.scalar_tensor_tensor(out=out, in0=z, scalar=0.0, in1=log, op0=ALU.min, op1=ALU.subtract)\
                 .then_inc(P.s("arg"), 1)

            def relu_hidden(P, i, u, k, buf):
                v.tensor_scalar(P.B[buf][:, u, :], at_bank(P, u, k), K["b1"], 0.0, ALU.add, ALU.max).then_inc(P.s("relu1"), 1)

            def node0(P, with_g):
                def body(i, us):
                    for u in us:
                        P.free(dv, "y", i, u)
                        if with_g:
                            P.free(dv, "g", i, u)
                        P.wait(dv, "hid", P.at(i, u))
                        relu_hidden(P, i, u, 1, "b")
                    for u in us:
                        normed(P, i, u, 0, K["cb2"])
                in_groups(dv, P, body)
                P.all_done(dv)

            node0(P_node0, False)

            dv.wait_ge(s_info, PAIRS_OF_BLOCKS)
            dv.wait_ge(s_pe_small, 4)
            dv.wait_ge(s_rows, 12 * 16)
            for q in (0, 1):
                for par in (0, 1):
                    v.tensor_copy(nat[:, q, TILE * par:TILE * par + TILE],
                                  bank[q][0:NAT, 128 * par:128 * par + TILE]).then_inc(s_info, 1)
            dv.wait_ge(s_info, PAIRS_OF_BLOCKS + 4)
            v.tensor_tensor(nat[:, 2, :], nat[:, 1, :], nat[:, 11, :], ALU.mult).then_inc(s_info, 1)

            def scan(P, n, u, out, same, msg):
                def part(k, ins):
                    own(P, "scan", n, ins, k)
                for h in (0, 1):
                    lo, hi = slice(64 * h, 64 * h + 64), slice(64 - 64 * h, 128 - 64 * h)
                    part(2 * h + 1, v.tensor_tensor_scan(out=out[lo, u, :], data0=same[lo, u, :], data1=msg[lo, u, :],
                                                         initial=carry[lo, 0:1], op0=ALU.mult, op1=ALU.add))
                    part(2 * h + 2, v.tensor_copy(carry[hi, 0:1], out[lo, u, COLS - 1:COLS]))

            def tt(out, a, b, op):
                return v.tensor_tensor(out, a, b, op)

            def sums(i, u):
                n = P_e0.at(i, u)
                P_e0.landed(dv, "ld", i, u)
                P_e0.stored(dv, "st", i, u)
                P_e0.wait(dv, "tr", n)
                own(P_e0, "evd", n, v.tensor_copy(P_e0.B["o2"][:, u, :], at_bank(P_e0, u, 1)))
                P_e0.wait(dv, "evs", n)
                own(P_e0, "msg", n, tt(P_e0.B["a"][:, u, :], P_e0.B["o1"][:, u, :], P_e0.B["wts"][:, u, :], ALU.mult))
                scan(P_e0, n, u, P_e0.B["e"], P_e0.B["same"], P_e0.B["a"])
                P_e0.free(dv, "hid", i, u)
                own(P_e0, "vec", n, tt(P_e0.B["f"][:, u, :], P_e0.B["o2"][:, u, :], P_e0.B["dinv"][:, u, :], ALU.mult), 1)
                own(P_e0, "vec", n, tt(P_e0.B["g"][:, u, :], P_e0.B["f"][:, u, :], P_e0.B["e"][:, u, :], ALU.add), 2)
                tt(P_e0.B["b"][:, u, :], P_e0.B["g"][:, u, :], P_e0.B["dinv"][:, u, :], ALU.mult).then_inc(P_e0.s("vec"), 1)

            def relu(i, u):
                P_e0.free(dv, "g", i, u)
                P_e0.wait(dv, "hid", P_e0.at(i, u))
                relu_hidden(P_e0, i, u, 1, "d")

            def times(i, u):
                P_e0.wait(dv, "g", P_e0.at(i, u))
                tt(P_e0.B["o0"][:, u, :], at_bank(P_e0, u, 0), P_e0.B["dinv"][:, u, :], ALU.mult).then_inc(P_e0.s("out"), 1)

            in_turn(dv, P_e0, [(0, sums), (1, relu), (2, times)])
            P_e0.all_done(dv)

            def clear_carry(k):
                v.memset(carry[:, :], 0.0).then_inc(s_dconst, 1)
                dv.wait_ge(s_dconst, CONST_END + k)
            node0(P_node0e, True)
            clear_carry(1)

            def overlay(P, i, u, out):
                n = P.at(i, u)
                P.landed(dv, "ld", i, u)
                own(P, "msg", n, tt(P.B["in0"][:, u, :], P.B["in0"][:, u, :], P.B["keep"][:, u, :], ALU.mult), 1)
                P.wait(dv, "tr", n)
                own(P, "msg", n, tt(out[:, u, :], P.B["in0"][:, u, :], at_bank(P, u, 0), ALU.add), 2)

            def sums(i, u):
                n = P_e1.at(i, u)
                overlay(P_e1, i, u, P_e1.B["a"])
                P_e1.free(dv, "y", i, u)
                scan(P_e1, n, u, P_e1.B["e"], P_e1.B["same"], P_e1.B["a"])
                own(P_e1, "vec", n, tt(P_e1.B["f"][:, u, :], P_e1.B["e"][:, u, :], P_e1.B["in2"][:, u, :], ALU.add), 1)
                own(P_e1, "vec", n, tt(P_e1.B["b"][:, u, :], P_e1.B["f"][:, u, :], P_e1.B["dinv"][:, u, :], ALU.mult), 2)
                tt(P_e1.B["c"][:, u, :], P_e1.B["b"][:, u, :], P_e1.B["in1"][:, u, :], ALU.add).then_inc(P_e1.s("vec"), 1)

            def out_rows(i, u):
                normed(P_e1, i, u, 1, K["cb2"])

            in_turn(dv, P_e1, [(0, sums), (1, out_rows)])
            P_e1.all_done(dv)
            clear_carry(2)

            def sums(i, u, P=P_e2):
                n = P_e2.at(i, u)
                P.stored(dv, "st", i, u)
                P.free(dv, "t", i, u)
                overlay(P, i, u, P_e2.B["o3"])
                own(P, "vec", n, v.scalar_tensor_tensor(out=P_e2.B["b"][:, u, :], in0=P_e2.B["more"][:, u, :], scalar=0.0,
                                                        in1=P_e2.B["in1"][:, u, :], op0=ALU.is_equal, op1=ALU.mult))
                for q, h in enumerate((1, 0)):
                    lo, hi = slice(64 * h, 64 * h + 64), slice(64 - 64 * h, 128 - 64 * h)
                    own(P, "scan", n, v.tensor_tensor_scan(
                        out=P_e2.B["o0"][lo, u, ::-1], data0=P_e2.B["more"][lo, u, ::-1], data1=P_e2.B["b"][lo, u, ::-1],
                        initial=carry[lo, 0:1], op0=ALU.mult, op1=ALU.add), 2 * q + 1)
                    own(P, "scan", n, v.tensor_copy(carry[hi, 0:1], P_e2.B["o0"][lo, u, 0:1]), 2 * q + 2)

            def bn(i, u, P=P_e2):
                n = P_e2.at(i, u)
                P.wait(dv, "evf", n)
                v.bn_stats(stats["f"][:, bass.ds(n, 1), :], P_e2.B["o1"][:, u, :]).then_inc(P.s("bnf"), 1)
                P.wait(dv, "evc", n)
                v.bn_stats(stats["c"][:, bass.ds(n, 1), :], P_e2.B["o2"][:, u, :]).then_inc(P.s("bnc"), 1)

            in_turn(dv, P_e2, [(0, sums), (2, bn)])
            P_e2.all_done(dv)

            small = [0]

            def sm(ins):
                ins.then_inc(s_dv_small, 1)
                small[0] += 1
                dv.wait_ge(s_dv_small, small[0])

            def moments(names):
                for k, name in enumerate(names):
                    sm(v.bn_aggr(mv[:, k, :], stats[name][:, :, :]))
                    sm(v.tensor_copy(mom[:, k, 0:1], mv[:, k, 0:1]))
                    sm(v.scalar_tensor_tensor(out=mom[:, k, 1:2], in0=mv[:, k, 0:1], scalar=mv[:, k, 0:1],
                                              in1=mv[:, k, 1:2], op0=ALU.mult, op1=ALU.add))

            roots = [0]

            def affine(mean, square, gain, shift, s, t):
                sm(v.tensor_tensor(K["tmp0"], mean, mean, ALU.mult))
                sm(v.tensor_tensor(K["tmp1"], square, K["tmp0"], ALU.subtract))
                roots[0] += 2
                dv.wait_ge(s_ac_small, roots[0])
                sm(v.tensor_tensor(s, gain, K["tmp1"], ALU.mult))
                sm(v.tensor_tensor(K["tmp0"], mean, s, ALU.mult))
                sm(v.tensor_tensor(t, shift, K["tmp0"], ALU.subtract))

            moments(("f", "c"))
            assert small[0] == STATS1
            dv.wait_ge(s_pe_small, 5)
            sm(v.tensor_copy(hold[:, 0:4], bank[0][:, 0:4]))
            affine(hold[:, 0:1], hold[:, 1:2], K["g1f"], K["be1f"], K["s1f"], K["t1f"])
            affine(hold[:, 2:3], hold[:, 3:4], K["g1c"], K["be1c"], K["s1c"], K["t1c"])
            assert small[0] == STATS1B, small
            clear_carry(3)

            def z(i, u):
                n = P_e3.at(i, u)
                P_e3.landed(dv, "ld", i, u)
                own(P_e3, "msg", n, v.tensor_scalar(P_e3.B["e"][:, u, :], P_e3.B["in1"][:, u, :], K["s1c"], K["t1c"],
                                                 ALU.mult, ALU.add), 1)
                own(P_e3, "msg", n, v.tensor_scalar(P_e3.B["f"][:, u, :], P_e3.B["in0"][:, u, :], K["s1f"], K["t1f"],
                                                 ALU.mult, ALU.add), 2)
                neg_abs(P_e3, i, u, P_e3.B["g2"][:, u, :], P_e3.B["f"][:, u, :])

            def arg(i, u):
                sigmoid_arg(P_e3, i, u, P_e3.B["in3"][:, u, :], P_e3.B["f"][:, u, :], P_e3.B["a"][:, u, :])

            def sums(i, u):
                P_e3.wait(dv, "sig", P_e3.at(i, u))
                n = P_e3.at(i, u)
                P_e3.wait(dv, "act", n)
                own(P_e3, "vec", n, v.scalar_tensor_tensor(out=P_e3.B["g"][:, u, :], in0=P_e3.B["e"][:, u, :], scalar=0.0,
                                                        in1=P_e3.B["d"][:, u, :], op0=ALU.max, op1=ALU.add), 1)
                own(P_e3, "vec", n, tt(P_e3.B["h"][:, u, :], P_e3.B["g"][:, u, :], P_e3.B["in4"][:, u, :], ALU.mult), 2)
                scan(P_e3, n, u, P_e3.B["o1"], P_e3.B["same"], P_e3.B["h"])
                P_e3.stored(dv, "st", i, u)
                own(P_e3, "out", n, v.scalar_tensor_tensor(out=P_e3.B["o0"][:, u, :], in0=P_e3.B["more"][:, u, :], scalar=0.0,
                                                        in1=P_e3.B["o1"][:, u, :], op0=ALU.is_equal, op1=ALU.mult))
                v.bn_stats(stats["u"][:, bass.ds(n, 1), :], P_e3.B["o0"][:, u, :]).then_inc(P_e3.s("bnf"), 1)

            in_turn(dv, P_e3, [(1, arg), (0, z), (2, sums)])
            P_e3.all_done(dv)

            moments(("u",))
            assert small[0] == STATS2, small
            dv.wait_ge(s_pe_small, 6)
            sm(v.tensor_scalar(hold[:, 0:2], bank[0][:, 0:2], float(EDGES) / NODES, None, ALU.mult))
            affine(hold[:, 0:1], hold[:, 1:2], K["g2"], K["be2"], K["s2"], K["t2"])
            sm(v.tensor_scalar(K["nt2"], K["t2"], -1.0, None, ALU.mult))
            assert small[0] == STATS2B, small
            dv.wait_ge(s_pe_small, 7)
            sm(v.tensor_copy(K["ct2"], bank[1][:, 0:1]))
            assert small[0] == STATS2C

            def body(i, us):
                P = P_e4
                for u in us:
                    P.landed(dv, "ld", i, u)
                    P.free(dv, "act", i, u)
                    v.scalar_tensor_tensor(out=P.B["e"][:, u, :], in0=P.B["in1"][:, u, :], scalar=K["s2"],
                                           in1=P.B["in0"][:, u, :], op0=ALU.mult, op1=ALU.add).then_inc(P.s("msg"), 1)
                for u in us:
                    n = P.at(i, u)
                    P.wait(dv, "act", n)
                    own(P, "vec", n, v.scalar_tensor_tensor(out=P.B["h"][:, u, :], in0=P.B["e"][:, u, :], scalar=K["nt2"],
                                                            in1=P.B["a"][:, u, :], op0=ALU.max, op1=ALU.add), 1)
                    P.free(dv, "y", i, u)
                    tt(P.B["c"][:, u, :], P.B["h"][:, u, :], P.B["in0"][:, u, :], ALU.add).then_inc(P.s("vec"), 1)
                for u in us:
                    normed(P, i, u, 0, K["ct2"])
            in_groups(dv, P_e4, body)
            P_e4.all_done(dv)

            def soft(P, stat):
                def body(i, us):
                    for u in us:
                        n = P.at(i, u)
                        P.landed(dv, "ld", i, u)
                        P.wait(dv, "act", n)
                        own(P, "vec", n, v.scalar_tensor_tensor(out=P.B["h"][:, u, :], in0=P.B["in0"][:, u, :],
                                                                scalar=K["nt2"], in1=P.B["a"][:, u, :],
                                                                op0=ALU.max, op1=ALU.add), 1)
                        P.free(dv, "y", i, u)
                        tt(P.B["c"][:, u, :], P.B["h"][:, u, :], P.B["in0"][:, u, :], ALU.add).then_inc(P.s("vec"), 1)
                    for u in us:
                        if stat:
                            P.free(dv, "h", i, u)
                        normed(P, i, u, 0, K["ct2"])
                    if stat:
                        for u in us:
                            n = P.at(i, u)
                            P.wait(dv, "h", n)
                            v.bn_stats(stats["n"][:, bass.ds(n, 1), :], at_bank(P, u, 0)).then_inc(P.s("bnf"), 1)
                in_groups(dv, P, body)
                P.all_done(dv)
            soft(P_node1, True)
            soft(P_node1e, False)
            clear_carry(4)

            def sums(i, u, P=P_e5):
                n = P_e5.at(i, u)
                P.stored(dv, "st", i, u)
                overlay(P, i, u, P_e5.B["o0"])
                P.free(dv, "h", i, u)
                scan(P, n, u, P_e5.B["e"], P_e5.B["same"], P_e5.B["o0"])
                tt(P_e5.B["b"][:, u, :], P_e5.B["e"][:, u, :], P_e5.B["in1"][:, u, :], ALU.add).then_inc(P.s("vec"), 1)

            def masked(i, u, P=P_e5):
                n = P_e5.at(i, u)
                P.wait(dv, "evs", n)
                for k, (buf, name, done) in enumerate((("f", "hd", "bnf"), ("g", "hu", "bnc"))):
                    own(P, "mask", n, v.scalar_tensor_tensor(out=P_e5.B[buf][:, u, :], in0=P_e5.B["more"][:, u, :], scalar=0.0,
                                                             in1=(P_e5.B["o1"][:, u, :], at_bank(P_e5, u, 1))[k], op0=ALU.is_equal, op1=ALU.mult), k + 1)
                    v.bn_stats(stats[name][:, bass.ds(n, 1), :], P_e5.B[buf][:, u, :]).then_inc(P.s(done), 1)

            in_turn(dv, P_e5, [(0, sums), (1, masked)])
            P_e5.all_done(dv)

            moments(("n", "hd", "hu"))
            assert small[0] == STATS3, small
            dv.wait_ge(s_pe_small, 8)
            sm(v.tensor_copy(hold[:, 0:6], bank[0][:, 0:6]))
            sm(v.tensor_tensor(hold[:, 2:4], hold[:, 2:4], hold[:, 4:6], ALU.subtract))
            sm(v.scalar_tensor_tensor(out=hold[:, 6:8], in0=hold[:, 2:4], scalar=float(EDGES) / NODES,
                                      in1=hold[:, 0:2], op0=ALU.mult, op1=ALU.add))
            affine(hold[:, 6:7], hold[:, 7:8], K["g3"], K["be3"], K["s3"], K["t3"])
            sm(v.tensor_tensor(K["tmp2"], hold[:, 6:7], K["bl2"], ALU.add))
            sm(v.tensor_tensor(K["tmp2"], K["bl2"], K["tmp2"], ALU.subtract))
            sm(v.tensor_tensor(K["tmp2"], K["tmp2"], K["s3"], ALU.mult))
            sm(v.tensor_tensor(K["t3"], K["be3"], K["tmp2"], ALU.add))
            assert small[0] == STATS3B, small

            def relu_bn(P, x2):
                def body(i, us):
                    for u in us:
                        P.landed(dv, "ld", i, u)
                        P.free(dv, "y", i, u)
                        P.wait(dv, "act", P.at(i, u))
                        tt(P.B["c"][:, u, :], P.B["a"][:, u, :], P.B[x2][:, u, :], ALU.add).then_inc(P.s("vec"), 1)
                    for u in us:
                        normed(P, i, u, 0, None)
                in_groups(dv, P, body)
                P.all_done(dv)
            relu_bn(P_e6, "in1")
            relu_bn(P_e6s, "in0")

            def node2(P):
                def vec(i, u):
                    P.landed(dv, "ld", i, u)
                    P.wait(dv, "act", P.at(i, u))
                    tt(P.B["b"][:, u, :], P.B["b"][:, u, :], P.B["in0"][:, u, :], ALU.add).then_inc(P.s("vec"), 1)

                def body(i, us, more):
                    for u in us:
                        P.wait(dv, "rstd", P.at(i, u))
                        tt(P.B["o0"][:, u, :], at_bank(P, u, 1), P.B["h"][:, u, :], ALU.mult).then_inc(P.s("out"), 1)
                    for u in us:
                        P.wait(dv, "hid", P.at(i, u))
                        P.free(dv, "g", i, u)
                        v.tensor_scalar(P.B["a"][:, u, :], at_bank(P, u, 0), K["b31"], 0.0, ALU.add, ALU.max).then_inc(P.s("relu0"), 1)
                    for u in us:
                        P.wait(dv, "g", P.at(i, u))
                        own(P, "z", P.at(i, u), v.tensor_scalar(P.B["e"][:, u, :], at_bank(P, u, 1), K["b32"], None, ALU.add))
                        neg_abs(P, i, u, P.B["in1"][:, u, :], P.B["e"][:, u, :])
                    for u in us:
                        sigmoid_arg(P, i, u, P.B["e"][:, u, :], P.B["e"][:, u, :], P.B["in1"][:, u, :])
                    for u in us:
                        P.free(dv, "y2", i, u)
                        P.wait(dv, "sig", P.at(i, u))
                        tt(P.B["o0"][:, u, :], P.B["e"][:, u, :], P.B["o0"][:, u, :], ALU.add).then_inc(P.s("add"), 1)
                    if more:
                        for u in us:
                            vec(i + 1, u)
                    for u in us:
                        P.wait(dv, "rstd2", P.at(i, u))
                        tt(P.B["o1"][:, u, :], at_bank(P, u, 0), P.B["c"][:, u, :], ALU.mult).then_inc(P.s("out2"), 1)
                in_groups_ahead(dv, P, vec, body)
                P.all_done(dv)
            node2(P_node2)
            clear_carry(5)

            P = P_e7

            def over(i, u):
                n = P_e7.at(i, u)
                overlay(P_e7, i, u, P_e7.B["a"])

            def sums(i, u):
                n = P_e7.at(i, u)
                P_e7.wait(dv, "evs", n)
                own(P_e7, "vec", n, tt(P_e7.B["g"][:, u, :], P_e7.B["b"][:, u, :], P_e7.B["wts"][:, u, :], ALU.mult), 1)
                scan(P_e7, n, u, P_e7.B["e"], P_e7.B["same"], P_e7.B["g"])
                P_e7.wait(dv, "evd", n)
                own(P_e7, "vec", n, tt(P_e7.B["f"][:, u, :], P_e7.B["c"][:, u, :], P_e7.B["dinv"][:, u, :], ALU.mult), 2)
                own(P_e7, "vec", n, tt(P_e7.B["in4"][:, u, :], P_e7.B["f"][:, u, :], P_e7.B["e"][:, u, :], ALU.add), 3)
                own(P_e7, "vec", n, tt(P_e7.B["in3"][:, u, :], P_e7.B["in4"][:, u, :], P_e7.B["dinv"][:, u, :], ALU.mult), 4)
                v.tensor_scalar(P_e7.B["h"][:, u, :], P_e7.B["in3"][:, u, :], 0.0, None, ALU.max).then_inc(P_e7.s("relu1"), 1)

            def times(i, u):
                n = P_e7.at(i, u)
                P_e7.wait(dv, "h", n)
                P_e7.stored(dv, "st", i, u)
                v.scalar_tensor_tensor(out=P_e7.B["o0"][:, u, :], in0=at_bank(P_e7, u, 0), scalar=K["b32"], in1=P_e7.B["dinv"][:, u, :],
                                       op0=ALU.add, op1=ALU.mult).then_inc(P_e7.s("out"), 1)

            in_turn(dv, P_e7, [(0, over), (1, sums), (2, times)])
            P.all_done(dv)
            clear_carry(6)

            node2(P_node2b)
            P = P_e8

            def sums(i, u):
                n = P_e8.at(i, u)
                overlay(P_e8, i, u, P_e8.B["a"])
                own(P_e8, "msg", n, tt(P_e8.B["g"][:, u, :], P_e8.B["a"][:, u, :], P_e8.B["wts"][:, u, :], ALU.mult), 3)
                P_e8.free(dv, "y", i, u)
                scan(P_e8, n, u, P_e8.B["b"], P_e8.B["same"], P_e8.B["g"])
                own(P_e8, "vec", n, tt(P_e8.B["h"][:, u, :], P_e8.B["b"][:, u, :], P_e8.B["in2"][:, u, :], ALU.add), 1)
                own(P_e8, "vec", n, tt(P_e8.B["c"][:, u, :], P_e8.B["h"][:, u, :], P_e8.B["dinv"][:, u, :], ALU.mult), 2)
                neg_abs(P_e8, i, u, P_e8.B["o1"][:, u, :], P_e8.B["c"][:, u, :])

            def arg(i, u):
                sigmoid_arg(P_e8, i, u, P_e8.B["in3"][:, u, :], P_e8.B["c"][:, u, :], P_e8.B["e"][:, u, :])

            def add(i, u):
                n = P_e8.at(i, u)
                P_e8.wait(dv, "sig", n)
                tt(P_e8.B["f"][:, u, :], P_e8.B["in4"][:, u, :], P_e8.B["in1"][:, u, :], ALU.add).then_inc(P_e8.s("add"), 1)

            def normal(i, u):
                P_e8.free(dv, "row", i, u)
                normed(P_e8, i, u, 1, None, stored=False, rs="g2")

            in_turn(dv, P_e8, [(1, arg), (2, add), (0, sums), (3, normal)])


KEYS, PER = 5000, EDGES // TILE
SORT_KEYS = 1 + PER * 6 + 3
SORT_RANKED = 4 + EDGES // KEYS * SORT_KEYS
SORT_END = SORT_RANKED + 5

WEIGHT_DMAS = 5 + 12 + 6 + 1 + 2 * 14
CONST_END = 7
SETUP_SCAN, SETUP_CARRY, SETUP_ROWS = 10, 15, 23
PAIRS_OF_BLOCKS = (BLOCKS + 1) // 2
INFO_ROWS = PAIRS_OF_BLOCKS + 5
STATS1 = 6
STATS1B = STATS1 + 1 + 10
STATS2 = STATS1B + 3
STATS2B = STATS2 + 1 + 5 + 1
STATS2C = STATS2B + 1
STATS3 = STATS2C + 9
STATS3B = STATS3 + 3 + 5 + 4

ROW_NAMES = ["sdinv", "dinv", "same", "keep", "more", "wd", "dinv", "same", "keep", "w"]
ROW_SETS = {"e0": (0, ("sdinv wts", "dinv", "same")), "e1": (1, ("dinv", "same", "keep")), "e2": (3, ("keep", "more")),
            "e3": (2, ("same", "keep", "more")), "e7": (5, ("wd wts", "dinv", "same", "keep")),
            "e8": (6, ("dinv", "same", "keep", "w wts"))}

_ARGS = ["xt", "x", "src", "dstp", "ea", "ew", "w1", "w2", "w2t", "b1", "b2", "wf", "bf", "g1", "be1", "g2",
         "be2", "wl2", "bl2", "g3", "be3", "w31t", "b31", "w32t", "b32"]


def kernel(**inputs):
    import concourse.bacc as _bacc
    from concourse import mybir as _mybir
    from concourse.bass_utils import run_bass_kernel_spmd as _run

    a = {k: np.asarray(v) for k, v in inputs.items()}
    x = a["x"]
    arrays = {
        "xt": x.reshape(NODE_CHUNKS, TILE, 2, 4, D).transpose(0, 2, 4, 3, 1).reshape(NODE_CHUNKS, 128, COLS),
        "x": x, "src": a["src"],
        "dstp": np.concatenate([np.full(1, -1, a["dst"].dtype), a["dst"], np.full(1, -1, a["dst"].dtype)]),
        "ea": a["edge_attr_64"], "ew": a["edge_weight1"].reshape(-1),
        "w1": a["L0_gnn_W1"], "w2": a["L0_gnn_W2"], "w2t": a["L0_gnn_W2"].T, "b1": a["L0_gnn_b1"],
        "b2": a["L0_gnn_b2"], "wf": a["L1_gnn_W_full"], "bf": a["L1_gnn_b_full"], "g1": a["L1_gnn_bn1_g"],
        "be1": a["L1_gnn_bn1_b"], "g2": a["L1_gnn_bn2_g"], "be2": a["L1_gnn_bn2_b"], "wl2": a["L2_gnn_W"],
        "bl2": a["L2_gnn_b"], "g3": a["L2_gnn_gamma"], "be3": a["L2_gnn_beta"], "w31t": a["L3_gnn_W1"].T,
        "b31": a["L3_gnn_b1"], "w32t": a["L3_gnn_W2"].T, "b32": a["L3_gnn_b2"],
    }
    nc = _bacc.Bacc("TRN2", target_bir_lowering=False, num_devices=1)
    feed, args = {}, []
    for name in _ARGS:
        v = np.ascontiguousarray(arrays[name])
        feed[f"in_{name}"] = v
        args.append(nc.dram_tensor(f"in_{name}", v.shape, _mybir.dt.from_np(v.dtype), kind="ExternalInput").ap())
    args.append(nc.dram_tensor("out_0", (NODES, D), _mybir.dt.float32, kind="ExternalOutput").ap())
    gnn(nc, *args)
    r = _run(nc, [feed], core_ids=[0])
    return r.results[0]["out_0"]
```
